# Optimizing a Trainium2 kernel written in Bass

```python
import numpy as np
import jax
import jax.numpy as jnp

def _softmax(x, axis=-1):
    return jax.nn.softmax(x, axis=axis)

def _gelu(x):
    return jax.nn.gelu(x, approximate=True)

def _silu(x):
    return jax.nn.silu(x)

def _sigmoid(x):
    return jax.nn.sigmoid(x)

def _layernorm(x, axis=-1, eps=1e-05):
    m = jnp.mean(x, axis=axis, keepdims=True)
    v = jnp.var(x, axis=axis, keepdims=True)
    return (x - m) / jnp.sqrt(v + eps)

def _scatter_add(tgt, idx, src, axis=0):
    return tgt.at[idx].add(src)

def _segment_sum(src, seg, n):
    return jax.ops.segment_sum(src, seg, n)
kernel_name = 'mk_decoder_postln_d2_seqx_r4_e88a4b'

def setup_inputs(seed: int=0):
    np.random.seed(seed)
    _w = jnp.asarray

    def _rec_inputs():
        import jax
        import jax.numpy as jnp
        _rk = jax.random.key(seed)
        x = -0.0003929 + 0.9999 * jax.random.normal(jax.random.fold_in(_rk, 1), (4, 512, 256), jnp.float32)
        _lenS = 512 - jax.random.randint(jax.random.fold_in(_rk, 7), (4,), 0, max(1, 512 // 4) + 1, jnp.int32)
        _lenS2 = 64 - jax.random.randint(jax.random.fold_in(_rk, 8), (4,), 0, max(1, 64 // 4) + 1, jnp.int32)
        _ctx_1024P = jax.random.normal(jax.random.fold_in(_rk, 11), (4, 16, 256), jnp.float32)
        _ctx_1024c = jax.random.dirichlet(jax.random.fold_in(_rk, 511), 0.3 * jnp.ones((16,), jnp.float32), (4, 64))
        _ctx_1024t = jnp.einsum('bsk,bkd->bsd', _ctx_1024c, _ctx_1024P)
        _ctx_1024t = _ctx_1024t * jax.lax.rsqrt(jnp.mean(jnp.square(_ctx_1024t)) + 1e-12) * 0.953939
        ctx_1024 = 2.81802e-05 + 1.00001 * (_ctx_1024t + 0.3 * jax.random.normal(jax.random.fold_in(_rk, 611), (4, 64, 256), jnp.float32))
        return (x, ctx_1024)
    x, ctx_1024 = _rec_inputs()

    def _L0_attn_setup():
        import jax, jax.numpy as jnp
        import numpy as np
        D = 256
        FW = 64
        DEPTH = 2
        E = D * (DEPTH + 1)
        B, L = (2, 1024)

        def _fftconv(x_bdl, h, bias_d):
            Lq = x_bdl.shape[-1]
            n = 2 * Lq
            Xf = jnp.fft.rfft(x_bdl, n=n)
            Hf = jnp.fft.rfft(h, n=n) / n
            y = jnp.fft.irfft(Xf * Hf, n=n, norm='forward')[..., :Lq]
            return y + x_bdl * bias_d[:, None]
        key = jax.random.key(seed)
        ks = jax.random.split(key, 12)
        s = lambda k, shape, scale: jax.random.normal(k, shape, dtype=jnp.float32) * scale
        return {'x': jax.random.normal(ks[0], (B, L, D), dtype=jnp.float32), 'w_in': s(ks[1], (D, E), 0.02), 'b_in': jnp.zeros((E,), jnp.float32), 'w_conv': s(ks[2], (E, 1, 3), 0.5), 'b_conv': jnp.zeros((E,), jnp.float32), 'w1': s(ks[3], (3, FW), 0.5), 'b1': jnp.zeros((FW,), jnp.float32), 'w2': s(ks[4], (FW, FW), 0.1), 'b2': jnp.zeros((FW,), jnp.float32), 'w3': s(ks[5], (FW, D), 0.1), 'filt_bias': jax.random.normal(ks[6], (D,), dtype=jnp.float32), 'w_out': s(ks[7], (D, D), 0.02), 'b_out': jnp.zeros((D,), jnp.float32)}
    _L0_attn_all = _L0_attn_setup()
    _L0_attn_in = {k: v for k, v in _L0_attn_all.items() if k in ('w_in', 'b_in', 'w_conv', 'b_conv', 'w1', 'b1', 'w2', 'b2', 'w3', 'filt_bias', 'w_out', 'b_out')}
    del _L0_attn_all

    def _L0_xattn_setup():
        import jax, jax.numpy as jnp
        import numpy as np
        D1, D2, D3 = (256, 256, 256)
        key = jax.random.key(seed)
        k1, k2, kw, kb = jax.random.split(key, 4)
        x1 = jax.random.normal(k1, (8, 512, D1), dtype=jnp.float32)
        x2 = jax.random.normal(k2, (8, 512, D2), dtype=jnp.float32)
        bound = 1.0 / np.sqrt(D1 + D2)
        W = jax.random.uniform(kw, (D3, D1 + D2), minval=-bound, maxval=bound, dtype=jnp.float32)
        b = jax.random.uniform(kb, (D3,), minval=-bound, maxval=bound, dtype=jnp.float32)
        return {'x1': x1, 'x2': x2, 'W': W, 'b': b}
    _L0_xattn_all = _L0_xattn_setup()
    _L0_xattn_in = {k: v for k, v in _L0_xattn_all.items() if k in ('W', 'b')}
    del _L0_xattn_all

    def _L0_ffn_setup():
        import jax, jax.numpy as jnp
        import numpy as np
        B, S, D_MODEL, D_HIDDEN = (4, 512, 256, 1024)

        def act_quant(x):
            scale = 127.0 / jnp.clip(jnp.max(jnp.abs(x), axis=-1, keepdims=True), 1e-05)
            return jnp.clip(jnp.round(x * scale), -128, 127) / scale

        def weight_quant(w):
            scale = 1.0 / jnp.clip(jnp.mean(jnp.abs(w)), 1e-05)
            return jnp.clip(jnp.round(w * scale), -1, 1) / scale

        def bit_linear(x, w):
            xq = x + jax.lax.stop_gradient(act_quant(x) - x)
            wq = w + jax.lax.stop_gradient(weight_quant(w) - w)
            return jnp.einsum('bsd,hd->bsh', xq, wq)

        def depthwise_conv1d(x_bcl, w, b):
            y = jax.lax.conv_general_dilated(x_bcl, w, window_strides=(1,), padding=[(1, 1)], dimension_numbers=('NCH', 'OIH', 'NCH'), feature_group_count=x_bcl.shape[1])
            return y + b[None, :, None]
        key = jax.random.key(seed)
        ks = jax.random.split(key, 5)
        lim1 = 1.0 / np.sqrt(D_MODEL)
        lim2 = 1.0 / np.sqrt(D_HIDDEN)
        limc = 1.0 / np.sqrt(3.0)
        return {'x': jax.random.normal(ks[0], (B, S, D_MODEL), dtype=jnp.float32), 'w1': jax.random.uniform(ks[1], (D_HIDDEN, D_MODEL), jnp.float32, -lim1, lim1), 'conv_w': jax.random.uniform(ks[2], (D_HIDDEN, 1, 3), jnp.float32, -limc, limc), 'conv_b': jax.random.uniform(ks[3], (D_HIDDEN,), jnp.float32, -limc, limc), 'w2': jax.random.uniform(ks[4], (D_MODEL, D_HIDDEN), jnp.float32, -lim2, lim2)}
    _L0_ffn_all = _L0_ffn_setup()
    _L0_ffn_in = {k: v for k, v in _L0_ffn_all.items() if k in ('w1', 'conv_w', 'conv_b', 'w2')}
    del _L0_ffn_all

    def _L1_attn_setup():
        import jax, jax.numpy as jnp
        import numpy as np
        from jax import lax
        B, L, D = (4, 1024, 256)
        EXPAND, K = (2, 4)
        INNER = D * EXPAND
        key = jax.random.key(seed)
        k0, k1, k2, k3, k4 = jax.random.split(key, 5)
        s = 0.02
        return {'x': jax.random.normal(k0, (B, L, D), jnp.float32), 'W_in': jax.random.normal(k1, (D, 2 * INNER), jnp.float32) * s, 'conv_w': jax.random.normal(k2, (INNER, 1, K), jnp.float32) * s, 'conv_b': jax.random.normal(k3, (INNER,), jnp.float32) * s, 'W_out': jax.random.normal(k4, (INNER, D), jnp.float32) * s}
    _L1_attn_all = _L1_attn_setup()
    _L1_attn_in = {k: v for k, v in _L1_attn_all.items() if k in ('W_in', 'conv_w', 'conv_b', 'W_out')}
    del _L1_attn_all

    def _L1_xattn_setup():
        import jax, jax.numpy as jnp
        import numpy as np
        B, S, D, H = (2, 512, 256, 16)
        DK = D // H
        key = jax.random.key(seed)
        ks = jax.random.split(key, 11)
        s = 1.0 / np.sqrt(D)
        return {'query': jax.random.normal(ks[0], (B, S, D), jnp.float32), 'key': jax.random.normal(ks[1], (B, S, D), jnp.float32), 'value': jax.random.normal(ks[2], (B, S, D), jnp.float32), 'Wq': jax.random.normal(ks[3], (D, D), jnp.float32) * s, 'bq': jnp.zeros((D,), jnp.float32), 'Wk': jax.random.normal(ks[4], (D, D), jnp.float32) * s, 'bk': jnp.zeros((D,), jnp.float32), 'Wv': jax.random.normal(ks[5], (D, D), jnp.float32) * s, 'bv': jnp.zeros((D,), jnp.float32), 'Wo': jax.random.normal(ks[6], (D, D), jnp.float32) * s, 'bo': jnp.zeros((D,), jnp.float32)}
    _L1_xattn_all = _L1_xattn_setup()
    _L1_xattn_in = {k: v for k, v in _L1_xattn_all.items() if k in ('Wq', 'bq', 'Wk', 'bk', 'Wv', 'bv', 'Wo', 'bo')}
    del _L1_xattn_all

    def _L1_ffn_setup():
        import jax, jax.numpy as jnp
        import numpy as np
        B, N, D = (4, 512, 256)
        SPARSITY = 0.01
        key = jax.random.key(seed)
        k1, k2, k3 = jax.random.split(key, 3)
        x = jax.random.normal(k1, (B, N, D), dtype=jnp.float32)
        spatial = jax.random.normal(k2, (D, D), dtype=jnp.float32) * 0.02
        freq = jnp.fft.fft(spatial, axis=-1)
        k = int(D * SPARSITY)
        mag = jnp.abs(freq)
        kth = jax.lax.top_k(mag, k)[0][:, -1:]
        w_sparse = jnp.where(mag >= kth, freq, 0.0 + 0j)
        bias = jax.random.normal(k3, (D,), dtype=jnp.float32) * 0.01
        return {'x': x, 'w_freq_real': jnp.real(w_sparse).astype(jnp.float32), 'w_freq_imag': jnp.imag(w_sparse).astype(jnp.float32), 'bias': bias}
    _L1_ffn_all = _L1_ffn_setup()
    _L1_ffn_in = {k: v for k, v in _L1_ffn_all.items() if k in ('w_freq_real', 'w_freq_imag', 'bias')}
    del _L1_ffn_all
    return {'x': x, 'ctx_1024': ctx_1024, 'L0_attn_w_in': _L0_attn_in['w_in'], 'L0_attn_b_in': _L0_attn_in['b_in'], 'L0_attn_w_conv': _L0_attn_in['w_conv'], 'L0_attn_b_conv': _L0_attn_in['b_conv'], 'L0_attn_w1': _L0_attn_in['w1'], 'L0_attn_b1': _L0_attn_in['b1'], 'L0_attn_w2': _L0_attn_in['w2'], 'L0_attn_b2': _L0_attn_in['b2'], 'L0_attn_w3': _L0_attn_in['w3'], 'L0_attn_filt_bias': _L0_attn_in['filt_bias'], 'L0_attn_w_out': _L0_attn_in['w_out'], 'L0_attn_b_out': _L0_attn_in['b_out'], 'L0_xattn_W': _L0_xattn_in['W'], 'L0_xattn_b': _L0_xattn_in['b'], 'L0_ffn_w1': _L0_ffn_in['w1'], 'L0_ffn_conv_w': _L0_ffn_in['conv_w'], 'L0_ffn_conv_b': _L0_ffn_in['conv_b'], 'L0_ffn_w2': _L0_ffn_in['w2'], 'L1_attn_W_in': _L1_attn_in['W_in'], 'L1_attn_conv_w': _L1_attn_in['conv_w'], 'L1_attn_conv_b': _L1_attn_in['conv_b'], 'L1_attn_W_out': _L1_attn_in['W_out'], 'L1_xattn_Wq': _L1_xattn_in['Wq'], 'L1_xattn_bq': _L1_xattn_in['bq'], 'L1_xattn_Wk': _L1_xattn_in['Wk'], 'L1_xattn_bk': _L1_xattn_in['bk'], 'L1_xattn_Wv': _L1_xattn_in['Wv'], 'L1_xattn_bv': _L1_xattn_in['bv'], 'L1_xattn_Wo': _L1_xattn_in['Wo'], 'L1_xattn_bo': _L1_xattn_in['bo'], 'L1_ffn_w_freq_real': _L1_ffn_in['w_freq_real'], 'L1_ffn_w_freq_imag': _L1_ffn_in['w_freq_imag'], 'L1_ffn_bias': _L1_ffn_in['bias']}

def reference(x, ctx_1024, L0_attn_w_in, L0_attn_b_in, L0_attn_w_conv, L0_attn_b_conv, L0_attn_w1, L0_attn_b1, L0_attn_w2, L0_attn_b2, L0_attn_w3, L0_attn_filt_bias, L0_attn_w_out, L0_attn_b_out, L0_xattn_W, L0_xattn_b, L0_ffn_w1, L0_ffn_conv_w, L0_ffn_conv_b, L0_ffn_w2, L1_attn_W_in, L1_attn_conv_w, L1_attn_conv_b, L1_attn_W_out, L1_xattn_Wq, L1_xattn_bq, L1_xattn_Wk, L1_xattn_bk, L1_xattn_Wv, L1_xattn_bv, L1_xattn_Wo, L1_xattn_bo, L1_ffn_w_freq_real, L1_ffn_w_freq_imag, L1_ffn_bias):
    import jax
    import jax.numpy as jnp

    def _L0_attn_ref(x, w_in, b_in, w_conv, b_conv, w1, b1, w2, b2, w3, filt_bias, w_out, b_out):
        import jax, jax.numpy as jnp
        import numpy as np
        D = 256
        FW = 64
        DEPTH = 2
        E = D * (DEPTH + 1)
        B, L = (2, 1024)

        def _fftconv(x_bdl, h, bias_d):
            Lq = x_bdl.shape[-1]
            n = 2 * Lq
            Xf = jnp.fft.rfft(x_bdl, n=n)
            Hf = jnp.fft.rfft(h, n=n) / n
            y = jnp.fft.irfft(Xf * Hf, n=n, norm='forward')[..., :Lq]
            return y + x_bdl * bias_d[:, None]
        _, Lx, Dm = x.shape
        u = (x @ w_in + b_in).transpose(0, 2, 1)
        u = jax.lax.conv_general_dilated(u, w_conv, window_strides=(1,), padding=[(2, 2)], feature_group_count=u.shape[1], dimension_numbers=('NCH', 'OIH', 'NCH'))
        u = (u + b_conv[None, :, None])[..., :Lx]
        streams = [u[:, i * Dm:(i + 1) * Dm, :] for i in range(DEPTH + 1)]
        t = jnp.linspace(0.0, 1.0, Lx)
        pos = jnp.tile(t[:, None], (1, 3))
        hmlp = jax.nn.silu(pos @ w1 + b1)
        hmlp = jax.nn.silu(hmlp @ w2 + b2)
        filters = hmlp @ w3 * jnp.exp(-t[:, None] * jnp.abs(filt_bias)[None, :])
        v = streams[-1]
        for i in range(DEPTH - 1):
            v = v * streams[i]
            v = _fftconv(v, filters[i], filt_bias)
        out = (v * streams[0]).transpose(0, 2, 1) @ w_out + b_out
        return out

    def _L0_xattn_ref(x1, x2, W, b):
        import jax, jax.numpy as jnp
        import numpy as np
        D1, D2, D3 = (256, 256, 256)
        d1 = x1.shape[-1]
        W1 = W[:, :d1]
        W2 = W[:, d1:]
        part1 = jnp.einsum('bld,ed->ble', x1, W1)
        part2 = jnp.einsum('bld,ed->be', x2, W2) / x2.shape[1]
        return part1 + part2[:, None, :] + b

    def _L0_ffn_ref(x, w1, conv_w, conv_b, w2):
        import jax, jax.numpy as jnp
        import numpy as np
        B, S, D_MODEL, D_HIDDEN = (4, 512, 256, 1024)

        def act_quant(x):
            scale = 127.0 / jnp.clip(jnp.max(jnp.abs(x), axis=-1, keepdims=True), 1e-05)
            return jnp.clip(jnp.round(x * scale), -128, 127) / scale

        def weight_quant(w):
            scale = 1.0 / jnp.clip(jnp.mean(jnp.abs(w)), 1e-05)
            return jnp.clip(jnp.round(w * scale), -1, 1) / scale

        def bit_linear(x, w):
            xq = x + jax.lax.stop_gradient(act_quant(x) - x)
            wq = w + jax.lax.stop_gradient(weight_quant(w) - w)
            return jnp.einsum('bsd,hd->bsh', xq, wq)

        def depthwise_conv1d(x_bcl, w, b):
            y = jax.lax.conv_general_dilated(x_bcl, w, window_strides=(1,), padding=[(1, 1)], dimension_numbers=('NCH', 'OIH', 'NCH'), feature_group_count=x_bcl.shape[1])
            return y + b[None, :, None]
        h = bit_linear(x, w1)
        h = depthwise_conv1d(h.transpose(0, 2, 1), conv_w, conv_b)
        h = h.transpose(0, 2, 1)
        h = jax.nn.silu(h)
        return bit_linear(h, w2)

    def _L1_attn_ref(x, W_in, conv_w, conv_b, W_out):
        import jax, jax.numpy as jnp
        import numpy as np
        from jax import lax
        B, L, D = (4, 1024, 256)
        EXPAND, K = (2, 4)
        INNER = D * EXPAND
        h = jnp.einsum('bld,df->blf', x, W_in)
        a, g = jnp.split(h, 2, axis=-1)
        h = a * jax.nn.sigmoid(g)
        hc = jnp.transpose(h, (0, 2, 1))
        y = lax.conv_general_dilated(hc, conv_w, window_strides=(1,), padding=[(K - 1, 0)], dimension_numbers=('NCH', 'OIH', 'NCH'), feature_group_count=INNER) + conv_b[None, :, None]
        y = jax.nn.silu(y)
        y = jnp.transpose(y, (0, 2, 1))
        return jnp.einsum('blf,fd->bld', y, W_out)

    def _L1_xattn_ref(query, key, value, Wq, bq, Wk, bk, Wv, bv, Wo, bo):
        import jax, jax.numpy as jnp
        import numpy as np
        B, S, D, H = (2, 512, 256, 16)
        DK = D // H
        b = query.shape[0]
        q = (query @ Wq + bq).reshape(b, -1, H, DK).transpose(0, 2, 1, 3)
        k = (key @ Wk + bk).reshape(b, -1, H, DK).transpose(0, 2, 1, 3)
        v = (value @ Wv + bv).reshape(b, -1, H, DK).transpose(0, 2, 1, 3)
        scores = jnp.einsum('bhqd,bhkd->bhqk', q, k) / jnp.sqrt(jnp.float32(DK))
        attn = jax.nn.softmax(scores, axis=-1)
        x = jnp.einsum('bhqk,bhkd->bhqd', attn, v)
        x = x.transpose(0, 2, 1, 3).reshape(b, -1, H * DK)
        return x @ Wo + bo

    def _L1_ffn_ref(x, w_freq_real, w_freq_imag, bias):
        import jax, jax.numpy as jnp
        import numpy as np
        B, N, D = (4, 512, 256)
        SPARSITY = 0.01
        w = jax.lax.complex(w_freq_real, w_freq_imag)
        x_freq = jnp.fft.fft(x, axis=-1)
        y_freq = jnp.einsum('bnd,do->bno', x_freq, w)
        y = jnp.real(jnp.fft.ifft(y_freq, axis=-1))
        return y + bias
    x = _layernorm(x + _L0_attn_ref(x, L0_attn_w_in, L0_attn_b_in, L0_attn_w_conv, L0_attn_b_conv, L0_attn_w1, L0_attn_b1, L0_attn_w2, L0_attn_b2, L0_attn_w3, L0_attn_filt_bias, L0_attn_w_out, L0_attn_b_out), axis=-1)
    x = _layernorm(x + _L0_xattn_ref(x, ctx_1024, L0_xattn_W, L0_xattn_b), axis=-1)
    x = _layernorm(x + _L0_ffn_ref(x, L0_ffn_w1, L0_ffn_conv_w, L0_ffn_conv_b, L0_ffn_w2), axis=-1)
    x = _layernorm(x + _L1_attn_ref(x, L1_attn_W_in, L1_attn_conv_w, L1_attn_conv_b, L1_attn_W_out), axis=-1)
    x = _layernorm(x + _L1_xattn_ref(x, ctx_1024, ctx_1024, L1_xattn_Wq, L1_xattn_bq, L1_xattn_Wk, L1_xattn_bk, L1_xattn_Wv, L1_xattn_bv, L1_xattn_Wo, L1_xattn_bo), axis=-1)
    x = _layernorm(x + _L1_ffn_ref(x, L1_ffn_w_freq_real, L1_ffn_w_freq_imag, L1_ffn_bias), axis=-1)
    return x

_drawn_inputs = setup_inputs


def setup_inputs(seed=0):
    import zlib

    import numpy as np

    out = dict(_drawn_inputs(seed))
    spreads = {'L0_attn_b_in': (0.0, 0.573),
     'L0_attn_b_conv': (0.0, 0.76),
     'L0_attn_b1': (0.0, 0.8),
     'L0_attn_b2': (0.0, 0.8),
     'L0_attn_b_out': (0.0, 2.0),
     'L1_xattn_bq': (0.0, 0.392),
     'L1_xattn_bk': (0.0, 2.0),
     'L1_xattn_bv': (0.0, 0.1),
     'L1_xattn_bo': (0.0, 0.1)}
    factors = {'L0_attn_w2': 8.0,
     'L0_attn_w3': 6.678,
     'L0_attn_filt_bias': 2.91,
     'L0_xattn_b': 2.838,
     'L1_attn_W_in': 8.0,
     'L1_attn_conv_w': 8.0,
     'L1_attn_conv_b': 8.0,
     'L1_attn_W_out': 8.0,
     'L1_ffn_bias': 6.927}
    for name, (base, spread) in spreads.items():
        noise = np.random.default_rng([zlib.crc32(name.encode()), seed]).standard_normal(out[name].shape)
        drawn = base * np.exp(spread * noise) if base else spread * noise
        out[name] = jnp.asarray(drawn.astype(out[name].dtype))
    for name, factor in factors.items():
        out[name] = (out[name] * factor).astype(out[name].dtype)
    return out
```

```python
from contextlib import ExitStack

import numpy as np

import concourse.bass as bass
from concourse import mybir

P = 128
B, S, D = 4, 512, 256
KD = D // P
NT = S // P
SLOTS = 2
CTX = 64
HEADS, DK = 16, 16
HG = P // DK
HID = 1024
KM = HID // P
INNER = 512
KI = INNER // P
FW = 64
TAPS0, TAPS_F, TAPS1 = 3, 3, 4
EPS = 1e-5
MAGIC = 1.5 * 2.0 ** 23
VW = DK + 1

F32, F32R, BF16 = mybir.dt.float32, mybir.dt.float32r, mybir.dt.bfloat16
ALU = mybir.AluOpType
ACT = mybir.ActivationFunctionType
AX = mybir.AxisListType.X

TURNS = {
    0: ["x1.0", "u.2", "y.0", "x2.0", "x3.0", "g.2", "g.6", "f.0", "a.0", "a.2", "j.0"]
    + [f"pT.{i}" for i in range(8)] + ["k.0", "m.0"],
    1: ["x1.1", "u.3", "y.1", "x2.1", "x3.1", "g.3", "g.7", "f.1", "t.0", "t.2", "j.1"]
    + [f"pv.{t}" for t in range(4)] + ["k.1", "m.1"],
    2: ["u.0", "v.0", "o.0", "e.0", "g.0", "g.4", "amax", "x4.0", "a.1", "a.3", "x5.0", "q.0"]
    + [f"s.{i}" for i in range(0, 8, 2)] + ["oT.0", "x6.0"],
    3: ["u.1", "v.1", "o.1", "e.1", "g.1", "g.5", "scale", "x4.1", "t.1", "t.3", "x5.1", "q.1"]
    + [f"s.{i}" for i in range(1, 8, 2)] + ["oT.1", "x6.1"],
}
TURN = {name: (bank, n) for bank, names in TURNS.items() for n, name in enumerate(names)}

JOBS = [("filt1", "act"), ("filt2", "act"), ("filt3", "act"), ("w1T", "dve"), ("w2T", "act"), ("ctxT", "act"),
        ("kT", "dve"), ("v.0", "dve"), ("v.1", "dve"), ("part2", "dve"), ("abssum", "dve"),
        ("fA", "act"), ("fB", "act")]
JOBS += [(f"q1.{i}", "act") for i in range(4)] + [("fM", "dve")] + [(f"q2.{i}", "dve") for i in range(4)]
JOB = {name: (n, sum(e == eng for _, e in JOBS[:n])) for n, (name, eng) in enumerate(JOBS)}
READER = dict(JOBS)
POOL_CONSTS = 9
U_ORDER = (0, 2, 1, 3)
UNITS = 2 * NT


def build(nc, x, ctx_in, w_in, b_in, w_conv, b_conv, fw1, fb1, fw2, fb2, fw3, filt_bias, w_out, b_out,
          xw, xb, w1, cw, cb, w2, W_in, cw1, cb1, W_out, Wq, bq, Wk, bk, Wv, bv, Wo, bo, wfr, wfi, fbias,
          eye, dft, head_mask, time0, out):
    with ExitStack() as ctx:
        def sb(name, shape, dt=F32):
            return ctx.enter_context(nc.sbuf_tensor(name, shape, dt))

        def sem(name):
            return ctx.enter_context(nc.semaphore(name))

        def sems(name):
            return [sem(f"{name}{s}") for s in range(SLOTS)]

        bank = [[ctx.enter_context(nc.psum_tensor(f"bank{s}{b}", [P, S], F32)) for b in range(4)]
                for s in range(SLOTS)]

        bank_full = [[sem(f"bank_full{s}{b}") for b in range(4)] for s in range(SLOTS)]
        bank_read = [[sem(f"bank_read{s}{b}") for b in range(4)] for s in range(SLOTS)]
        mid_ready = sems("mid_ready")
        v_ready = sems("v_ready")
        z_ready = sems("z_ready")
        var_ready = sems("var_ready")
        rstd_ready = sems("rstd_ready")
        shift_ready = sems("shift_ready")
        xn_ready = sems("xn_ready")
        xq_ready = sems("xq_ready")
        xhi_ready = sems("xhi_ready")
        gmid_ready = sems("gmid_ready")
        hid_ready = sems("hid_ready")
        colmax_ready = sems("colmax_ready")
        scale_ready = sems("scale_ready")
        diag_ready = sems("diag_ready")
        scaled_ready = sems("scaled_ready")
        hq_ready = sems("hq_ready")
        conv_ready = sems("conv_ready")
        y_ready = sems("y_ready")
        p_ready = sems("p_ready")
        stored = sems("stored")
        vec_step = sem("vec_step")
        at_end = sem("at_end")
        first_cleared, last_cleared = bank_full[0][0], at_end

        restart = sem("restart")
        x_loaded = sems("x_loaded")
        w_loaded = {n: sem(f"ld_{n}") for n in
                    ("eye", "win", "uconst", "filter", "wout", "xw", "ctx", "w1", "w2", "bias", "kv", "dft",
                     "cffn", "W_in", "c1", "W_out", "attn")}
        job_done = sem("job_done")
        job_read = {"act": sem("job_read_act"), "dve": sem("job_read_dve")}
        consts_set = sem("consts_set")
        hrow_zeroed = sem("hrow_zeroed")
        wsum_ready = sem("wsum_ready")
        csum_ready = sem("csum_ready")
        ctxT2_ready = sem("ctxT2_ready")
        ternary_ready = sem("ternary_ready")
        rows_split = sem("rows_split")
        kbd_ready = sem("kbd_ready")
        prep_step = sem("prep_step")
        prep_done = sem("prep_done")
        filt_step = sem("filt_step")
        h_stored = sem("h_stored")
        toep_loaded = sem("toep_loaded")
        rows_loaded = sem("rows_loaded")

        eye_sb = sb("eye_sb", [P, KD, D])
        ident = eye_sb[:, 0, 0:P]
        ones = sb("ones", [P, P])
        ones_b = sb("ones_b", [P, P], BF16)
        mask_sb = sb("mask_sb", [P, HG])
        halfneg = sb("halfneg", [P, NT])
        w_in_sb = sb("w_in_sb", [P, KD, 4, P])
        uc = sb("uc", [P, 4, TAPS0 + 2])
        fbc = sb("fbc", [P, KD])
        w_out_sb = sb("w_out_sb", [P, KD, D])
        xw1 = sb("xw1", [P, KD, D])
        w1q = sb("w1q", [P, KD, HID], F32R)
        w2q = sb("w2q", [P, KM, D], BF16)
        fc = sb("fc", [P, KM, TAPS_F + 1])
        fcs = sb("fcs", [P, KM, TAPS_F])
        W_in_sb = sb("W_in_sb", [P, KD, 2 * INNER])
        ac = sb("ac", [P, KI, TAPS1 + 1])
        acs = sb("acs", [P, KI, TAPS1])
        W_out_sb = sb("W_out_sb", [P, KI, D])
        wq_sb = sb("wq_sb", [P, KD, D])
        bq_sb = sb("bq_sb", [P, KD])
        bk_sb = sb("bk_sb", [P, KD])
        wo_sb = sb("wo_sb", [P, KD, D])
        kbd = sb("kbd", [P, B, KD, HG * CTX])
        vbd = sb("vbd", [P, B, HEADS // 2, 2 * VW])
        fm = sb("fm", [P, KD, D])
        toep = sb("toep", [P, 3 * P])
        rows3 = sb("rows3", [P, 7, D], BF16)
        hrow = sb("hrow", [1, 4 * P])
        wsum = sb("wsum", [P, 2])
        wmean = sb("wmean", [P, 2])
        wscale = sb("wscale", [P, 2])
        ffn_mean = sb("ffn_mean", [P, 1])

        xin = [sb(f"xin{s}", [P, NT, D]) for s in range(SLOTS)]
        xn = [sb(f"xn{s}", [P, NT, D]) for s in range(SLOTS)]
        xT = [sb(f"xT{s}", [P, KD, S]) for s in range(SLOTS)]
        xhi = [sb(f"xhi{s}", [P, KD, S], F32R) for s in range(SLOTS)]
        xlo = [sb(f"xlo{s}", [P, KD, S], F32R) for s in range(SLOTS)]
        res = [sb(f"res{s}", [P, NT, D]) for s in range(SLOTS)]
        stats = [sb(f"stats{s}", [P, NT, 6]) for s in range(SLOTS)]
        mv = [sb(f"mv{s}", [P, NT, 2]) for s in range(SLOTS)]
        vareps = [sb(f"vareps{s}", [P, NT]) for s in range(SLOTS)]
        rstd = [sb(f"rstd{s}", [P, NT]) for s in range(SLOTS)]
        shift = [sb(f"shift{s}", [P, NT]) for s in range(SLOTS)]
        amax = [sb(f"amax{s}", [P, 4, NT]) for s in range(SLOTS)]
        amax2 = [sb(f"amax2{s}", [P, 4, NT]) for s in range(SLOTS)]
        ARENA = 15 * S + S // 2
        arena = [sb(f"arena{s}", [P, ARENA]) for s in range(SLOTS)]

        def carve(s, at, *shape, dt=F32):
            n = int(np.prod(shape)) * (2 if dt == BF16 else 4) // 4
            assert at + n <= ARENA, (at, n)
            a = arena[s][:, at:at + n]
            if dt == BF16:
                a = a.bitcast(BF16)
            if len(shape) == 2:
                a = a.rearrange("p (a b) -> p a b", a=shape[0])
            return a

        PADW = S + 4
        pad = [sb(f"pad{s}", [P, 4, PADW]) for s in range(SLOTS)]
        uconv = [carve(s, 0, 4, S) for s in range(SLOTS)]
        v1 = [carve(s, 4 * S, KD, S) for s in range(SLOTS)]
        vn = [carve(s, 6 * S, NT, D) for s in range(SLOTS)]
        z1 = [carve(s, 8 * S, KD, S) for s in range(SLOTS)]
        gconv = [carve(s, 0, 2, S) for s in range(SLOTS)]
        hid = [carve(s, 2 * S, KM, S) for s in range(SLOTS)]
        hq = [carve(s, 10 * S, KM, S, dt=BF16) for s in range(SLOTS)]
        diag = [carve(s, 14 * S, NT, P) for s in range(SLOTS)]
        colmax = [sb(f"colmax{s}", [P, 2, S]) for s in range(SLOTS)]
        th = [carve(s, 0, 2, S) for s in range(SLOTS)]
        aconv = [carve(s, 2 * S, 2, S) for s in range(SLOTS)]
        y4 = [carve(s, 4 * S, KI, S) for s in range(SLOTS)]
        qT = [carve(s, 0, KD, S) for s in range(SLOTS)]
        sub = [carve(s, 2 * S, 2, S) for s in range(SLOTS)]
        prob = [carve(s, 4 * S, 2, S) for s in range(SLOTS)]
        pT = [carve(s, 6 * S, 2, S) for s in range(SLOTS)]
        o5 = [carve(s, 8 * S, NT, D) for s in range(SLOTS)]
        oT = [carve(s, 10 * S, KD, S) for s in range(SLOTS)]
        smax = [sb(f"smax{s}", [P, 2, HG]) for s in range(SLOTS)]
        rsum = [sb(f"rsum{s}", [P, HEADS]) for s in range(SLOTS)]
        outb = [carve(s, 12 * S, NT, D) for s in range(SLOTS)]

        w1_nat = carve(0, 0, KM, D)
        w2_nat = carve(0, 4 * S, KD, HID)
        xw_nat = carve(0, 8 * S, KD, 2 * D)
        wk_sb = carve(0, 10 * S, KD, D)
        wv_sb = carve(0, 11 * S, KD, D)
        dft_sb = carve(0, 12 * S, 3 * KD, D)
        wf_nat = [carve(1, i * S, KD, D) for i in range(2)]
        fAB = [carve(1, 2 * S + i * S, KD, D) for i in range(2)]
        ctx_nat = carve(1, 4 * S, 2, D)
        ctxT = carve(1, 5 * S, KD, B * CTX)
        ctxT2 = carve(1, 6 * S, KD, B * 2 * CTX)
        xw2 = carve(1, 8 * S, KD, D)
        kT = carve(1, 9 * S, KD, B * CTX)
        bvb = carve(1, 10 * S, D)
        csum = carve(1, 10 * S + D, KD * B)
        fmlp = carve(1, 11 * S, 3 * D)
        brow = [carve(1, 13 * S + i * D, D) for i in range(3)]
        brow_b = [carve(1, 14 * S + D + i * D // 2, D, dt=BF16) for i in range(3)]
        toep_rev = colmax[0][:, 0, 0:3 * P]

        fw1b, fw2_sb, fw3_sb = fmlp[0:4, 0:FW], fmlp[0:FW, FW:2 * FW], fmlp[0:FW, 2 * FW:2 * FW + D]
        f_t0, f_h1, f_h2, f_b2 = (fmlp[0:n, 500 + i:501 + i] for i, n in enumerate((4, FW, FW, FW)))

        h_dram = nc.dram_tensor("h_padded", (4 * P,), F32, kind="Internal")

        def wait_full(eng, s, name):
            b, n = TURN[name]
            eng.wait_ge(bank_full[s][b], n + 1)

        def wait_read(eng, s, name):
            b, n = TURN[name]
            eng.wait_ge(bank_read[s][b], n + 1)

        def read_by(s, name, ins):
            ins.then_inc(bank_read[s][TURN[name][0]], 1)

        def job_bank(name):
            n = JOB[name][0] % 8
            return bank[n // 4][n % 4]

        def wait_job_read(eng, name):
            eng.wait_ge(job_read[READER[name]], JOB[name][1] + 1)

        def two(p):
            return p[:].rearrange("p (a d) -> p a d", a=2)

        def psum(s, name):
            return bank[s][TURN[name][0]]

        block = ctx.enter_context(nc.Block())

        def chunks(w):
            return w.rearrange("(k p) n -> p k n", p=P)

        def column(v):
            return v.rearrange("(c p) -> p c", p=P)

        @block.sync
        def _(sp):
            sp.dma_start(eye_sb[:], chunks(eye)).then_inc(w_loaded["eye"], 16)
            for s in range(SLOTS):
                sp.dma_start(xin[s][:], x[s].rearrange("(t p) d -> p t d", p=P)).then_inc(x_loaded[s], 16)
            with nc.allow_non_contiguous_dma(reason="small per-channel constants"):
                for src, dst in ((fw1, fw1b[0:3]), (fb1.rearrange("(o d) -> o d", o=1), fw1b[3:4]),
                                 (fw2, fw2_sb), (fw3, fw3_sb), (time0, f_t0),
                                 (fb2.rearrange("(p o) -> p o", o=1), f_b2)):
                    sp.dma_start(dst, src).then_inc(w_loaded["filter"], 16)
                for i, c in enumerate((0, 2 * D)):
                    sp.dma_start(w_in_sb[:, :, 2 * i:2 * i + 2, :],
                                 w_in[:, c:c + D].rearrange("(k p) (c n) -> p k c n", p=P, n=P))\
                      .then_inc(w_loaded["win"], 16)
                for i, c in enumerate((0, 2 * D)):
                    e = slice(2 * i, 2 * i + 2)
                    sp.dma_start(uc[:, e, 0:TAPS0], w_conv[c:c + D].rearrange("(c p) o j -> p c (o j)", p=P))\
                      .then_inc(w_loaded["uconst"], 16)
                    sp.dma_start(uc[:, e, TAPS0], column(b_conv[c:c + D])).then_inc(w_loaded["uconst"], 16)
                    sp.dma_start(uc[:, e, TAPS0 + 1], column(b_in[c:c + D])).then_inc(w_loaded["uconst"], 16)
                sp.dma_start(fbc[:], column(filt_bias)).then_inc(w_loaded["uconst"], 16)
                sp.dma_start(w_out_sb[:], chunks(w_out)).then_inc(w_loaded["wout"], 16)
                sp.dma_start(xw_nat, chunks(xw)).then_inc(w_loaded["xw"], 16)
                sp.dma_start(ctx_nat, ctx_in.rearrange("(j b) t d -> (b t) j d", b=2)).then_inc(w_loaded["ctx"], 16)
                for b in range(B):
                    sp.dma_start(brow[0][b:b + 1], xb.rearrange("(o d) -> o d", o=1)).then_inc(w_loaded["bias"], 16)
                for r, v in enumerate((b_out, bo, fbias)):
                    sp.dma_start(brow[0][B + r:B + r + 1], v.rearrange("(o d) -> o d", o=1))\
                      .then_inc(w_loaded["bias"], 16)
                sp.dma_start(w1_nat, chunks(w1)).then_inc(w_loaded["w1"], 16)
                sp.dma_start(w2_nat, chunks(w2)).then_inc(w_loaded["w2"], 16)
                for src, dst in ((chunks(Wk), wk_sb), (chunks(Wv), wv_sb), (column(bk), bk_sb[:]),
                                 (bv.partition_broadcast(P), bvb), (head_mask, mask_sb[:])):
                    sp.dma_start(dst, src).then_inc(w_loaded["kv"], 16)
                sp.dma_start(dft_sb, dft.rearrange("(q p) n -> p q n", p=P)).then_inc(w_loaded["dft"], 16)
                sp.dma_start(wf_nat[0], chunks(wfr)).then_inc(w_loaded["dft"], 16)
                sp.dma_start(wf_nat[1], chunks(wfi)).then_inc(w_loaded["dft"], 16)
                sp.dma_start(fc[:, :, 0:TAPS_F], cw.rearrange("(c p) o j -> p c (o j)", p=P))\
                  .then_inc(w_loaded["cffn"], 16)
                sp.dma_start(fc[:, :, TAPS_F], column(cb)).then_inc(w_loaded["cffn"], 16)
                sp.dma_start(W_in_sb[:], chunks(W_in)).then_inc(w_loaded["W_in"], 16)
                sp.dma_start(ac[:, :, 0:TAPS1], cw1.rearrange("(c p) o j -> p c (o j)", p=P))\
                  .then_inc(w_loaded["c1"], 16)
                sp.dma_start(ac[:, :, TAPS1], column(cb1)).then_inc(w_loaded["c1"], 16)
                sp.dma_start(W_out_sb[:], chunks(W_out)).then_inc(w_loaded["W_out"], 16)
                for src, dst in ((chunks(Wq), wq_sb[:]), (column(bq), bq_sb[:]), (chunks(Wo), wo_sb[:])):
                    sp.dma_start(dst, src).then_inc(w_loaded["attn"], 16)
                sp.wait_ge(job_read["act"], JOB["filt3"][1] + 1)
                sp.dma_start(h_dram.ap().rearrange("(o d) -> o d", o=1), hrow[:]).then_inc(h_stored, 16)
                sp.wait_ge(h_stored, 16)
                sp.dma_start(toep_rev, bass.AP(h_dram, 0, [[1, P], [1, 3 * P]])).then_inc(toep_loaded, 16)
                sp.wait_ge(rows_split, 1)
                sp.wait_ge(consts_set, POOL_CONSTS)
                for i in range(3):
                    sp.dma_start(rows3[i:i + 1], brow_b[i][0:7]).then_inc(rows_loaded, 16)

            def iteration(it, more):
                if more:
                    for s in range(SLOTS):
                        sp.wait_ge(xn_ready[s], NT)
                        sp.dma_start(xin[s][:], x[(it + 1) * SLOTS + s].rearrange("(t p) d -> p t d", p=P))\
                          .then_inc(x_loaded[s], 16)
                for s in range(SLOTS):
                    for h in range(2):
                        wait_read(sp, s, f"m.{h}")
                    sp.dma_start(out[it * SLOTS + s].rearrange("(t p) d -> p t d", p=P), outb[s])\
                      .then_inc(stored[s], 16)
                for s in range(SLOTS):
                    sp.wait_ge(stored[s], 16)
                sp.wait_ge(at_end, 4)
                sp.sem_clear(range(first_cleared.num, last_cleared.num + 1))
                sp.sem_inc(restart, 1)

            with sp.Fori(0, B // SLOTS - 1) as it:
                iteration(it, True)
            iteration(B // SLOTS - 1, False)

        @block.tensor
        def _(pe):
            def job(name):
                n = JOB[name][0]
                if n >= 8:
                    wait_job_read(pe, JOBS[n - 8][0])
                return job_bank(name)

            def done(ins):
                ins.then_inc(job_done, 1)

            pe.wait_ge(w_loaded["filter"], 6 * 16)
            p = job("filt1")
            done(pe.matmul(p[0:FW, 0:1], fw1b, f_t0, start=True, stop=True))
            wait_job_read(pe, "filt1")
            p = job("filt2")
            done(pe.matmul(p[0:FW, 0:1], fw2_sb, f_h1, start=True, stop=True))
            wait_job_read(pe, "filt2")
            p = job("filt3")
            done(pe.matmul(p[0:1, 0:D], f_h2, fw3_sb, start=True, stop=True))

            pe.wait_ge(w_loaded["eye"], 16)
            pe.wait_ge(w_loaded["xw"], 16)
            for half, name in enumerate(("w1T", "w2T")):
                p = job(name)
                for k in range(KD):
                    for j in range(KD):
                        last = pe.transpose(p[:, k * D + j * P:k * D + (j + 1) * P],
                                            xw_nat[:, j, half * D + k * P:half * D + (k + 1) * P], ident)
                done(last)
            pe.wait_ge(w_loaded["ctx"], 16)
            p = job("ctxT")
            for k in range(KD):
                for j in range(2):
                    last = pe.transpose(p[:, k * D + j * P:k * D + (j + 1) * P],
                                        ctx_nat[:, j, k * P:(k + 1) * P], ident)
            done(last)
            pe.wait_ge(w_loaded["kv"], 5 * 16)
            wait_job_read(pe, "ctxT")
            p = job("kT")
            for f in range(KD):
                for k in range(KD):
                    last = pe.matmul(p[:, f * B * CTX:(f + 1) * B * CTX], wk_sb[:, k, f * P:(f + 1) * P],
                                     ctxT[:, k, :], start=k == 0, stop=k == KD - 1)
            done(last)
            pe.wait_ge(ctxT2_ready, KD)
            for h in range(2):
                p = job(f"v.{h}")
                for b in range(2):
                    for k in range(KD):
                        last = pe.matmul(p[:, b * D:(b + 1) * D], ctxT2[:, k, (2 * h + b) * P:(2 * h + b + 1) * P],
                                         wv_sb[:, k, :], start=k == 0, stop=k == KD - 1)
                done(last)
            pe.wait_ge(csum_ready, 1)
            wait_job_read(pe, "w2T")
            p = job("part2")
            for k in range(KD):
                last = pe.matmul(p[0:B, 0:D], csum[:, k * B:(k + 1) * B], xw2[:, k, :],
                                 start=k == 0, stop=k == KD - 1)
            done(last)
            pe.wait_ge(consts_set, POOL_CONSTS)
            pe.wait_ge(wsum_ready, 2)
            p = job("abssum")
            done(pe.matmul(p[:, 0:2], ones[:], wsum[:], start=True, stop=True))
            pe.wait_ge(w_loaded["dft"], 3 * 16)
            for name, terms in (("fA", ((0, 0), (1, 1))), ("fB", ((1, 0), (0, 2)))):
                p = job(name)
                for j in range(KD):
                    for n, (w, c) in enumerate(terms):
                        for k in range(KD):
                            last = pe.matmul(p[:, j * D:(j + 1) * D], wf_nat[w][:, k, j * P:(j + 1) * P],
                                             dft_sb[:, c * KD + k, :], start=n == 0 and k == 0,
                                             stop=n == 1 and k == KD - 1)
                done(last)
            pe.wait_ge(ternary_ready, 1)
            for i in range(4):
                p = job(f"q1.{i}")
                k, half = i // 2, i % 2
                for m in range(4):
                    last = pe.transpose(p[:, m * P:(m + 1) * P],
                                        w1_nat[:, half * 4 + m, k * P:(k + 1) * P], ident)
                done(last)
            wait_job_read(pe, "fB")
            p = job("fM")
            for j in range(KD):
                for n, c in enumerate((0, 2)):
                    for k in range(KD):
                        last = pe.matmul(p[:, j * D:(j + 1) * D], fAB[n][:, k, j * P:(j + 1) * P],
                                         dft_sb[:, c * KD + k, :], start=n == 0 and k == 0,
                                         stop=n == 1 and k == KD - 1)
            done(last)
            pe.wait_ge(ternary_ready, 2)
            for i in range(4):
                p = job(f"q2.{i}")
                for m in range(2):
                    for j in range(KD):
                        last = pe.transpose(p[:, m * D + j * P:m * D + (j + 1) * P],
                                            w2_nat[:, j, (2 * i + m) * P:(2 * i + m + 1) * P], ident)
                done(last)
            wait_job_read(pe, [n for n, e in JOBS if e == "act"][-1])
            wait_job_read(pe, [n for n, e in JOBS if e == "dve"][-1])
            for name, n in (("win", 2), ("wout", 1), ("W_in", 1), ("W_out", 1), ("attn", 3)):
                pe.wait_ge(w_loaded[name], 16 * n)
            pe.wait_ge(prep_done, 1)
            pe.wait_ge(rows_loaded, 3 * 16)
            pe.wait_ge(kbd_ready, B * KD)

            def take(s, name):
                b, n = TURN[name]
                if n:
                    pe.wait_ge(bank_read[s][b], n)
                return bank[s][b]

            def fill(s, name, ins):
                ins.then_inc(bank_full[s][TURN[name][0]], 1)

            def transpose_x(s, layer, src, wait):
                for k in range(KD):
                    p = take(s, f"{layer}.{k}")
                    for t in range(NT):
                        if k == 0:
                            wait(t)
                        last = pe.transpose(p[:, t * P:(t + 1) * P], src[:, t, k * P:(k + 1) * P], ident)
                    fill(s, f"{layer}.{k}", last)

            def project(s, name, lhs, weights, nk, wait, row=None):
                for h in range(2):
                    p = take(s, f"{name}.{h}")
                    for t in range(2):
                        tt = 2 * h + t
                        o = p[:, t * D:(t + 1) * D]
                        for k in range(nk):
                            if tt == 0:
                                wait(k)
                            last = pe.matmul(o, lhs[:, k, tt * P:(tt + 1) * P], weights[:, k, :],
                                             start=k == 0, stop=row is None and k == nk - 1)
                        if row is not None:
                            last = pe.matmul(o, ones_b[:], row, start=False, stop=True)
                    fill(s, f"{name}.{h}", last)

            with pe.Fori(0, B // SLOTS) as it:
                for s in range(SLOTS):
                    pe.wait_ge(x_loaded[s], it * 16 + 16)
                    transpose_x(s, "x1", xin[s], lambda t: None)
                for s in range(SLOTS):
                    for n, e in enumerate(U_ORDER):
                        p = take(s, f"u.{e}")
                        for k in range(KD):
                            if n == 0:
                                wait_read(pe, s, f"x1.{k}")
                            last = pe.matmul(p[:], w_in_sb[:, k, e, :], xT[s][:, k, :], start=k == 0, stop=k == 1)
                        fill(s, f"u.{e}", last)
                for s in range(SLOTS):
                    for h in range(2):
                        p = take(s, f"v.{h}")
                        for t in range(2):
                            for k in range(KD):
                                if h == 0 and t == 0:
                                    pe.wait_ge(v_ready[s], k + 1)
                                last = pe.transpose(p[:, t * D + k * P:t * D + (k + 1) * P],
                                                    v1[s][:, k, (2 * h + t) * P:(2 * h + t + 1) * P], ident)
                        fill(s, f"v.{h}", last)
                for s in range(SLOTS):
                    for k in range(KD):
                        p = take(s, f"y.{k}")
                        for t in range(NT):
                            if k == 0 and t % 2 == 0:
                                wait_read(pe, s, f"v.{t // 2}")
                            n = min(3 * P, S - t * P)
                            last = pe.matmul(p[:, t * P:t * P + n], vn[s][:, t, k * P:(k + 1) * P], toep[:, 0:n],
                                             start=t == 0, stop=t == NT - 1, skip_group_check=True)
                        fill(s, f"y.{k}", last)
                for s in range(SLOTS):
                    project(s, "o", z1[s], w_out_sb, KD, lambda k, s=s: pe.wait_ge(z_ready[s], k + 1), rows3[:, B, :])
                for s in range(SLOTS):
                    transpose_x(s, "x2", xn[s], lambda t, s=s: pe.wait_ge(xn_ready[s], t + 1))
                for s in range(SLOTS):
                    project(s, "e", xT[s], xw1, KD, lambda k, s=s: wait_read(pe, s, f"x2.{k}"),
                            rows3[:, it * SLOTS + s, :])
                for s in range(SLOTS):
                    transpose_x(s, "x3", res[s], lambda t, s=s: pe.wait_ge(xq_ready[s], t + 1))
                for s in range(SLOTS):
                    for m in range(KM):
                        p = take(s, f"g.{m}")
                        for part, buf in enumerate((xhi[s], xlo[s])):
                            for k in range(KD):
                                if m == 0 and part == 0:
                                    pe.wait_ge(xhi_ready[s], k + 1)
                                if m == 0 and part == 1:
                                    wait_read(pe, s, f"x3.{k}")
                                last = pe.matmul(p[:], w1q[:, k, m * P:(m + 1) * P], buf[:, k, :],
                                                 start=part + k == 0, stop=part + k == 2)
                        fill(s, f"g.{m}", last)
                for s in range(SLOTS):
                    p = take(s, "amax")
                    pe.wait_ge(colmax_ready[s], 1)
                    for t in range(NT):
                        last = pe.transpose(p[:, t * P:(t + 1) * P], colmax[s][:, 0, t * P:(t + 1) * P], ident)
                    fill(s, "amax", last)
                for s in range(SLOTS):
                    p = take(s, "scale")
                    for t in range(NT):
                        pe.wait_ge(diag_ready[s], t + 1)
                        last = pe.matmul(p[:, t * P:(t + 1) * P], ones[:], diag[s][:, t, :], start=True, stop=True)
                    fill(s, "scale", last)
                for s in range(SLOTS):
                    project(s, "f", hq[s], w2q, KM, lambda k, s=s: pe.wait_ge(hq_ready[s], k + 1))
                for s in range(SLOTS):
                    transpose_x(s, "x4", xn[s], lambda t, s=s: pe.wait_ge(xn_ready[s], NT + t + 1))
                for s in range(SLOTS):
                    for m in range(KI):
                        for name, c in ((f"t.{m}", INNER), (f"a.{m}", 0)):
                            p = take(s, name)
                            for k in range(KD):
                                if m == 0 and c:
                                    wait_read(pe, s, f"x4.{k}")
                                last = pe.matmul(p[:], W_in_sb[:, k, c + m * P:c + (m + 1) * P], xT[s][:, k, :],
                                                 start=k == 0, stop=k == 1)
                            fill(s, name, last)
                for s in range(SLOTS):
                    project(s, "j", y4[s], W_out_sb, KI, lambda k, s=s: pe.wait_ge(y_ready[s], k + 1))
                for s in range(SLOTS):
                    transpose_x(s, "x5", xn[s], lambda t, s=s: pe.wait_ge(xn_ready[s], 2 * NT + t + 1))
                for s in range(SLOTS):
                    for f in range(KD):
                        p = take(s, f"q.{f}")
                        for k in range(KD):
                            if f == 0:
                                wait_read(pe, s, f"x5.{k}")
                            last = pe.matmul(p[:], wq_sb[:, k, f * P:(f + 1) * P], xT[s][:, k, :],
                                             start=k == 0, stop=k == 1)
                        fill(s, f"q.{f}", last)
                for i in range(UNITS + 2):
                    for s in range(SLOTS):
                        if i < UNITS:
                            t, g = i // 2, i % 2
                            p = take(s, f"s.{i}")
                            wait_read(pe, s, f"q.{g}")
                            fill(s, f"s.{i}", pe.matmul(p[:], qT[s][:, g, t * P:(t + 1) * P],
                                                        kbd[:, it * SLOTS + s, g, :], start=True, stop=True))
                        if 0 <= i - 1 < UNITS:
                            n = i - 1
                            p = take(s, f"pT.{n}")
                            pe.wait_ge(p_ready[s], n + 1)
                            for c in range(4):
                                last = pe.transpose(p[:, c * P:(c + 1) * P], prob[s][:, n % 2, c * P:(c + 1) * P],
                                                    ident)
                            fill(s, f"pT.{n}", last)
                        if i >= 2:
                            n = i - 2
                            t, g = n // 2, n % 2
                            p = take(s, f"pv.{t}") if g == 0 else psum(s, f"pv.{t}")
                            wait_read(pe, s, f"pT.{n}")
                            for c in range(4):
                                j = 4 * g + c
                                last = pe.matmul(p[:, j * 2 * VW:(j + 1) * 2 * VW],
                                                 pT[s][:, n % 2, c * P:(c + 1) * P],
                                                 vbd[:, it * SLOTS + s, j, :], start=True, stop=True)
                            if g == 1:
                                fill(s, f"pv.{t}", last)
                for s in range(SLOTS):
                    transpose_x(s, "oT", o5[s], lambda t, s=s: wait_read(pe, s, f"pv.{t}"))
                for s in range(SLOTS):
                    project(s, "k", oT[s], wo_sb, KD, lambda k, s=s: wait_read(pe, s, f"oT.{k}"), rows3[:, B + 1, :])
                for s in range(SLOTS):
                    transpose_x(s, "x6", xn[s], lambda t, s=s: pe.wait_ge(xn_ready[s], 3 * NT + t + 1))
                for s in range(SLOTS):
                    project(s, "m", xT[s], fm, KD, lambda k, s=s: wait_read(pe, s, f"x6.{k}"), rows3[:, B + 2, :])
                pe.drain().then_inc(at_end, 1)
                pe.wait_ge(restart, it + 1)

        @block.scalar
        def _(act):
            def job(name):
                act.wait_ge(job_done, JOB[name][0] + 1)
                return job_bank(name)

            def read(ins):
                ins.then_inc(job_read["act"], 1)

            p = job("filt1")
            read(act.activation(f_h1, p[0:FW, 0:1], ACT.Silu))
            p = job("filt2")
            read(act.activation(f_h2, p[0:FW, 0:1], ACT.Silu, bias=f_b2))
            act.wait_ge(hrow_zeroed, 1)
            p = job("filt3")
            read(act.activation(hrow[:, 3 * P - 1:3 * P - 1 - D:-1], p[0:1, 0:D], ACT.Copy))
            p = job("w2T")
            read(act.activation(xw2, two(p), ACT.Copy))
            p = job("ctxT")
            for k in range(KD):
                act.activation(ctxT2[:, k, :].rearrange("p (b r t) -> p b r t", b=B, r=2),
                               p[:, k * D:(k + 1) * D].rearrange("p (b t) -> p b t", b=B).unsqueeze(2)
                               .broadcast_to([P, B, 2, CTX]), ACT.Copy).then_inc(ctxT2_ready, 1)
            read(act.activation(ctxT, two(p), ACT.Copy))
            for i, name in enumerate(("fA", "fB")):
                p = job(name)
                read(act.activation(fAB[i], two(p), ACT.Copy))
            for i in range(4):
                p = job(f"q1.{i}")
                k, half = i // 2, i % 2
                read(act.activation(w1q[:, k, half * S:(half + 1) * S], p[:], ACT.Copy))
            act.wait_ge(prep_done, 1)
            act.wait_ge(w_loaded["uconst"], 7 * 16)
            act.wait_ge(w_loaded["cffn"], 2 * 16)
            act.wait_ge(w_loaded["attn"], 3 * 16)

            def copy_xT(s, layer, to):
                for k in range(KD):
                    wait_full(act, s, f"{layer}.{k}")
                    read_by(s, f"{layer}.{k}", act.activation(to[:, k, :], psum(s, f"{layer}.{k}")[:], ACT.Copy))

            def normalise(s, name, layer_norm, to):
                act.wait_ge(rstd_ready[s], layer_norm)
                act.wait_ge(shift_ready[s], 1 if layer_norm == 2 else 2)
                for t in range(NT):
                    ins = act.activation(to[:, t, :], psum(s, f"{name}.{t // 2}")[:, t % 2 * D:(t % 2 + 1) * D],
                                         ACT.Identity, bias=shift[s][:, t:t + 1], scale=rstd[s][:, t:t + 1])
                    if t % 2:
                        read_by(s, f"{name}.{t // 2}", ins)

            with act.Fori(0, B // SLOTS) as it:
                for s in range(SLOTS):
                    copy_xT(s, "x1", xT[s])
                for s in range(SLOTS):
                    for e in U_ORDER:
                        wait_full(act, s, f"u.{e}")
                        read_by(s, f"u.{e}", act.activation(pad[s][:, e, 4:], psum(s, f"u.{e}")[:], ACT.Identity,
                                                            bias=uc[:, e, TAPS0 + 1:TAPS0 + 2]))
                for s in range(SLOTS):
                    for h in range(2):
                        wait_full(act, s, f"v.{h}")
                        read_by(s, f"v.{h}", act.activation(vn[s][:, 2 * h:2 * h + 2, :], two(psum(s, f"v.{h}")),
                                                            ACT.Copy))
                for s in range(SLOTS):
                    copy_xT(s, "x2", xT[s])
                for s in range(SLOTS):
                    normalise(s, "e", 2, xn[s])
                for s in range(SLOTS):
                    for k in range(KD):
                        wait_full(act, s, f"x3.{k}")
                        act.activation(xhi[s][:, k, :], psum(s, f"x3.{k}")[:], ACT.Copy).then_inc(xhi_ready[s], 1)
                for s in range(SLOTS):
                    for m in range(KM + 1):
                        if m < KM:
                            wait_full(act, s, f"g.{m}")
                            if m >= 2:
                                act.wait_ge(hid_ready[s], m - 1)
                            act.activation(gconv[s][:, m % 2, :], psum(s, f"g.{m}")[:], ACT.Identity,
                                           bias=fc[:, m, TAPS_F:TAPS_F + 1], scale=fcs[:, m, 1:2])\
                               .then_inc(gmid_ready[s], 1)
                        if m >= 1:
                            wait_read(act, s, f"g.{m - 1}")
                            act.activation(hid[s][:, m - 1, :], gconv[s][:, (m - 1) % 2, :], ACT.Silu)\
                               .then_inc(hid_ready[s], 1)
                for s in range(SLOTS):
                    wait_full(act, s, "scale")
                    read_by(s, "scale", act.activation(colmax[s][:, 1, :], psum(s, "scale")[:], ACT.Copy))
                for s in range(SLOTS):
                    copy_xT(s, "x4", xT[s])
                for s in range(SLOTS):
                    for m in range(KI + 1):
                        if m < KI:
                            wait_full(act, s, f"t.{m}")
                            if m >= 2:
                                wait_read(act, s, f"a.{m - 2}")
                            read_by(s, f"t.{m}", act.activation(th[s][:, m % 2, :], psum(s, f"t.{m}")[:], ACT.Tanh,
                                                                scale=0.5))
                        if m >= 1:
                            act.wait_ge(conv_ready[s], m)
                            act.activation(y4[s][:, m - 1, :], aconv[s][:, (m - 1) % 2, :], ACT.Silu)\
                               .then_inc(y_ready[s], 1)
                for s in range(SLOTS):
                    copy_xT(s, "x5", xT[s])
                for s in range(SLOTS):
                    for f in range(KD):
                        wait_full(act, s, f"q.{f}")
                        read_by(s, f"q.{f}", act.activation(qT[s][:, f, :], psum(s, f"q.{f}")[:], ACT.Identity,
                                                            bias=bq_sb[:, f:f + 1]))
                for i in range(UNITS + 1):
                    for s in range(SLOTS):
                        if i < UNITS:
                            wait_read(act, s, f"s.{i}")
                            act.activation(prob[s][:, i % 2, :], sub[s][:, i % 2, :], ACT.Exp).then_inc(p_ready[s], 1)
                        if i >= 1:
                            wait_full(act, s, f"pT.{i - 1}")
                            read_by(s, f"pT.{i - 1}", act.activation(pT[s][:, (i - 1) % 2, :],
                                                                     psum(s, f"pT.{i - 1}")[:], ACT.Copy))
                for s in range(SLOTS):
                    copy_xT(s, "oT", oT[s])
                for s in range(SLOTS):
                    copy_xT(s, "x6", xT[s])
                for s in range(SLOTS):
                    normalise(s, "m", 6, outb[s])
                act.drain().then_inc(at_end, 1)
                act.wait_ge(restart, it + 1)

        @block.gpsimd
        def _(pool):
            for n, (buf, value) in enumerate(((ones[:], 1.0), (ones_b[:], 1.0), (halfneg[:], -0.5), (rows3[:], 0.0),
                                              (vbd[:], 0.0), (pad[0][:, :, 0:4], 0.0), (pad[1][:, :, 0:4], 0.0))):
                pool.memset(buf, value).then_inc(consts_set, 1)
            pool.wait_ge(consts_set, 7)
            for half in range(2):
                pool.memset(vbd[64 * half:64 * half + 64, :, :, half * VW + DK], 1.0).then_inc(consts_set, 1)
            pool.wait_ge(consts_set, POOL_CONSTS)
            pool.wait_ge(w_loaded["kv"], 5 * 16)
            wait_job_read(pool, "kT")
            for b in range(B):
                for g in range(KD):
                    pool.tensor_tensor(kbd[:, b, g, :].rearrange("p (h t) -> p h t", h=HG),
                                       kT[:, g, b * CTX:(b + 1) * CTX].unsqueeze(1).broadcast_to([P, HG, CTX]),
                                       mask_sb[:].unsqueeze(2).broadcast_to([P, HG, CTX]), ALU.mult)\
                        .then_inc(kbd_ready, 1)
            pool.wait_ge(w_loaded["uconst"], 7 * 16)
            pool.wait_ge(w_loaded["c1"], 2 * 16)
            pool.wait_ge(prep_done, 1)

            def power(s, n):
                pool.wait_ge(var_ready[s], n)
                pool.tensor_tensor(rstd[s][:], vareps[s][:], halfneg[:], ALU.pow).then_inc(rstd_ready[s], 1)

            with pool.Fori(0, B // SLOTS) as it:
                for s in range(SLOTS):
                    for e in U_ORDER:
                        wait_read(pool, s, f"u.{e}")
                        pool.tensor_scalar(uconv[s][:, e, :], pad[s][:, e, 4:], uc[:, e, 2:3], uc[:, e, TAPS0:TAPS0 + 1],
                                           ALU.mult, ALU.add).then_inc(mid_ready[s], 1)
                for n in (1, 2):
                    for s in range(SLOTS):
                        power(s, n)
                for s in range(SLOTS):
                    pool.wait_ge(scale_ready[s], 1)
                    for t in range(NT):
                        pool.tensor_scalar(diag[s][:, t, :], ident, amax2[s][:, 3, t:t + 1], 1.0, ALU.mult, ALU.mult)\
                            .then_inc(diag_ready[s], 1)
                for s in range(SLOTS):
                    wait_read(pool, s, "scale")
                    for m in range(KM):
                        pool.tensor_tensor(hid[s][:, m, :], hid[s][:, m, :], colmax[s][:, 1, :], ALU.mult)\
                            .then_inc(scaled_ready[s], 1)
                for s in range(SLOTS):
                    power(s, 3)
                for s in range(SLOTS):
                    for m in range(KI):
                        wait_read(pool, s, f"a.{m}")
                        if m >= 2:
                            pool.wait_ge(y_ready[s], m - 1)
                        pool.tensor_scalar(aconv[s][:, m % 2, :], pad[s][:, m, 4:], acs[:, m, 3:4],
                                           ac[:, m, TAPS1:TAPS1 + 1], ALU.mult, ALU.add).then_inc(mid_ready[s], 1)
                for n in (4, 5, 6):
                    for s in range(SLOTS):
                        power(s, n)
                pool.drain().then_inc(at_end, 1)
                pool.wait_ge(restart, it + 1)

        @block.vector
        def _(vec):
            count = {"n": 0}

            def step(ins, on=prep_step):
                count["n"] += 1
                ins.then_inc(on, 1)
                return count["n"]

            def need(n, on=prep_step):
                vec.wait_ge(on, n)

            def job(name):
                vec.wait_ge(job_done, JOB[name][0] + 1)
                return job_bank(name)

            def read(ins):
                ins.then_inc(job_read["dve"], 1)

            vec.memset(hrow[:], 0.0).then_inc(hrow_zeroed, 1)
            p = job("w1T")
            vec.wait_ge(w_loaded["eye"], 16)
            read(vec.tensor_tensor(xw1[:], two(p), eye_sb[:], ALU.add))
            vec.wait_ge(w_loaded["uconst"], 7 * 16)
            p = job("kT")
            vec.wait_ge(w_loaded["kv"], 5 * 16)
            for f in range(KD):
                ins = vec.tensor_scalar(kT[:, f, :], p[:, f * D:(f + 1) * D], bk_sb[:, f:f + 1], DK ** -0.5,
                                        ALU.add, ALU.mult)
            read(ins)
            vec.wait_ge(consts_set, POOL_CONSTS)
            for i in range(2):
                p = job(f"v.{i}")
                for b in range(2):
                    for half in range(2):
                        q = slice(64 * half, 64 * half + 64)
                        ins = vec.tensor_tensor(
                            vbd[q, 2 * i + b, :, half * VW:half * VW + DK],
                            p[q, b * D:(b + 1) * D].rearrange("p (j r d) -> p j r d", r=2, d=DK)[:, :, half, :],
                            bvb[q, :].rearrange("p (j r d) -> p j r d", r=2, d=DK)[:, :, half, :], ALU.add)
                read(ins)
            wait_job_read(vec, "ctxT")
            n = step(vec.tensor_reduce(csum, ctxT.rearrange("p k (b t) -> p (k b) t", b=B), AX, ALU.add))
            need(n)
            vec.tensor_scalar(csum, csum, 1.0 / CTX, None, ALU.mult).then_inc(csum_ready, 1)
            vec.wait_ge(w_loaded["w1"], 16)
            vec.tensor_reduce(wsum[:, 0:1], w1_nat, mybir.AxisListType.XY, ALU.add, apply_absolute_value=True)\
               .then_inc(wsum_ready, 1)
            vec.wait_ge(w_loaded["w2"], 16)
            vec.tensor_reduce(wsum[:, 1:2], w2_nat, mybir.AxisListType.XY, ALU.add, apply_absolute_value=True)\
               .then_inc(wsum_ready, 1)
            p = job("part2")
            vec.wait_ge(w_loaded["bias"], 7 * 16)
            vec.tensor_tensor(brow[0][0:B], p[0:B, 0:D], brow[0][0:B], ALU.add).then_inc(job_read["dve"], 1)
            wait_job_read(vec, "part2")
            R = B + 3
            for i in range(2):
                n = step(vec.tensor_copy(brow_b[i][0:R], brow[i][0:R]))
                need(n)
                n = step(vec.tensor_tensor(brow[i + 1][0:R], brow[i][0:R], brow_b[i][0:R], ALU.subtract))
                need(n)
            vec.tensor_copy(brow_b[2][0:R], brow[2][0:R]).then_inc(rows_split, 1)
            p = job("abssum")
            n = step(vec.tensor_scalar(wmean[:], p[:, 0:2], 1.0 / (HID * D), 1e-5, ALU.mult, ALU.max))
            need(n)
            vec.reciprocal(wscale[:], wmean[:]).then_inc(job_read["dve"], 1)
            wait_job_read(vec, "abssum")
            for i, w in enumerate((w1_nat, w2_nat)):
                n = step(vec.tensor_scalar(w, w, wscale[:, i:i + 1], MAGIC, ALU.mult, ALU.add))
                need(n)
                n = step(vec.tensor_scalar(w, w, -MAGIC, 1.0, ALU.add, ALU.min))
                need(n)
                vec.tensor_scalar(w, w, -1.0, None, ALU.max).then_inc(ternary_ready, 1)
            vec.wait_ge(w_loaded["cffn"], 2 * 16)
            vec.wait_ge(w_loaded["c1"], 2 * 16)
            step(vec.tensor_scalar(fcs[:], fc[:, :, 0:TAPS_F], wmean[:, 0:1], None, ALU.mult))
            last_taps = step(vec.tensor_scalar(acs[:], ac[:, :, 0:TAPS1], 0.5, None, ALU.mult))
            p = job("fM")
            read(vec.scalar_tensor_tensor(fm[:], two(p), 1.0 / D, eye_sb[:], ALU.mult, ALU.add))
            for i in range(4):
                p = job(f"q2.{i}")
                read(vec.tensor_copy(w2q[:, 2 * i:2 * i + 2, :], two(p)))
            need(last_taps)
            wait_job_read(vec, "q2.3")
            vec.wait_ge(toep_loaded, 16)
            vec.tensor_copy(toep[:], toep_rev[:, ::-1]).then_inc(prep_done, 1)

            def stats_of(s, n, tile, wait):
                for t in range(NT):
                    wait(t)
                    k = st(vec.bn_stats(stats[s][:, t, :], tile(t)))
                wt(k)
                for t in range(NT):
                    k = st(vec.bn_aggr(mv[s][:, t, :], stats[s][:, t, :]))
                wt(k)
                vec.tensor_scalar(vareps[s][:], mv[s][:, :, 1], EPS, None, ALU.add).then_inc(var_ready[s], 1)

            def normalise(s, n):
                vec.wait_ge(rstd_ready[s], n)
                for t in range(NT):
                    vec.tensor_scalar(xn[s][:, t, :], res[s][:, t, :], mv[s][:, t, 0:1], rstd[s][:, t:t + 1],
                                      ALU.subtract, ALU.mult).then_inc(xn_ready[s], 1)

            def shift_of(s, n):
                vec.wait_ge(rstd_ready[s], n)
                vec.scalar_tensor_tensor(shift[s][:], mv[s][:, :, 0], -1.0, rstd[s][:], ALU.mult, ALU.mult)\
                   .then_inc(shift_ready[s], 1)

            def add_residual(s, name, old):
                for h in range(2):
                    wait_full(vec, s, f"{name}.{h}")
                    read_by(s, f"{name}.{h}", vec.tensor_tensor(res[s][:, 2 * h:2 * h + 2, :], two(psum(s, f"{name}.{h}")),
                                                                old[:, 2 * h:2 * h + 2, :], ALU.add))

            def layer_sums(s, n, name, old):
                add_residual(s, name, old)
                stats_of(s, n, lambda t: res[s][:, t, :], lambda t: wait_read(vec, s, f"{name}.{t // 2}"))

            def scales(s, a, factor):
                k = st(vec.tensor_scalar(a[:, 1, :], a[:, 0, :], 1e-5, None, ALU.max))
                wt(k)
                st(vec.tensor_scalar(a[:, 2, :], a[:, 1, :], 1.0 / 127.0, factor, ALU.mult, ALU.mult))
                k = st(vec.reciprocal(a[:, 3, :], a[:, 1, :]))
                wt(k)
                return vec.tensor_scalar(a[:, 3, :], a[:, 3, :], 127.0, None, ALU.mult)

            def st(ins):
                return step(ins, vec_step)

            def wt(n):
                need(n, vec_step)

            count["n"] = 0
            with vec.Fori(0, B // SLOTS) as it:
                for s in range(SLOTS):
                    for k in range(KD):
                        for tap in (1, 0):
                            for e in (k, KD + k):
                                if tap == 1:
                                    vec.wait_ge(mid_ready[s], U_ORDER.index(e) + 1)
                                else:
                                    wt(tapped[e])
                                n = st(vec.scalar_tensor_tensor(uconv[s][:, e, :], pad[s][:, e, 2 + tap:2 + tap + S],
                                                                uc[:, e, tap:tap + 1], uconv[s][:, e, :],
                                                                ALU.mult, ALU.add))
                                tapped = {e: n} if tap == 1 and e == k else {**tapped, e: n}
                        wt(n)
                        vec.tensor_tensor(v1[s][:, k, :], uconv[s][:, KD + k, :], uconv[s][:, k, :], ALU.mult)\
                           .then_inc(v_ready[s], 1)
                for s in range(SLOTS):
                    for k in range(KD):
                        wait_full(vec, s, f"y.{k}")
                        vec.wait_ge(v_ready[s], k + 1)
                        read_by(s, f"y.{k}", vec.scalar_tensor_tensor(z1[s][:, k, :], v1[s][:, k, :], fbc[:, k:k + 1],
                                                                      psum(s, f"y.{k}")[:], ALU.mult, ALU.add))
                        wait_read(vec, s, f"y.{k}")
                        vec.tensor_tensor(z1[s][:, k, :], z1[s][:, k, :], uconv[s][:, k, :], ALU.mult)\
                           .then_inc(z_ready[s], 1)
                for s in range(SLOTS):
                    vec.wait_ge(x_loaded[s], it * 16 + 16)
                    layer_sums(s, 1, "o", xin[s])
                for s in range(SLOTS):
                    normalise(s, 1)
                for s in range(SLOTS):
                    stats_of(s, 2, lambda t, s=s: psum(s, f"e.{t // 2}")[:, t % 2 * D:(t % 2 + 1) * D],
                             lambda t, s=s: wait_full(vec, s, f"e.{t // 2}"))
                for s in range(SLOTS):
                    shift_of(s, 2)
                for s in range(SLOTS):
                    for h in range(2):
                        wait_read(vec, s, f"e.{h}")
                    n = st(vec.tensor_reduce(amax[s][:, 0, :], xn[s][:], AX, ALU.max, apply_absolute_value=True))
                    wt(n)
                    n = st(scales(s, amax[s], 1.0))
                    wt(n)
                    for t in range(NT):
                        n = st(vec.tensor_scalar(res[s][:, t, :], xn[s][:, t, :], amax[s][:, 3, t:t + 1], MAGIC,
                                                 ALU.mult, ALU.add))
                    for t in range(NT):
                        wt(n - NT + 1 + t)
                        vec.tensor_scalar(res[s][:, t, :], res[s][:, t, :], -MAGIC, amax[s][:, 2, t:t + 1],
                                          ALU.add, ALU.mult).then_inc(xq_ready[s], 1)
                for s in range(SLOTS):
                    for k in range(KD):
                        vec.wait_ge(xhi_ready[s], k + 1)
                        read_by(s, f"x3.{k}", vec.tensor_tensor(xlo[s][:, k, :], psum(s, f"x3.{k}")[:],
                                                                xhi[s][:, k, :].bitcast(F32), ALU.subtract))
                for s in range(SLOTS):
                    for m in range(KM):
                        g = psum(s, f"g.{m}")
                        c = gconv[s][:, m % 2, :]
                        vec.wait_ge(gmid_ready[s], m + 1)
                        n = st(vec.scalar_tensor_tensor(c[:, 1:S], g[:, 0:S - 1], fcs[:, m, 0:1], c[:, 1:S],
                                                        ALU.mult, ALU.add))
                        wt(n)
                        read_by(s, f"g.{m}", vec.scalar_tensor_tensor(c[:, 0:S - 1], g[:, 1:S], fcs[:, m, 2:3],
                                                                      c[:, 0:S - 1], ALU.mult, ALU.add))
                    for half in range(2):
                        vec.wait_ge(hid_ready[s], 4 * half + 4)
                        n = st(vec.tensor_reduce(colmax[s][:, half, :],
                                                 hid[s][:, 4 * half:4 * half + 4, :].rearrange("p m t -> p t m"),
                                                 AX, ALU.max, apply_absolute_value=True))
                    wt(n)
                    vec.tensor_tensor(colmax[s][:, 0, :], colmax[s][:, 0, :], colmax[s][:, 1, :], ALU.max)\
                       .then_inc(colmax_ready[s], 1)
                for s in range(SLOTS):
                    wait_full(vec, s, "amax")
                    read_by(s, "amax", vec.tensor_reduce(amax2[s][:, 0, :],
                                                         psum(s, "amax")[:].rearrange("p (t h) -> p t h", t=NT),
                                                         AX, ALU.max))
                    wait_read(vec, s, "amax")
                    scales(s, amax2[s], wmean[:, 1:2]).then_inc(scale_ready[s], 1)
                for s in range(SLOTS):
                    for m in range(KM):
                        vec.wait_ge(scaled_ready[s], m + 1)
                        vec.tensor_scalar(hq[s][:, m, :], hid[s][:, m, :], MAGIC, -MAGIC, ALU.add, ALU.add)\
                           .then_inc(hq_ready[s], 1)
                for s in range(SLOTS):
                    for t in range(NT):
                        wait_full(vec, s, f"f.{t // 2}")
                        ins = vec.scalar_tensor_tensor(res[s][:, t, :], psum(s, f"f.{t // 2}")[:, t % 2 * D:(t % 2 + 1) * D],
                                                       amax2[s][:, 2, t:t + 1], xn[s][:, t, :], ALU.mult, ALU.add)
                        if t % 2:
                            read_by(s, f"f.{t // 2}", ins)
                    stats_of(s, 3, lambda t, s=s: res[s][:, t, :], lambda t, s=s: wait_read(vec, s, f"f.{t // 2}"))
                for s in range(SLOTS):
                    normalise(s, 3)
                for s in range(SLOTS):
                    for m in range(KI + 1):
                        if m < KI:
                            wait_read(vec, s, f"t.{m}")
                            wait_full(vec, s, f"a.{m}")
                            read_by(s, f"a.{m}", vec.scalar_tensor_tensor(pad[s][:, m, 4:], th[s][:, m % 2, :], 1.0,
                                                                          psum(s, f"a.{m}")[:], ALU.add, ALU.mult))
                        if m >= 1:
                            j = m - 1
                            c = aconv[s][:, j % 2, :]
                            vec.wait_ge(mid_ready[s], 4 + j + 1)
                            for tap in (2, 1, 0):
                                ins = vec.scalar_tensor_tensor(c, pad[s][:, j, 1 + tap:1 + tap + S],
                                                               acs[:, j, tap:tap + 1], c, ALU.mult, ALU.add)
                                if tap:
                                    wt(st(ins))
                            ins.then_inc(conv_ready[s], 1)
                for s in range(SLOTS):
                    layer_sums(s, 4, "j", xn[s])
                for s in range(SLOTS):
                    normalise(s, 4)
                for i in range(UNITS + 3):
                    for s in range(SLOTS):
                        if i < UNITS:
                            wait_full(vec, s, f"s.{i}")
                            p = psum(s, f"s.{i}")[:].rearrange("p (h t) -> p h t", h=HG)
                            n = st(vec.tensor_reduce(smax[s][:, i % 2, :], p, AX, ALU.max))
                            wt(n)
                            if i >= 2:
                                vec.wait_ge(p_ready[s], i - 1)
                            read_by(s, f"s.{i}", vec.tensor_tensor(
                                sub[s][:, i % 2, :].rearrange("p (h t) -> p h t", h=HG), p,
                                smax[s][:, i % 2, :].unsqueeze(2).broadcast_to([P, HG, CTX]), ALU.subtract))
                        if i >= 4 and i % 2 == 0:
                            t = (i - 4) // 2
                            wait_full(vec, s, f"pv.{t}")
                            pv = psum(s, f"pv.{t}")[:, 0:HEADS * VW].rearrange("p (h d) -> p h d", h=HEADS)
                            n = st(vec.reciprocal(rsum[s][:], pv[:, :, DK]))
                            wt(n)
                            read_by(s, f"pv.{t}", vec.tensor_tensor(
                                o5[s][:, t, :].rearrange("p (h d) -> p h d", h=HEADS), pv[:, :, 0:DK],
                                rsum[s][:].unsqueeze(2).broadcast_to([P, HEADS, DK]), ALU.mult))
                for s in range(SLOTS):
                    layer_sums(s, 5, "k", xn[s])
                for s in range(SLOTS):
                    normalise(s, 5)
                for s in range(SLOTS):
                    stats_of(s, 6, lambda t, s=s: psum(s, f"m.{t // 2}")[:, t % 2 * D:(t % 2 + 1) * D],
                             lambda t, s=s: wait_full(vec, s, f"m.{t // 2}"))
                for s in range(SLOTS):
                    shift_of(s, 6)
                vec.drain().then_inc(at_end, 1)
                vec.wait_ge(restart, it + 1)


_INS = ['x', 'ctx_1024', 'L0_attn_w_in', 'L0_attn_b_in', 'L0_attn_w_conv', 'L0_attn_b_conv', 'L0_attn_w1',
        'L0_attn_b1', 'L0_attn_w2', 'L0_attn_b2', 'L0_attn_w3', 'L0_attn_filt_bias', 'L0_attn_w_out',
        'L0_attn_b_out', 'L0_xattn_W', 'L0_xattn_b', 'L0_ffn_w1', 'L0_ffn_conv_w', 'L0_ffn_conv_b', 'L0_ffn_w2',
        'L1_attn_W_in', 'L1_attn_conv_w', 'L1_attn_conv_b', 'L1_attn_W_out', 'L1_xattn_Wq', 'L1_xattn_bq',
        'L1_xattn_Wk', 'L1_xattn_bk', 'L1_xattn_Wv', 'L1_xattn_bv', 'L1_xattn_Wo', 'L1_xattn_bo',
        'L1_ffn_w_freq_real', 'L1_ffn_w_freq_imag', 'L1_ffn_bias']


def constants():
    angle = 2 * np.pi * (np.outer(np.arange(D), np.arange(D)) % D) / D
    return {"eye": np.eye(D, dtype=np.float32),
            "dft": np.concatenate([np.cos(angle), np.sin(angle), -np.sin(angle)]).astype(np.float32),
            "head_mask": np.kron(np.eye(HG), np.ones((DK, 1))).astype(np.float32),
            "time0": np.array([[0], [0], [0], [1]], np.float32)}


def kernel(**inputs):
    import concourse.bacc as _bacc
    from concourse import mybir as _mybir
    from concourse.bass_utils import run_bass_kernel_spmd as _run

    nc = _bacc.Bacc("TRN2", target_bir_lowering=False, num_devices=1)
    arrays, args = {}, []
    for name, a in [(n, inputs[n]) for n in _INS] + list(constants().items()):
        a = np.ascontiguousarray(a)
        arrays[f"in_{name}_dram"] = a
        args.append(nc.dram_tensor(f"in_{name}_dram", a.shape, _mybir.dt.from_np(a.dtype), kind="ExternalInput").ap())
    args.append(nc.dram_tensor("out_0_dram", (B, S, D), F32, kind="ExternalOutput").ap())
    build(nc, *args)
    r = _run(nc, [arrays], core_ids=[0])
    return r.results[0]["out_0_dram"]
```

```python
from contextlib import ExitStack

import numpy as np

import concourse.bass as bass
from concourse import mybir

P = 128
B, S, D = 4, 512, 256
KD = D // P
NT = S // P
CTX = 64
HEADS, DK = 16, 16
HG = P // DK
HID = 1024
KM = HID // P
INNER = 512
KI = INNER // P
FW = 64
TAPS0, TAPS_F, TAPS1 = 3, 3, 4
EPS = 1e-5
MAGIC = 1.5 * 2.0 ** 23
VW = DK + 1

F32, F32R, BF16 = mybir.dt.float32, mybir.dt.float32r, mybir.dt.bfloat16
ALU = mybir.AluOpType
ACT = mybir.ActivationFunctionType
AX = mybir.AxisListType.X

SLOTS = 2
ROUNDS = B // SLOTS

TURNS = {
    0: ["x1.0", "u.2", "y.0", "x2.0", "x3.0", "g.2", "g.6", "f.0", "a.0", "a.2", "j.0"]
    + [f"pT.{i}" for i in range(8)] + ["k.0", "m.0"],
    1: ["x1.1", "u.3", "y.1", "x2.1", "x3.1", "g.3", "g.7", "f.1", "t.0", "t.2", "j.1"]
    + [f"pv.{t}" for t in range(4)] + ["k.1", "m.1"],
    2: ["u.0", "v.0", "o.0", "e.0", "g.0", "g.4", "amax", "x4.0", "a.1", "a.3", "x5.0", "q.0"]
    + [f"s.{i}" for i in range(0, 8, 2)] + ["oT.0", "x6.0"],
    3: ["u.1", "v.1", "o.1", "e.1", "g.1", "g.5", "scale", "x4.1", "t.1", "t.3", "x5.1", "q.1"]
    + [f"s.{i}" for i in range(1, 8, 2)] + ["oT.1", "x6.1"],
}
TURN = {name: (bank, n) for bank, names in TURNS.items() for n, name in enumerate(names)}

JOBS = [("filt1", "act"), ("filt2", "act"), ("filt3", "act"), ("w1T", "dve"), ("w2T", "act"), ("ctxT", "act"),
        ("part2", "dve"), ("abssum", "dve")]
JOBS += [(f"q1.{i}", "act") for i in range(4)] + [(f"q2.{i}", "dve") for i in range(4)]
JOBS += [("kT", "dve"), ("v.0", "dve"), ("v.1", "dve"), ("fA", "act"), ("fB", "act"), ("fM", "dve")]
JOB = {name: (n, sum(e == eng for _, e in JOBS[:n])) for n, (name, eng) in enumerate(JOBS)}
READER = dict(JOBS)
POOL_CONSTS = 9
U_ORDER = (0, 2, 1, 3)
UNITS = 2 * NT

POOL_SCALES = (0, 1, 3, 4, 6, 7)

PER_BATCH = {
    "mid": 8,
    "v": KD,
    "z": KD,
    "var": 12,
    "rstd": 12,
    "shift": 12,
    "xn": 4 * NT,
    "xq": NT,
    "xhi": 2,
    "gmid": KM,
    "hid": KM,
    "colmax": 1,
    "scale": 1,
    "diag": NT,
    "scaled": len(POOL_SCALES),
    "hq": KM,
    "kbd": KD,
    "conv": KI,
    "y": KI,
    "p": UNITS,
    "stored": 32,
    "x": 16,
}

MERGE = {
    "pe":
        "000101011110000011001111111111111001001111110000001100111001111010010100100100111110100000000100"
        "101011110111010111001100111001000000110000001100000110011000011011111111001011101110111010101110"
        "110110011010001111010100111110100001000111001111110101110000000011001011101110100010101110101100"
        "11110100100011110000010001011001110100110100111100100110010011011111011000011111",
    "act":
        "000101011100011110011001010111100001000010000000001011101111111111110100101101110100001000101110"
        "010010110000110000110000101011011001111100110110110110001101010101101011111010101011100000010100"
        "100100010100010101111111101111111101000001100110011001111001010001111001100000100111100110011010"
        "1011001110110001110100111",
    "dve":
        "100000000001111100011011011010110111110001011000000000000111111001110100000010110010010101101010"
        "110010111111011101010010010001101010101010010111111011101010010000000001011011111101001010110101"
        "101111010010110011001010101110100001111111001000010111001100101111001100011101110100000111010110"
        "101010110110100000000111111111010000100101001000110111011001000001101110011010110101010101011011"
        "111101010101100110100010100010000111111111101111011100100000001000001111111100000001101111111111"
        "1101000000011001011100110001110011011101100100000101111111010000001111111",
    "pool":
        "000101100000011111101100000011000010011111101011111110000000101110011110000111111000000001011111"
        "1010100111001110011000111",
}


def build(nc, x, ctx_in, w_in, b_in, w_conv, b_conv, fw1, fb1, fw2, fb2, fw3, filt_bias, w_out, b_out,
          xw, xb, w1, cw, cb, w2, W_in, cw1, cb1, W_out, Wq, bq, Wk, bk, Wv, bv, Wo, bo, wfr, wfi, fbias,
          eye, dft, head_mask, time0, out):
    with ExitStack() as ctx:
        def sb(name, shape, dt=F32):
            return ctx.enter_context(nc.sbuf_tensor(name, shape, dt))

        def sem(name):
            return ctx.enter_context(nc.semaphore(name))

        bank = [[ctx.enter_context(nc.psum_tensor(f"bank{s}{b}", [P, S], F32)) for b in range(4)]
                for s in range(SLOTS)]
        bank_full = [[sem(f"bank_full{s}{b}") for b in range(4)] for s in range(SLOTS)]
        bank_read = [[sem(f"bank_read{s}{b}") for b in range(4)] for s in range(SLOTS)]
        ready = {name: [sem(f"{name}_ready{s}") for s in range(SLOTS)] for name in PER_BATCH}
        vec_step = [sem(f"vec_step{s}") for s in range(SLOTS)]

        w_loaded = {n: sem(f"ld_{n}") for n in
                    ("eye", "win", "uconst", "filter", "wout", "xw", "rows", "ctx", "w1", "w2", "bias", "kv", "dft",
                     "cffn", "W_in", "c1", "W_out", "attn")}
        job_done = sem("job_done")
        job_read = {"act": sem("job_read_act"), "dve": sem("job_read_dve")}
        consts_set = sem("consts_set")
        hrow_zeroed = sem("hrow_zeroed")
        wsum_ready = sem("wsum_ready")
        csum_ready = sem("csum_ready")
        ctxT2_ready = sem("ctxT2_ready")
        ternary_ready = sem("ternary_ready")
        rows_split = sem("rows_split")
        taps_ready = sem("taps_ready")
        h_stored = sem("h_stored")
        toep_loaded = sem("toep_loaded")
        toep_ready = sem("toep_ready")
        rows_loaded = [sem("rows_loaded0"), sem("rows_loaded1")]

        eye_sb = sb("eye_sb", [P, KD, D])
        ident = eye_sb[:, 0, 0:P]
        ones = sb("ones", [P, P])
        ones_b = sb("ones_b", [P, P], BF16)
        mask_sb = sb("mask_sb", [P, HG])
        halfneg = sb("halfneg", [P, NT])
        w_in_sb = sb("w_in_sb", [P, KD, 4, P])
        uc = sb("uc", [P, 4, TAPS0 + 2])
        fbc = sb("fbc", [P, KD])
        w_out_sb = sb("w_out_sb", [P, KD, D])
        xw1 = sb("xw1", [P, KD, D])
        w1q = sb("w1q", [P, KD, HID], F32R)
        w2q = sb("w2q", [P, KM, D], BF16)
        fc = sb("fc", [P, KM, TAPS_F + 1])
        fcs = sb("fcs", [P, KM, TAPS_F])
        W_in_sb = sb("W_in_sb", [P, KD, 2 * INNER])
        ac = sb("ac", [P, KI, TAPS1 + 1])
        acs = sb("acs", [P, KI, TAPS1])
        W_out_sb = sb("W_out_sb", [P, KI, D])
        wq_sb = sb("wq_sb", [P, KD, D])
        bq_sb = sb("bq_sb", [P, KD])
        bk_sb = sb("bk_sb", [P, KD])
        wo_sb = sb("wo_sb", [P, KD, D])
        kT = sb("kT", [P, KD, B * CTX])
        kbd = [sb(f"kbd{s}", [P, KD, HG * CTX]) for s in range(SLOTS)]
        vbd = sb("vbd", [P, B, HEADS // 2, 2 * VW])
        fm = sb("fm", [P, KD, D])
        toep = sb("toep", [P, 3 * P])
        rows3 = sb("rows3", [P, 7, D], BF16)
        hrow = sb("hrow", [1, 4 * P])
        wsum = sb("wsum", [P, 2])
        wmean = sb("wmean", [P, 2])
        wscale = sb("wscale", [P, 2])

        xin = [sb(f"xin{s}", [P, NT, D]) for s in range(SLOTS)]
        xn = [sb(f"xn{s}", [P, NT, D]) for s in range(SLOTS)]
        xT = [sb(f"xT{s}", [P, KD, S]) for s in range(SLOTS)]
        xhi = [sb(f"xhi{s}", [P, KD, S], F32R) for s in range(SLOTS)]
        xlo = [sb(f"xlo{s}", [P, KD, S], F32R) for s in range(SLOTS)]
        res = [sb(f"res{s}", [P, NT, D]) for s in range(SLOTS)]
        stats = [sb(f"stats{s}", [P, NT, 6]) for s in range(SLOTS)]
        mv = [sb(f"mv{s}", [P, NT, 2]) for s in range(SLOTS)]
        vareps = [sb(f"vareps{s}", [P, NT]) for s in range(SLOTS)]
        rstd = [sb(f"rstd{s}", [P, NT]) for s in range(SLOTS)]
        shift = [sb(f"shift{s}", [P, NT]) for s in range(SLOTS)]
        amax = [sb(f"amax{s}", [P, 4, NT]) for s in range(SLOTS)]
        amax2 = [sb(f"amax2{s}", [P, 4, NT]) for s in range(SLOTS)]
        ARENA = 15 * S + S // 2
        arena = [sb(f"arena{s}", [P, ARENA]) for s in range(SLOTS)]

        def carve(s, at, *shape, dt=F32):
            n = int(np.prod(shape)) * (2 if dt == BF16 else 4) // 4
            assert at + n <= ARENA, (at, n)
            a = arena[s][:, at:at + n]
            if dt == BF16:
                a = a.bitcast(BF16)
            if len(shape) == 2:
                a = a.rearrange("p (a b) -> p a b", a=shape[0])
            return a

        PADW = S + 4
        pad = [sb(f"pad{s}", [P, 4, PADW]) for s in range(SLOTS)]
        uconv = [carve(s, 0, 4, S) for s in range(SLOTS)]
        v1 = [carve(s, 4 * S, KD, S) for s in range(SLOTS)]
        vn = [carve(s, 6 * S, NT, D) for s in range(SLOTS)]
        z1 = [carve(s, 8 * S, KD, S) for s in range(SLOTS)]
        gconv = [pad[s][:, :, 4:] for s in range(SLOTS)]
        hid = [carve(s, 2 * S, KM, S) for s in range(SLOTS)]
        hq = [carve(s, 10 * S, KM, S, dt=BF16) for s in range(SLOTS)]
        diag = [carve(s, 14 * S, NT, P) for s in range(SLOTS)]
        colmax = [sb(f"colmax{s}", [P, 2, S]) for s in range(SLOTS)]
        th = [carve(s, 0, KI, S) for s in range(SLOTS)]
        aconv = [carve(s, 4 * S, KI, S) for s in range(SLOTS)]
        y4 = [carve(s, 8 * S, KI, S) for s in range(SLOTS)]
        qT = [carve(s, 0, KD, S) for s in range(SLOTS)]
        sub = [carve(s, 2 * S, 2, S) for s in range(SLOTS)]
        prob = [carve(s, 4 * S, 2, S) for s in range(SLOTS)]
        pT = [carve(s, 6 * S, 2, S) for s in range(SLOTS)]
        o5 = [carve(s, 8 * S, NT, D) for s in range(SLOTS)]
        oT = [carve(s, 10 * S, KD, S) for s in range(SLOTS)]
        smax = [sb(f"smax{s}", [P, 2, HG]) for s in range(SLOTS)]
        rsum = [sb(f"rsum{s}", [P, HEADS]) for s in range(SLOTS)]
        outb = [carve(s, 12 * S, NT, D) for s in range(SLOTS)]

        w1_nat = carve(1, 0, KM, D)
        w2_nat = carve(1, 4 * S, KD, HID)
        dft_sb = carve(1, 0, 3 * KD, D)
        wf_nat = [carve(1, (3 + i) * S, KD, D) for i in range(2)]
        fAB = [carve(1, (5 + i) * S, KD, D) for i in range(2)]
        xw_nat = carve(1, 8 * S, KD, 2 * D)
        wk_sb = carve(1, 10 * S, KD, D)
        wv_sb = carve(1, 11 * S, KD, D)
        ctx_nat = carve(1, 12 * S, 2, D)
        ctxT = carve(1, 13 * S, KD, B * CTX)
        xw2 = carve(1, 14 * S, KD, D)
        ctxT2 = xn[1][:].rearrange("p t d -> p (t d)").rearrange("p (k n) -> p k n", k=KD)
        bvb = res[1][:, 0, :]
        csum = res[1][:, 1, 0:KD * B]
        fmlp = res[1][:, 2:4, :].rearrange("p t d -> p (t d)")
        misc = colmax[1][:].rearrange("p t d -> p (t d)")

        fw1b, fw2_sb, fw3_sb = fmlp[0:4, 0:FW], fmlp[0:FW, FW:2 * FW], fmlp[0:FW, 2 * FW:2 * FW + D]
        f_t0, f_h1, f_h2, f_b2 = (fmlp[0:n, 500 + i:501 + i] for i, n in enumerate((4, FW, FW, FW)))
        brow = [[misc[:, i * D:(i + 1) * D] for i in range(3)],
                [xT[1][:, i // 2, (i % 2) * D:(i % 2 + 1) * D] for i in range(3)]]
        brow_b = [[pad[1][:, n, 4 + i * D // 2:4 + (i + 1) * D // 2].bitcast(BF16) for i in range(3)]
                  for n in range(2)]
        toep_rev = colmax[0][:, 0, 0:3 * P]

        h_dram = nc.dram_tensor("h_padded", (4 * P,), F32, kind="Internal")

        def full_value(r, name):
            b, n = TURN[name]
            return r * len(TURNS[b]) + n + 1

        class Side:
            def __init__(self, eng, s, r):
                self.eng, self.s, self.r = eng, s, r

            def wait(self, name, n):
                self.eng.wait_ge(ready[name][self.s], self.r * PER_BATCH[name] + n)

            def full(self, name):
                self.eng.wait_ge(bank_full[self.s][TURN[name][0]], full_value(self.r, name))
                return self.psum(name)

            def read(self, name):
                self.eng.wait_ge(bank_read[self.s][TURN[name][0]], full_value(self.r, name))

            def psum(self, name):
                return bank[self.s][TURN[name][0]]

        def done(ins, name, s):
            ins.then_inc(ready[name][s], 1)

        def read_by(s, name, ins):
            ins.then_inc(bank_read[s][TURN[name][0]], 1)

        def job_bank(name):
            return bank[1][JOB[name][0] % 4]

        def wait_job_read(eng, name):
            eng.wait_ge(job_read[READER[name]], JOB[name][1] + 1)

        def two(p):
            return p[:].rearrange("p (a d) -> p a d", a=2)

        def merged(engine, slot_programs):
            for c in MERGE[engine]:
                next(slot_programs[int(c)], None)
            for program in slot_programs:
                for _ in program:
                    pass

        def slot_programs(prepare, batch):
            def program(s):
                if s == 1:
                    yield from prepare()
                for r in range(ROUNDS):
                    yield from batch(s, r)
            return [program(s) for s in range(SLOTS)]

        block = ctx.enter_context(nc.Block())

        def chunks(w):
            return w.rearrange("(k p) n -> p k n", p=P)

        def column(v):
            return v.rearrange("(c p) -> p c", p=P)

        @block.sync
        def _(sp):
            def load(name, dst, src):
                sp.dma_start(dst, src).then_inc(w_loaded[name], 16)

            def load_x(b):
                s = b % SLOTS
                sp.dma_start(xin[s][:], x[b].rearrange("(t p) d -> p t d", p=P)).then_inc(ready["x"][s], 16)

            with nc.allow_non_contiguous_dma(reason="small per-channel constants"):
                load("eye", eye_sb[:], chunks(eye))
                load_x(0)
                for i, c in enumerate((0, 2 * D)):
                    load("win", w_in_sb[:, :, 2 * i:2 * i + 2, :],
                         w_in[:, c:c + D].rearrange("(k p) (c n) -> p k c n", p=P, n=P))
                for src, dst in ((fw1, fw1b[0:3]), (fb1.rearrange("(o d) -> o d", o=1), fw1b[3:4]),
                                 (fw2, fw2_sb), (fw3, fw3_sb), (time0, f_t0),
                                 (fb2.rearrange("(p o) -> p o", o=1), f_b2)):
                    load("filter", dst, src)
                for i, c in enumerate((0, 2 * D)):
                    e = slice(2 * i, 2 * i + 2)
                    load("uconst", uc[:, e, TAPS0 + 1], column(b_in[c:c + D]))
                    load("uconst", uc[:, e, 0:TAPS0], w_conv[c:c + D].rearrange("(c p) o j -> p c (o j)", p=P))
                    load("uconst", uc[:, e, TAPS0], column(b_conv[c:c + D]))
                load("uconst", fbc[:], column(filt_bias))
                load("xw", xw_nat, chunks(xw))
                for r, v in enumerate((b_out, bo, fbias)):
                    load("rows", brow[1][0][r:r + 1], v.rearrange("(o d) -> o d", o=1))
                load("w1", w1_nat, chunks(w1))
                load("w2", w2_nat, chunks(w2))
                load("ctx", ctx_nat, ctx_in.rearrange("(j b) t d -> (b t) j d", b=2))
                for b in range(B):
                    load("bias", brow[0][0][b:b + 1], xb.rearrange("(o d) -> o d", o=1))
                load("wout", w_out_sb[:], chunks(w_out))
                load("cffn", fc[:, :, 0:TAPS_F], cw.rearrange("(c p) o j -> p c (o j)", p=P))
                load("cffn", fc[:, :, TAPS_F], column(cb))
                load("W_in", W_in_sb[:], chunks(W_in))
                load("c1", ac[:, :, 0:TAPS1], cw1.rearrange("(c p) o j -> p c (o j)", p=P))
                load("c1", ac[:, :, TAPS1], column(cb1))
                load("W_out", W_out_sb[:], chunks(W_out))
                for src, dst in ((chunks(Wk), wk_sb), (chunks(Wv), wv_sb), (column(bk), bk_sb[:]),
                                 (bv.partition_broadcast(P), bvb), (head_mask, mask_sb[:])):
                    load("kv", dst, src)
                for src, dst in ((chunks(Wq), wq_sb[:]), (column(bq), bq_sb[:]), (chunks(Wo), wo_sb[:])):
                    load("attn", dst, src)
                load_x(1)
                wait_job_read(sp, "q1.3")
                wait_job_read(sp, "q2.3")
                load("dft", dft_sb, dft.rearrange("(q p) n -> p q n", p=P))
                load("dft", wf_nat[0], chunks(wfr))
                load("dft", wf_nat[1], chunks(wfi))
            for b in range(B):
                s, r = b % SLOTS, b // SLOTS
                side = Side(sp, s, r)
                if b + SLOTS < B:
                    side.wait("xn", NT)
                    load_x(b + SLOTS)
            for b in range(B):
                s, r = b % SLOTS, b // SLOTS
                for h in range(2):
                    Side(sp, s, r).read(f"m.{h}")
                    sp.dma_start(out[b, 2 * h * P:(2 * h + 2) * P].rearrange("(t p) d -> p t d", p=P),
                                 outb[s][:, 2 * h:2 * h + 2, :]).then_inc(ready["stored"][s], 16)
            for s in range(SLOTS):
                sp.wait_ge(ready["stored"][s], 32 * ROUNDS)

        @block.tensor
        def _(pe):
            def job(name):
                n = JOB[name][0]
                if n >= 4:
                    wait_job_read(pe, JOBS[n - 4][0])
                return job_bank(name)

            def job_end(ins):
                ins.then_inc(job_done, 1)

            def prepare():
                pe.wait_ge(w_loaded["filter"], 6 * 16)
                p = job("filt1")
                job_end(pe.matmul(p[0:FW, 0:1], fw1b, f_t0, start=True, stop=True))
                yield
                wait_job_read(pe, "filt1")
                p = job("filt2")
                job_end(pe.matmul(p[0:FW, 0:1], fw2_sb, f_h1, start=True, stop=True))
                yield
                wait_job_read(pe, "filt2")
                p = job("filt3")
                job_end(pe.matmul(p[0:1, 0:D], f_h2, fw3_sb, start=True, stop=True))
                yield
                pe.wait_ge(w_loaded["eye"], 16)
                pe.wait_ge(w_loaded["xw"], 16)
                for half, name in enumerate(("w1T", "w2T")):
                    p = job(name)
                    for k in range(KD):
                        for j in range(KD):
                            last = pe.transpose(p[:, k * D + j * P:k * D + (j + 1) * P],
                                                xw_nat[:, j, half * D + k * P:half * D + (k + 1) * P], ident)
                    job_end(last)
                    yield
                pe.wait_ge(w_loaded["ctx"], 16)
                p = job("ctxT")
                for k in range(KD):
                    for j in range(2):
                        last = pe.transpose(p[:, k * D + j * P:k * D + (j + 1) * P],
                                            ctx_nat[:, j, k * P:(k + 1) * P], ident)
                job_end(last)
                yield
                pe.wait_ge(csum_ready, 1)
                wait_job_read(pe, "w2T")
                p = job("part2")
                for k in range(KD):
                    last = pe.matmul(p[0:B, 0:D], csum[:, k * B:(k + 1) * B], xw2[:, k, :],
                                     start=k == 0, stop=k == KD - 1)
                job_end(last)
                yield
                pe.wait_ge(consts_set, POOL_CONSTS)
                pe.wait_ge(wsum_ready, 2)
                p = job("abssum")
                job_end(pe.matmul(p[:, 0:2], ones[:], wsum[:], start=True, stop=True))
                yield
                pe.wait_ge(ternary_ready, 1)
                for i in range(4):
                    p = job(f"q1.{i}")
                    k, half = i // 2, i % 2
                    for m in range(4):
                        last = pe.transpose(p[:, m * P:(m + 1) * P],
                                            w1_nat[:, half * 4 + m, k * P:(k + 1) * P], ident)
                    job_end(last)
                    yield
                pe.wait_ge(ternary_ready, 2)
                for i in range(4):
                    p = job(f"q2.{i}")
                    for m in range(2):
                        for j in range(KD):
                            last = pe.transpose(p[:, m * D + j * P:m * D + (j + 1) * P],
                                                w2_nat[:, j, (2 * i + m) * P:(2 * i + m + 1) * P], ident)
                    job_end(last)
                    yield
                pe.wait_ge(w_loaded["kv"], 5 * 16)
                wait_job_read(pe, "ctxT")
                p = job("kT")
                for f in range(KD):
                    for k in range(KD):
                        last = pe.matmul(p[:, f * B * CTX:(f + 1) * B * CTX], wk_sb[:, k, f * P:(f + 1) * P],
                                         ctxT[:, k, :], start=k == 0, stop=k == KD - 1)
                job_end(last)
                yield
                pe.wait_ge(ctxT2_ready, KD)
                for h in range(2):
                    p = job(f"v.{h}")
                    for b in range(2):
                        for k in range(KD):
                            last = pe.matmul(p[:, b * D:(b + 1) * D], ctxT2[:, k, (2 * h + b) * P:(2 * h + b + 1) * P],
                                             wv_sb[:, k, :], start=k == 0, stop=k == KD - 1)
                    job_end(last)
                    yield
                pe.wait_ge(w_loaded["dft"], 3 * 16)
                for name, terms in (("fA", ((0, 0), (1, 1))), ("fB", ((1, 0), (0, 2)))):
                    p = job(name)
                    for j in range(KD):
                        for n, (w, c) in enumerate(terms):
                            for k in range(KD):
                                last = pe.matmul(p[:, j * D:(j + 1) * D], wf_nat[w][:, k, j * P:(j + 1) * P],
                                                 dft_sb[:, c * KD + k, :], start=n == 0 and k == 0,
                                                 stop=n == 1 and k == KD - 1)
                    job_end(last)
                    yield
                wait_job_read(pe, "fB")
                p = job("fM")
                for j in range(KD):
                    for n, c in enumerate((0, 2)):
                        for k in range(KD):
                            last = pe.matmul(p[:, j * D:(j + 1) * D], fAB[n][:, k, j * P:(j + 1) * P],
                                             dft_sb[:, c * KD + k, :], start=n == 0 and k == 0,
                                             stop=n == 1 and k == KD - 1)
                job_end(last)
                yield
                wait_job_read(pe, [n for n, e in JOBS if e == "act"][-1])
                wait_job_read(pe, [n for n, e in JOBS if e == "dve"][-1])

            def batch(s, r):
                b = r * SLOTS + s
                side = Side(pe, s, r)

                def take(name):
                    if full_value(r, name) > 1:
                        pe.wait_ge(bank_read[s][TURN[name][0]], full_value(r, name) - 1)
                    return side.psum(name)

                def fill(name, ins):
                    ins.then_inc(bank_full[s][TURN[name][0]], 1)

                def half(h):
                    return slice(2 * h * P, (2 * h + 2) * P)

                def transpose_x(layer, src, wait):
                    for h in range(2):
                        p = take(f"{layer}.{h}")
                        for t in range(2):
                            wait(2 * h + t)
                            for k in range(KD):
                                last = pe.transpose(p[:, k * D + t * P:k * D + (t + 1) * P],
                                                    src[:, 2 * h + t, k * P:(k + 1) * P], ident)
                        fill(f"{layer}.{h}", last)
                        yield

                def project_halves(name, weights, wait, row):
                    lhs = oT[s] if name == "k" else xT[s]
                    for h in range(2):
                        p = take(f"{name}.{h}")
                        for t in range(2):
                            tt = 2 * h + t
                            o = p[:, t * D:(t + 1) * D]
                            pe.matmul(o, ones_b[:], row, start=True, stop=False)
                            if t == 0:
                                wait(h)
                            for k in range(KD):
                                last = pe.matmul(o, lhs[:, k, tt * P:(tt + 1) * P], weights[:, k, :],
                                                 start=False, stop=k == KD - 1)
                        fill(f"{name}.{h}", last)
                        yield

                def project_chunks(name, lhs, weights, nk, wait, row=None):
                    p = [take(f"{name}.{h}") for h in range(2)]
                    if row is not None:
                        for tt in range(NT):
                            pe.matmul(p[tt // 2][:, tt % 2 * D:(tt % 2 + 1) * D], ones_b[:], row,
                                      start=tt % 2 == 0, stop=False, skip_group_check=True)
                    for k in range(nk):
                        wait(k)
                        for tt in range(NT):
                            last = pe.matmul(p[tt // 2][:, tt % 2 * D:(tt % 2 + 1) * D],
                                             lhs[:, k, tt * P:(tt + 1) * P], weights[:, k, :],
                                             start=row is None and k == 0 and tt % 2 == 0,
                                             stop=k == nk - 1 and tt % 2 == 1, skip_group_check=True)
                            if k == nk - 1 and tt % 2:
                                fill(f"{name}.{tt // 2}", last)
                        yield

                pe.wait_ge(w_loaded["eye"], 16)
                side.wait("x", 16)
                yield from transpose_x("x1", xin[s], lambda t: None)
                pe.wait_ge(w_loaded["win"], 2 * 16)
                for n, e in enumerate(U_ORDER):
                    p = take(f"u.{e}")
                    if n == 0:
                        for h in range(2):
                            side.read(f"x1.{h}")
                    for k in range(KD):
                        last = pe.matmul(p[:], w_in_sb[:, k, e, :], xT[s][:, k, :], start=k == 0, stop=k == 1)
                    fill(f"u.{e}", last)
                    yield
                for h in range(2):
                    p = take(f"v.{h}")
                    for t in range(2):
                        for k in range(KD):
                            if h == 0 and t == 0:
                                side.wait("v", k + 1)
                            last = pe.transpose(p[:, t * D + k * P:t * D + (k + 1) * P],
                                                v1[s][:, k, (2 * h + t) * P:(2 * h + t + 1) * P], ident)
                    fill(f"v.{h}", last)
                    yield
                pe.wait_ge(toep_ready, 1)
                for k in range(KD):
                    p = take(f"y.{k}")
                    for t in range(NT):
                        if k == 0 and t % 2 == 0:
                            side.read(f"v.{t // 2}")
                        n = min(3 * P, S - t * P)
                        last = pe.matmul(p[:, t * P:t * P + n], vn[s][:, t, k * P:(k + 1) * P], toep[:, 0:n],
                                         start=t == 0, stop=t == NT - 1, skip_group_check=True)
                    fill(f"y.{k}", last)
                    yield
                pe.wait_ge(w_loaded["wout"], 16)
                pe.wait_ge(consts_set, POOL_CONSTS)
                pe.wait_ge(rows_loaded[1], 3 * 16)
                yield from project_chunks("o", z1[s], w_out_sb, KD, lambda k: side.wait("z", k + 1), rows3[:, B, :])
                yield from transpose_x("x2", xn[s], lambda t: side.wait("xn", t + 1))
                wait_job_read(pe, "w1T")
                pe.wait_ge(rows_loaded[0], 3 * 16)
                yield from project_halves("e", xw1, lambda h: side.read(f"x2.{h}"), rows3[:, b, :])
                yield from transpose_x("x3", res[s], lambda t: side.wait("xq", t + 1))
                wait_job_read(pe, "q1.3")
                for m in range(KM):
                    p = take(f"g.{m}")
                    for cols in [half(0), half(1)] if m == 0 else [slice(0, S)]:
                        for part, buf in enumerate((xhi[s], xlo[s])):
                            if m == 0 and part == 0:
                                side.wait("xhi", cols.stop // (2 * P))
                            if m == 0 and part == 1:
                                side.read(f"x3.{cols.start // (2 * P)}")
                            for k in range(KD):
                                last = pe.matmul(p[:, cols], w1q[:, k, m * P:(m + 1) * P], buf[:, k, cols],
                                                 start=part + k == 0, stop=part + k == 2)
                    fill(f"g.{m}", last)
                    yield
                p = take("amax")
                side.wait("colmax", 1)
                for t in range(NT):
                    last = pe.transpose(p[:, t * P:(t + 1) * P], colmax[s][:, 0, t * P:(t + 1) * P], ident)
                fill("amax", last)
                yield
                p = take("scale")
                for t in range(NT):
                    side.wait("diag", t + 1)
                    last = pe.matmul(p[:, t * P:(t + 1) * P], ones[:], diag[s][:, t, :], start=True, stop=True)
                fill("scale", last)
                yield
                wait_job_read(pe, "q2.3")
                yield from project_chunks("f", hq[s], w2q, KM, lambda k: side.wait("hq", k + 1))
                yield from transpose_x("x4", xn[s], lambda t: side.wait("xn", NT + t + 1))
                pe.wait_ge(w_loaded["W_in"], 16)
                for m in range(KI):
                    for name, c in ((f"t.{m}", INNER), (f"a.{m}", 0)):
                        p = take(name)
                        for cols in [half(0), half(1)] if name == "t.0" else [slice(0, S)]:
                            if name == "t.0":
                                side.read(f"x4.{cols.start // (2 * P)}")
                            for k in range(KD):
                                last = pe.matmul(p[:, cols], W_in_sb[:, k, c + m * P:c + (m + 1) * P],
                                                 xT[s][:, k, cols], start=k == 0, stop=k == 1)
                        fill(name, last)
                        yield
                pe.wait_ge(w_loaded["W_out"], 16)
                yield from project_chunks("j", y4[s], W_out_sb, KI, lambda k: side.wait("y", k + 1))
                yield from transpose_x("x5", xn[s], lambda t: side.wait("xn", 2 * NT + t + 1))
                pe.wait_ge(w_loaded["attn"], 3 * 16)
                for h in range(2):
                    p = take(f"q.{h}")
                    side.read(f"x5.{h}")
                    for f in range(KD):
                        for k in range(KD):
                            last = pe.matmul(p[:, f * D:(f + 1) * D], wq_sb[:, k, f * P:(f + 1) * P],
                                             xT[s][:, k, half(h)], start=k == 0, stop=k == 1)
                    fill(f"q.{h}", last)
                    yield
                wait_job_read(pe, "v.1")
                for i in range(UNITS + 2):
                    if i < UNITS:
                        t, g = i // 2, i % 2
                        p = take(f"s.{i}")
                        side.read(f"q.{t // 2}")
                        side.wait("kbd", g + 1)
                        fill(f"s.{i}", pe.matmul(p[:], qT[s][:, g, t * P:(t + 1) * P], kbd[s][:, g, :],
                                                 start=True, stop=True))
                        yield
                    if 0 <= i - 1 < UNITS:
                        n = i - 1
                        p = take(f"pT.{n}")
                        side.wait("p", n + 1)
                        for c in range(4):
                            last = pe.transpose(p[:, c * P:(c + 1) * P], prob[s][:, n % 2, c * P:(c + 1) * P], ident)
                        fill(f"pT.{n}", last)
                        yield
                    if i >= 2:
                        n = i - 2
                        t, g = n // 2, n % 2
                        p = take(f"pv.{t}") if g == 0 else side.psum(f"pv.{t}")
                        side.read(f"pT.{n}")
                        for c in range(4):
                            j = 4 * g + c
                            last = pe.matmul(p[:, j * 2 * VW:(j + 1) * 2 * VW], pT[s][:, n % 2, c * P:(c + 1) * P],
                                             vbd[:, b, j, :], start=True, stop=True)
                        if g == 1:
                            fill(f"pv.{t}", last)
                        yield
                yield from transpose_x("oT", o5[s], lambda t: side.read(f"pv.{t}"))
                yield from project_halves("k", wo_sb, lambda h: side.read(f"oT.{h}"), rows3[:, B + 1, :])
                yield from transpose_x("x6", xn[s], lambda t: side.wait("xn", 3 * NT + t + 1))
                wait_job_read(pe, "fM")
                yield from project_halves("m", fm, lambda h: side.read(f"x6.{h}"), rows3[:, B + 2, :])

            merged("pe", slot_programs(prepare, batch))

        @block.scalar
        def _(act):
            def job(name):
                act.wait_ge(job_done, JOB[name][0] + 1)
                return job_bank(name)

            def job_end(ins):
                ins.then_inc(job_read["act"], 1)

            def prepare():
                p = job("filt1")
                job_end(act.activation(f_h1, p[0:FW, 0:1], ACT.Silu))
                yield
                p = job("filt2")
                job_end(act.activation(f_h2, p[0:FW, 0:1], ACT.Silu, bias=f_b2))
                yield
                act.wait_ge(hrow_zeroed, 1)
                p = job("filt3")
                job_end(act.activation(hrow[:, 3 * P - 1:3 * P - 1 - D:-1], p[0:1, 0:D], ACT.Copy))
                yield
                p = job("w2T")
                job_end(act.activation(xw2, two(p), ACT.Copy))
                yield
                p = job("ctxT")
                for k in range(KD):
                    act.activation(ctxT2[:, k, :].rearrange("p (b r t) -> p b r t", b=B, r=2),
                                   p[:, k * D:(k + 1) * D].rearrange("p (b t) -> p b t", b=B).unsqueeze(2)
                                   .broadcast_to([P, B, 2, CTX]), ACT.Copy).then_inc(ctxT2_ready, 1)
                job_end(act.activation(ctxT, two(p), ACT.Copy))
                yield
                for i in range(4):
                    p = job(f"q1.{i}")
                    k, half = i // 2, i % 2
                    job_end(act.activation(w1q[:, k, half * S:(half + 1) * S], p[:], ACT.Copy))
                    yield
                for i, name in enumerate(("fA", "fB")):
                    p = job(name)
                    job_end(act.activation(fAB[i], two(p), ACT.Copy))
                    yield
                for n in range(2):
                    act.wait_ge(rows_loaded[n], 3 * 16)

            def batch(s, r):
                side = Side(act, s, r)

                def copy_xT(layer, to):
                    for h in range(2):
                        p = side.full(f"{layer}.{h}")
                        read_by(s, f"{layer}.{h}", act.activation(to[:, :, h * D:(h + 1) * D], two(p), ACT.Copy))
                        yield

                def normalise(n, to):
                    for h in range(2):
                        side.wait("rstd", 2 * n - 1 + h)
                        side.wait("shift", 2 * n - 1 + h)
                        for t in (2 * h, 2 * h + 1):
                            done(act.activation(to[:, t, :], res[s][:, t, :], ACT.Identity,
                                                bias=shift[s][:, t:t + 1], scale=rstd[s][:, t:t + 1]), "xn", s)
                        yield

                def normalise_banks(n, name, to):
                    for h in range(2):
                        side.wait("rstd", 2 * n - 1 + h)
                        side.wait("shift", 2 * n - 1 + h)
                        p = side.psum(f"{name}.{h}")
                        for t in range(2):
                            tt = 2 * h + t
                            ins = act.activation(to[:, tt, :], p[:, t * D:(t + 1) * D], ACT.Identity,
                                                 bias=shift[s][:, tt:tt + 1], scale=rstd[s][:, tt:tt + 1])
                        read_by(s, f"{name}.{h}", ins)
                        yield

                yield from copy_xT("x1", xT[s])
                act.wait_ge(w_loaded["uconst"], 7 * 16)
                for e in U_ORDER:
                    p = side.full(f"u.{e}")
                    read_by(s, f"u.{e}", act.activation(pad[s][:, e, 4:], p[:], ACT.Identity,
                                                        bias=uc[:, e, TAPS0 + 1:TAPS0 + 2]))
                    yield
                for h in range(2):
                    p = side.full(f"v.{h}")
                    read_by(s, f"v.{h}", act.activation(vn[s][:, 2 * h:2 * h + 2, :], two(p), ACT.Copy))
                    yield
                yield from normalise(1, xn[s])
                yield from copy_xT("x2", xT[s])
                yield from normalise_banks(2, "e", xn[s])
                for h in range(2):
                    p = side.full(f"x3.{h}")
                    done(act.activation(xhi[s][:, :, h * D:(h + 1) * D], two(p), ACT.Copy), "xhi", s)
                    yield
                act.wait_ge(taps_ready, 2)
                for m in range(KM + 1):
                    if m < KM:
                        p = side.full(f"g.{m}")
                        if m >= 4:
                            side.wait("hid", m - 3)
                        done(act.activation(gconv[s][:, m % 4, :], p[:], ACT.Identity,
                                            bias=fc[:, m, TAPS_F:TAPS_F + 1], scale=fcs[:, m, 1:2]), "gmid", s)
                        yield
                    if m >= 1:
                        side.read(f"g.{m - 1}")
                        done(act.activation(hid[s][:, m - 1, :], gconv[s][:, (m - 1) % 4, :], ACT.Silu), "hid", s)
                        yield
                p = side.full("scale")
                read_by(s, "scale", act.activation(colmax[s][:, 1, :], p[:], ACT.Copy))
                yield
                yield from normalise(3, xn[s])
                yield from copy_xT("x4", xT[s])
                for m in range(KI + 1):
                    if m < KI:
                        p = side.full(f"t.{m}")
                        read_by(s, f"t.{m}", act.activation(th[s][:, m, :], p[:], ACT.Tanh, scale=0.5))
                        yield
                    if m >= 1:
                        side.wait("conv", m)
                        done(act.activation(y4[s][:, m - 1, :], aconv[s][:, m - 1, :], ACT.Silu), "y", s)
                        yield
                yield from normalise(4, xn[s])
                yield from copy_xT("x5", xT[s])
                act.wait_ge(w_loaded["attn"], 3 * 16)
                for h in range(2):
                    p = side.full(f"q.{h}")
                    for f in range(KD):
                        ins = act.activation(qT[s][:, f, h * D:(h + 1) * D], p[:, f * D:(f + 1) * D], ACT.Identity,
                                             bias=bq_sb[:, f:f + 1])
                    read_by(s, f"q.{h}", ins)
                    yield
                for i in range(UNITS + 1):
                    if i < UNITS:
                        side.read(f"s.{i}")
                        done(act.activation(prob[s][:, i % 2, :], sub[s][:, i % 2, :], ACT.Exp), "p", s)
                        yield
                    if i >= 1:
                        p = side.full(f"pT.{i - 1}")
                        read_by(s, f"pT.{i - 1}", act.activation(pT[s][:, (i - 1) % 2, :], p[:], ACT.Copy))
                        yield
                yield from copy_xT("oT", oT[s])
                yield from normalise(5, xn[s])
                yield from copy_xT("x6", xT[s])
                if r:
                    act.wait_ge(ready["stored"][s], 32 * r)
                yield from normalise_banks(6, "m", outb[s])

            merged("act", slot_programs(prepare, batch))

        @block.gpsimd
        def _(pool):
            def prepare():
                wait_job_read(pool, "filt3")
                pool.dma_start(h_dram.ap().rearrange("(o d) -> o d", o=1), hrow[:]).then_inc(h_stored, 16)
                pool.wait_ge(h_stored, 16)
                pool.dma_start(toep_rev, bass.AP(h_dram, 0, [[1, P], [1, 3 * P]])).then_inc(toep_loaded, 16)
                yield
                for n, rows in ((1, slice(B, B + 3)), (0, slice(0, B))):
                    pool.wait_ge(rows_split, 2 - n)
                    for i in range(3):
                        pool.dma_start(rows3[i:i + 1, rows], brow_b[n][i][0:rows.stop - rows.start])\
                            .then_inc(rows_loaded[n], 16)
                    yield

            def batch(s, r):
                side = Side(pool, s, r)

                def power(n):
                    for h in range(2):
                        side.wait("var", 2 * n - 1 + h)
                        done(pool.tensor_tensor(rstd[s][:, 2 * h:2 * h + 2], vareps[s][:, 2 * h:2 * h + 2],
                                                halfneg[:, 0:2], ALU.pow), "rstd", s)
                        yield

                pool.wait_ge(w_loaded["uconst"], 7 * 16)
                for e in U_ORDER:
                    side.read(f"u.{e}")
                    done(pool.tensor_scalar(uconv[s][:, e, :], pad[s][:, e, 4:], uc[:, e, 2:3],
                                            uc[:, e, TAPS0:TAPS0 + 1], ALU.mult, ALU.add), "mid", s)
                    yield
                for n in (1, 2):
                    yield from power(n)
                pool.wait_ge(w_loaded["kv"], 5 * 16)
                wait_job_read(pool, "kT")
                if r:
                    for i in (UNITS - 2, UNITS - 1):
                        Side(pool, s, r - 1).full(f"s.{i}")
                for g in range(KD):
                    b = r * SLOTS + s
                    done(pool.tensor_tensor(kbd[s][:, g, :].rearrange("p (h t) -> p h t", h=HG),
                                            kT[:, g, b * CTX:(b + 1) * CTX].unsqueeze(1).broadcast_to([P, HG, CTX]),
                                            mask_sb[:].unsqueeze(2).broadcast_to([P, HG, CTX]), ALU.mult), "kbd", s)
                    yield
                side.wait("scale", 1)
                for t in range(NT):
                    done(pool.tensor_scalar(diag[s][:, t, :], ident, amax2[s][:, 3, t:t + 1], 1.0,
                                            ALU.mult, ALU.mult), "diag", s)
                yield
                side.read("scale")
                for m in POOL_SCALES:
                    done(pool.tensor_tensor(hid[s][:, m, :], hid[s][:, m, :], colmax[s][:, 1, :], ALU.mult),
                         "scaled", s)
                    yield
                yield from power(3)
                pool.wait_ge(taps_ready, 2)
                for m in range(KI):
                    side.read(f"a.{m}")
                    done(pool.tensor_scalar(aconv[s][:, m, :], pad[s][:, m, 4:], acs[:, m, 3:4],
                                            ac[:, m, TAPS1:TAPS1 + 1], ALU.mult, ALU.add), "mid", s)
                    yield
                for n in (4, 5, 6):
                    yield from power(n)

            for n, (buf, value) in enumerate(((ones[:], 1.0), (ones_b[:], 1.0), (halfneg[:], -0.5), (rows3[:], 0.0),
                                              (vbd[:], 0.0), (pad[0][:, :, 0:4], 0.0), (pad[1][:, :, 0:4], 0.0))):
                pool.memset(buf, value).then_inc(consts_set, 1)
            pool.wait_ge(consts_set, 7)
            for half in range(2):
                pool.memset(vbd[64 * half:64 * half + 64, :, :, half * VW + DK], 1.0).then_inc(consts_set, 1)
            pool.wait_ge(consts_set, POOL_CONSTS)
            merged("pool", slot_programs(prepare, batch))

        @block.vector
        def _(vec):
            steps = [0] * SLOTS

            def step(s, ins):
                steps[s] += 1
                ins.then_inc(vec_step[s], 1)
                return steps[s]

            def need(s, n):
                vec.wait_ge(vec_step[s], n)

            def job(name):
                vec.wait_ge(job_done, JOB[name][0] + 1)
                return job_bank(name)

            def job_end(ins):
                ins.then_inc(job_read["dve"], 1)

            def split_rows(n, rows):
                for i in range(2):
                    k = step(1, vec.tensor_copy(brow_b[n][i][0:rows], brow[n][i][0:rows]))
                    need(1, k)
                    k = step(1, vec.tensor_tensor(brow[n][i + 1][0:rows], brow[n][i][0:rows], brow_b[n][i][0:rows],
                                                  ALU.subtract))
                    need(1, k)
                vec.tensor_copy(brow_b[n][2][0:rows], brow[n][2][0:rows]).then_inc(rows_split, 1)

            def prepare():
                vec.wait_ge(w_loaded["rows"], 3 * 16)
                split_rows(1, 3)
                yield
                vec.wait_ge(toep_loaded, 16)
                vec.tensor_copy(toep[:], toep_rev[:, ::-1]).then_inc(toep_ready, 1)
                yield
                p = job("w1T")
                vec.wait_ge(w_loaded["eye"], 16)
                job_end(vec.tensor_tensor(xw1[:], two(p), eye_sb[:], ALU.add))
                yield
                vec.wait_ge(w_loaded["w1"], 16)
                vec.tensor_reduce(wsum[:, 0:1], w1_nat, mybir.AxisListType.XY, ALU.add, apply_absolute_value=True)\
                   .then_inc(wsum_ready, 1)
                yield
                vec.wait_ge(w_loaded["w2"], 16)
                vec.tensor_reduce(wsum[:, 1:2], w2_nat, mybir.AxisListType.XY, ALU.add, apply_absolute_value=True)\
                   .then_inc(wsum_ready, 1)
                yield
                wait_job_read(vec, "ctxT")
                n = step(1, vec.tensor_reduce(csum, ctxT.rearrange("p k (b t) -> p (k b) t", b=B), AX, ALU.add))
                need(1, n)
                vec.tensor_scalar(csum, csum, 1.0 / CTX, None, ALU.mult).then_inc(csum_ready, 1)
                yield
                p = job("part2")
                vec.wait_ge(w_loaded["bias"], B * 16)
                job_end(vec.tensor_tensor(brow[0][0][0:B], p[0:B, 0:D], brow[0][0][0:B], ALU.add))
                wait_job_read(vec, "part2")
                split_rows(0, B)
                yield
                p = job("abssum")
                n = step(1, vec.tensor_scalar(wmean[:], p[:, 0:2], 1.0 / (HID * D), 1e-5, ALU.mult, ALU.max))
                need(1, n)
                job_end(vec.reciprocal(wscale[:], wmean[:]))
                wait_job_read(vec, "abssum")
                yield
                for i, w in enumerate((w1_nat, w2_nat)):
                    n = step(1, vec.tensor_scalar(w, w, wscale[:, i:i + 1], MAGIC, ALU.mult, ALU.add))
                    yield
                    need(1, n)
                    n = step(1, vec.tensor_scalar(w, w, -MAGIC, 1.0, ALU.add, ALU.min))
                    yield
                    need(1, n)
                    vec.tensor_scalar(w, w, -1.0, None, ALU.max).then_inc(ternary_ready, 1)
                    yield
                vec.wait_ge(w_loaded["cffn"], 2 * 16)
                vec.wait_ge(w_loaded["c1"], 2 * 16)
                vec.tensor_scalar(fcs[:], fc[:, :, 0:TAPS_F], wmean[:, 0:1], None, ALU.mult).then_inc(taps_ready, 1)
                vec.tensor_scalar(acs[:], ac[:, :, 0:TAPS1], 0.5, None, ALU.mult).then_inc(taps_ready, 1)
                yield
                for i in range(4):
                    p = job(f"q2.{i}")
                    job_end(vec.tensor_copy(w2q[:, 2 * i:2 * i + 2, :], two(p)))
                    yield
                p = job("kT")
                vec.wait_ge(w_loaded["kv"], 5 * 16)
                for f in range(KD):
                    ins = vec.tensor_scalar(kT[:, f, :], p[:, f * D:(f + 1) * D], bk_sb[:, f:f + 1], DK ** -0.5,
                                            ALU.add, ALU.mult)
                job_end(ins)
                yield
                vec.wait_ge(consts_set, POOL_CONSTS)
                for i in range(2):
                    p = job(f"v.{i}")
                    for b in range(2):
                        for half in range(2):
                            q = slice(64 * half, 64 * half + 64)
                            ins = vec.tensor_tensor(
                                vbd[q, 2 * i + b, :, half * VW:half * VW + DK],
                                p[q, b * D:(b + 1) * D].rearrange("p (j r d) -> p j r d", r=2, d=DK)[:, :, half, :],
                                bvb[q, :].rearrange("p (j r d) -> p j r d", r=2, d=DK)[:, :, half, :], ALU.add)
                    job_end(ins)
                    yield
                p = job("fM")
                job_end(vec.scalar_tensor_tensor(fm[:], two(p), 1.0 / D, eye_sb[:], ALU.mult, ALU.add))
                yield

            def batch(s, r):
                side = Side(vec, s, r)

                def st(ins):
                    return step(s, ins)

                def wt(n):
                    need(s, n)

                def layer_norm(n, tile, sums):
                    def shift_of(h):
                        side.wait("rstd", 2 * n - 1 + h)
                        q = slice(2 * h, 2 * h + 2)
                        done(vec.scalar_tensor_tensor(shift[s][:, q], mv[s][:, q, 0], -1.0, rstd[s][:, q],
                                                      ALU.mult, ALU.mult), "shift", s)

                    for h in range(2):
                        q = slice(2 * h, 2 * h + 2)
                        yield from sums(h)
                        for t in (2 * h, 2 * h + 1):
                            k = st(vec.bn_stats(stats[s][:, t, :], tile(t)))
                        yield
                        if h:
                            shift_of(0)
                            yield
                        wt(k)
                        for t in (2 * h, 2 * h + 1):
                            k = st(vec.bn_aggr(mv[s][:, t, :], stats[s][:, t, :]))
                        wt(k)
                        done(vec.tensor_scalar(vareps[s][:, q], mv[s][:, q, 1], EPS, None, ALU.add), "var", s)
                        yield
                    shift_of(1)
                    yield

                def layer_sums(n, name, old):
                    def sums(h):
                        p = side.full(f"{name}.{h}")
                        read_by(s, f"{name}.{h}", vec.tensor_tensor(res[s][:, 2 * h:2 * h + 2, :], two(p),
                                                                    old[:, 2 * h:2 * h + 2, :], ALU.add))
                        yield
                        side.read(f"{name}.{h}")
                    yield from layer_norm(n, lambda t: res[s][:, t, :], sums)

                def bank_sums(n, name):
                    def sums(h):
                        side.full(f"{name}.{h}")
                        yield from ()
                    yield from layer_norm(n, lambda t: side.psum(f"{name}.{t // 2}")[:, t % 2 * D:(t % 2 + 1) * D],
                                          sums)

                def scales(a, factor):
                    k = st(vec.tensor_scalar(a[:, 1, :], a[:, 0, :], 1e-5, None, ALU.max))
                    wt(k)
                    st(vec.tensor_scalar(a[:, 2, :], a[:, 1, :], 1.0 / 127.0, factor, ALU.mult, ALU.mult))
                    k = st(vec.reciprocal(a[:, 3, :], a[:, 1, :]))
                    wt(k)
                    return vec.tensor_scalar(a[:, 3, :], a[:, 3, :], 127.0, None, ALU.mult)

                vec.wait_ge(w_loaded["uconst"], 7 * 16)
                if s == 0 and r == 0:
                    vec.wait_ge(consts_set, POOL_CONSTS)
                for k in range(KD):
                    tapped = {}
                    for tap in (1, 0):
                        for e in (k, KD + k):
                            if tap == 1:
                                side.wait("mid", U_ORDER.index(e) + 1)
                            else:
                                wt(tapped[e])
                            tapped[e] = st(vec.scalar_tensor_tensor(uconv[s][:, e, :], pad[s][:, e, 2 + tap:2 + tap + S],
                                                                    uc[:, e, tap:tap + 1], uconv[s][:, e, :],
                                                                    ALU.mult, ALU.add))
                            yield
                    wt(tapped[KD + k])
                    done(vec.tensor_tensor(v1[s][:, k, :], uconv[s][:, KD + k, :], uconv[s][:, k, :], ALU.mult),
                         "v", s)
                    yield
                for k in range(KD):
                    p = side.full(f"y.{k}")
                    side.wait("v", k + 1)
                    read_by(s, f"y.{k}", vec.scalar_tensor_tensor(z1[s][:, k, :], v1[s][:, k, :], fbc[:, k:k + 1],
                                                                  p[:], ALU.mult, ALU.add))
                    yield
                    side.read(f"y.{k}")
                    done(vec.tensor_tensor(z1[s][:, k, :], z1[s][:, k, :], uconv[s][:, k, :], ALU.mult), "z", s)
                    yield
                side.wait("x", 16)
                yield from layer_sums(1, "o", xin[s])
                yield from bank_sums(2, "e")
                for h in range(2):
                    q = slice(2 * h, 2 * h + 2)
                    side.read(f"e.{h}")
                    n = st(vec.tensor_reduce(amax[s][:, 0, q], xn[s][:, q, :], AX, ALU.max,
                                             apply_absolute_value=True))
                    yield
                    wt(n)
                    n = st(scales(amax[s][:, :, q], 1.0))
                    yield
                    wt(n)
                    for t in range(2 * h, 2 * h + 2):
                        n = st(vec.tensor_scalar(res[s][:, t, :], xn[s][:, t, :], amax[s][:, 3, t:t + 1], MAGIC,
                                                 ALU.mult, ALU.add))
                    for t in range(2 * h, 2 * h + 2):
                        wt(n - 1 + t % 2)
                        done(vec.tensor_scalar(res[s][:, t, :], res[s][:, t, :], -MAGIC, amax[s][:, 2, t:t + 1],
                                               ALU.add, ALU.mult), "xq", s)
                    yield
                for h in range(2):
                    side.wait("xhi", h + 1)
                    q = slice(h * D, (h + 1) * D)
                    read_by(s, f"x3.{h}", vec.tensor_tensor(xlo[s][:, :, q], two(side.psum(f"x3.{h}")),
                                                            xhi[s][:, :, q].bitcast(F32), ALU.subtract))
                    yield
                vec.wait_ge(taps_ready, 2)
                for m in range(KM):
                    g = side.psum(f"g.{m}")
                    c = gconv[s][:, m % 4, :]
                    side.wait("gmid", m + 1)
                    n = st(vec.scalar_tensor_tensor(c[:, 1:S], g[:, 0:S - 1], fcs[:, m, 0:1], c[:, 1:S],
                                                    ALU.mult, ALU.add))
                    yield
                    wt(n)
                    read_by(s, f"g.{m}", vec.scalar_tensor_tensor(c[:, 0:S - 1], g[:, 1:S], fcs[:, m, 2:3],
                                                                  c[:, 0:S - 1], ALU.mult, ALU.add))
                    yield
                    if m % 4 == 3:
                        half = m // 4
                        side.wait("hid", m + 1)
                        n = st(vec.tensor_reduce(colmax[s][:, half, :],
                                                 hid[s][:, 4 * half:4 * half + 4, :].rearrange("p m t -> p t m"),
                                                 AX, ALU.max, apply_absolute_value=True))
                        yield
                wt(n)
                done(vec.tensor_tensor(colmax[s][:, 0, :], colmax[s][:, 0, :], colmax[s][:, 1, :], ALU.max),
                     "colmax", s)
                yield
                p = side.full("amax")
                read_by(s, "amax", vec.tensor_reduce(amax2[s][:, 0, :], p[:].rearrange("p (t h) -> p t h", t=NT),
                                                     AX, ALU.max))
                side.read("amax")
                done(scales(amax2[s], wmean[:, 1:2]), "scale", s)
                yield
                if r:
                    vec.wait_ge(ready["stored"][s], 32 * r)
                side.read("scale")
                for m in range(KM):
                    if m in POOL_SCALES:
                        side.wait("scaled", POOL_SCALES.index(m) + 1)
                    else:
                        n = st(vec.tensor_tensor(hid[s][:, m, :], hid[s][:, m, :], colmax[s][:, 1, :], ALU.mult))
                        yield
                        wt(n)
                    done(vec.tensor_scalar(hq[s][:, m, :], hid[s][:, m, :], MAGIC, -MAGIC, ALU.add, ALU.add), "hq", s)
                    yield
                def sums(h):
                    p = side.full(f"f.{h}")
                    for t in range(2):
                        tt = 2 * h + t
                        ins = vec.scalar_tensor_tensor(res[s][:, tt, :], p[:, t * D:(t + 1) * D],
                                                       amax2[s][:, 2, tt:tt + 1], xn[s][:, tt, :], ALU.mult, ALU.add)
                    read_by(s, f"f.{h}", ins)
                    yield
                    side.read(f"f.{h}")
                yield from layer_norm(3, lambda t: res[s][:, t, :], sums)
                for m in range(KI + 1):
                    if m < KI:
                        side.read(f"t.{m}")
                        p = side.full(f"a.{m}")
                        read_by(s, f"a.{m}", vec.scalar_tensor_tensor(pad[s][:, m, 4:], th[s][:, m, :], 1.0,
                                                                      p[:], ALU.add, ALU.mult))
                        yield
                    if m >= 1:
                        j = m - 1
                        c = aconv[s][:, j, :]
                        side.wait("mid", 4 + j + 1)
                        for tap in (2, 1, 0):
                            ins = vec.scalar_tensor_tensor(c, pad[s][:, j, 1 + tap:1 + tap + S],
                                                           acs[:, j, tap:tap + 1], c, ALU.mult, ALU.add)
                            if tap:
                                n = st(ins)
                                yield
                                wt(n)
                        done(ins, "conv", s)
                        yield
                yield from layer_sums(4, "j", xn[s])
                for i in range(UNITS + 3):
                    if i < UNITS:
                        p = side.full(f"s.{i}")[:].rearrange("p (h t) -> p h t", h=HG)
                        n = st(vec.tensor_reduce(smax[s][:, i % 2, :], p, AX, ALU.max))
                        yield
                        wt(n)
                        if i >= 2:
                            side.wait("p", i - 1)
                        read_by(s, f"s.{i}", vec.tensor_tensor(
                            sub[s][:, i % 2, :].rearrange("p (h t) -> p h t", h=HG), p,
                            smax[s][:, i % 2, :].unsqueeze(2).broadcast_to([P, HG, CTX]), ALU.subtract))
                        yield
                    if i >= 4 and i % 2 == 0:
                        t = (i - 4) // 2
                        pv = side.full(f"pv.{t}")[:, 0:HEADS * VW].rearrange("p (h d) -> p h d", h=HEADS)
                        n = st(vec.reciprocal(rsum[s][:], pv[:, :, DK]))
                        wt(n)
                        read_by(s, f"pv.{t}", vec.tensor_tensor(
                            o5[s][:, t, :].rearrange("p (h d) -> p h d", h=HEADS), pv[:, :, 0:DK],
                            rsum[s][:].unsqueeze(2).broadcast_to([P, HEADS, DK]), ALU.mult))
                        yield
                yield from layer_sums(5, "k", xn[s])
                yield from bank_sums(6, "m")

            vec.memset(hrow[:], 0.0).then_inc(hrow_zeroed, 1)
            merged("dve", slot_programs(prepare, batch))

_INS = ['x', 'ctx_1024', 'L0_attn_w_in', 'L0_attn_b_in', 'L0_attn_w_conv', 'L0_attn_b_conv', 'L0_attn_w1',
        'L0_attn_b1', 'L0_attn_w2', 'L0_attn_b2', 'L0_attn_w3', 'L0_attn_filt_bias', 'L0_attn_w_out',
        'L0_attn_b_out', 'L0_xattn_W', 'L0_xattn_b', 'L0_ffn_w1', 'L0_ffn_conv_w', 'L0_ffn_conv_b', 'L0_ffn_w2',
        'L1_attn_W_in', 'L1_attn_conv_w', 'L1_attn_conv_b', 'L1_attn_W_out', 'L1_xattn_Wq', 'L1_xattn_bq',
        'L1_xattn_Wk', 'L1_xattn_bk', 'L1_xattn_Wv', 'L1_xattn_bv', 'L1_xattn_Wo', 'L1_xattn_bo',
        'L1_ffn_w_freq_real', 'L1_ffn_w_freq_imag', 'L1_ffn_bias']


def constants():
    angle = 2 * np.pi * (np.outer(np.arange(D), np.arange(D)) % D) / D
    return {"eye": np.eye(D, dtype=np.float32),
            "dft": np.concatenate([np.cos(angle), np.sin(angle), -np.sin(angle)]).astype(np.float32),
            "head_mask": np.kron(np.eye(HG), np.ones((DK, 1))).astype(np.float32),
            "time0": np.array([[0], [0], [0], [1]], np.float32)}


def kernel(**inputs):
    import concourse.bacc as _bacc
    from concourse import mybir as _mybir
    from concourse.bass_utils import run_bass_kernel_spmd as _run

    nc = _bacc.Bacc("TRN2", target_bir_lowering=False, num_devices=1)
    arrays, args = {}, []
    for name, a in [(n, inputs[n]) for n in _INS] + list(constants().items()):
        a = np.ascontiguousarray(a)
        arrays[f"in_{name}_dram"] = a
        args.append(nc.dram_tensor(f"in_{name}_dram", a.shape, _mybir.dt.from_np(a.dtype), kind="ExternalInput").ap())
    args.append(nc.dram_tensor("out_0_dram", (B, S, D), F32, kind="ExternalOutput").ap())
    build(nc, *args)
    r = _run(nc, [arrays], core_ids=[0])
    return r.results[0]["out_0_dram"]
```

```python
from contextlib import ExitStack

import numpy as np

import concourse.bass as bass
from concourse import mybir

P = 128
B, S, D = 4, 512, 256
KD = D // P
NT = S // P
CTX = 64
HEADS, DK = 16, 16
HG = P // DK
HID = 1024
KM = HID // P
INNER = 512
KI = INNER // P
FW = 64
TAPS0, TAPS_F, TAPS1 = 3, 3, 4
EPS = 1e-5
MAGIC = 1.5 * 2.0 ** 23
VW = DK + 1

F32, F32R, BF16 = mybir.dt.float32, mybir.dt.float32r, mybir.dt.bfloat16
ALU = mybir.AluOpType
ACT = mybir.ActivationFunctionType
AX = mybir.AxisListType.X

SLOTS = 2
ROUNDS = B // SLOTS

TURNS = {
    0: ["x1.0", "u.2", "y.0", "x2.0", "x3.0", "g.2", "g.6", "f.0", "a.0", "a.2", "j.0"]
    + [f"pT.{i}" for i in range(8)] + ["k.0", "m.0"],
    1: ["x1.1", "u.3", "y.1", "x2.1", "x3.1", "g.3", "g.7", "f.1", "t.0", "t.2", "j.1"]
    + [f"pv.{t}" for t in range(4)] + ["k.1", "m.1"],
    2: ["u.0", "v.0", "o.0", "e.0", "g.0", "g.4", "amax", "x4.0", "a.1", "a.3", "x5.0", "q.0"]
    + [f"s.{i}" for i in range(0, 8, 2)] + ["oT.0", "x6.0"],
    3: ["u.1", "v.1", "o.1", "e.1", "g.1", "g.5", "scale", "x4.1", "t.1", "t.3", "x5.1", "q.1"]
    + [f"s.{i}" for i in range(1, 8, 2)] + ["oT.1", "x6.1"],
}
TURN = {name: (bank, n) for bank, names in TURNS.items() for n, name in enumerate(names)}

JOBS = [("filt1", "act"), ("filt2", "act"), ("filt3", "act"), ("w1T", "dve"), ("w2T", "act"), ("ctxT", "act"),
        ("part2", "dve"), ("abssum", "dve")]
JOBS += [(f"q1.{i}", "act") for i in range(4)] + [(f"q2.{i}", "dve") for i in range(4)]
JOBS += [("kT", "dve"), ("v.0", "dve"), ("v.1", "dve"), ("fA", "act"), ("fB", "act"), ("fM", "dve")]
JOB = {name: (n, sum(e == eng for _, e in JOBS[:n])) for n, (name, eng) in enumerate(JOBS)}
READER = dict(JOBS)
POOL_CONSTS = 10
U_ORDER = (0, 2, 1, 3)
UNITS = 2 * NT

POOL_SCALES = (1, 3, 5, 7)

SIDE_U = (1, 3)

PER_BATCH = {
    "side": 2 + KI,
    "part": 2 + KI,
    "mid": 8,
    "xhi1": 2,
    "xhi4": 2,
    "xlo4": 2,
    "v": KD,
    "z": KD,
    "var": 12,
    "rstd": 12,
    "shift": 12,
    "xn_even": 8,
    "xn_odd": 8,
    "xr": 2,
    "xq_odd": 2,
    "xq_even": 2,
    "xscale": 2,
    "xhi": 2,
    "gmid": KM,
    "hid": KM,
    "colmax": 1,
    "scale": 1,
    "diag": NT,
    "scaled": len(POOL_SCALES),
    "hq": KM,
    "kbd": KD,
    "conv": KI,
    "y": KI,
    "p": UNITS,
    "stored": 32,
    "x": 16,
}

MERGE = {
    "pe":
        "100111100001011000001111111111101000110011000111100001011111111100110011001000011110100000000010"
        "100110111101100011001111111111001100000011111100011000111111001000111100100100111101111010001100"
        "000011101001000111110000111111000001011100001111111111000100010000110110111100001000001001011111"
        "11101011001101101100001100001110111000001101000011110011001101101101110001001111",
    "act":
        "010011100000100011111000010010011000010111110001001000001101111011111111110100000111011100100000"
        "001000000011110110011111111111010011100101101110110011011000110011111010010000010001010100011111"
        "011011001110000010111000010010011101001101111011011111011000000010000000111001010111011101111010"
        "11011100110010011100100111001001100011011011100001111000111",
    "dve":
        "000111110000001001010001110110101110000101100000000000010011000000111111001100101101001011111101"
        "000111110111111101000100001000010101100100101011111110110101001000001100111110100010001110111111"
        "110000111111111111001111111010000111100110011011100011101100011100001000000011111110010000001100"
        "110100101001000001011111110000010011010001010110111010001101101001111110110100011101101101011010"
        "101111101010000100000010100000011101111111111111010000010000000001000011110111111111111111000011"
        "1001110000110111000001100011111010010000010111111100000001111111",
    "pool":
        "001000010100100000000011111111111101111000011000000000000100111100001111111111111111110000001111"
        "000000110100101111000000010111111111110000011110100000110010001001010110011011111111000011110001"
        "11",
}


def build(nc, x, ctx_in, w_in, b_in, w_conv, b_conv, fw1, fb1, fw2, fb2, fw3, filt_bias, w_out, b_out,
          xw, xb, w1, cw, cb, w2, W_in, cw1, cb1, W_out, Wq, bq, Wk, bk, Wv, bv, Wo, bo, wfr, wfi, fbias,
          eye, dft, head_mask, time0, out):
    with ExitStack() as ctx:
        def sb(name, shape, dt=F32):
            return ctx.enter_context(nc.sbuf_tensor(name, shape, dt))

        def sem(name):
            return ctx.enter_context(nc.semaphore(name))

        bank = [[ctx.enter_context(nc.psum_tensor(f"bank{s}{b}", [P, S], F32)) for b in range(4)]
                for s in range(SLOTS)]
        bank_full = [[sem(f"bank_full{s}{b}") for b in range(4)] for s in range(SLOTS)]
        bank_read = [[sem(f"bank_read{s}{b}") for b in range(4)] for s in range(SLOTS)]
        ready = {name: [sem(f"{name}_ready{s}") for s in range(SLOTS)] for name in PER_BATCH}
        vec_step = [sem(f"vec_step{s}") for s in range(SLOTS)]

        w_loaded = {n: sem(f"ld_{n}") for n in
                    ("eye", "win", "uconst", "filter", "wout", "xw", "rows", "ctx", "w1", "w2", "bias", "kv", "dft",
                     "cffn", "W_in", "c1", "W_out", "attn")}
        job_done = sem("job_done")
        job_read = {"act": sem("job_read_act"), "dve": sem("job_read_dve")}
        consts_set = sem("consts_set")
        hrow_zeroed = sem("hrow_zeroed")
        wsum_ready = sem("wsum_ready")
        csum_ready = sem("csum_ready")
        ctxT2_ready = sem("ctxT2_ready")
        ternary_ready = sem("ternary_ready")
        rows_split = sem("rows_split")
        win_hi = sem("win_hi")
        win_split = sem("win_split")
        W_in_hi = sem("W_in_hi")
        W_in_split = sem("W_in_split")
        taps_ready = sem("taps_ready")
        toep_loaded = sem("toep_loaded")
        toep_ready = sem("toep_ready")
        rows_loaded = [sem("rows_loaded0"), sem("rows_loaded1")]

        eye_sb = sb("eye_sb", [P, KD, D])
        ident = eye_sb[:, 0, 0:P]
        ones = sb("ones", [P, P])
        ones_b = sb("ones_b", [P, P], BF16)
        mask_sb = sb("mask_sb", [P, HG])
        halfneg = sb("halfneg", [P, NT])
        magicneg = sb("magicneg", [P, 1])
        w_in_hi = sb("w_in_hi", [P, KD, 4, P], F32R)
        w_in_lo = sb("w_in_lo", [P, KD, 4, P], F32R)
        uc = sb("uc", [P, 4, TAPS0 + 2])
        fbc = sb("fbc", [P, KD])
        w_out_sb = sb("w_out_sb", [P, KD, D])
        xw1 = sb("xw1", [P, KD, D])
        w1q = sb("w1q", [P, KD, HID], F32R)
        w2q = sb("w2q", [P, KM, D], BF16)
        fc = sb("fc", [P, KM, TAPS_F + 1])
        fcs = sb("fcs", [P, KM, TAPS_F])
        W_in_top = sb("W_in_top", [P, KD, 2 * INNER], F32R)
        W_in_lo = sb("W_in_lo", [P, KD, 2 * INNER], F32R)
        ac = sb("ac", [P, KI, TAPS1 + 1])
        acs = sb("acs", [P, KI, TAPS1])
        W_out_sb = sb("W_out_sb", [P, KI, D])
        wq_sb = sb("wq_sb", [P, KD, D])
        bq_sb = sb("bq_sb", [P, KD])
        bk_sb = sb("bk_sb", [P, KD])
        wo_sb = sb("wo_sb", [P, KD, D])
        kT = sb("kT", [P, KD, B * CTX])
        kbd = [sb(f"kbd{s}", [P, KD, HG * CTX]) for s in range(SLOTS)]
        vbd = sb("vbd", [P, B, HEADS // 2, 2 * VW])
        fm = sb("fm", [P, KD, D])
        toep = sb("toep", [P, 3 * P])
        rows3 = sb("rows3", [P, 7, D], BF16)
        hrow = sb("hrow", [1, 4 * P])
        wsum = sb("wsum", [P, 2])
        wmean = sb("wmean", [P, 2])
        wscale = sb("wscale", [P, 2])

        xin = [sb(f"xin{s}", [P, NT, D]) for s in range(SLOTS)]
        xn = [sb(f"xn{s}", [P, NT, D]) for s in range(SLOTS)]
        xT = [sb(f"xT{s}", [P, KD, S]) for s in range(SLOTS)]
        xhi = [sb(f"xhi{s}", [P, KD, S], F32R) for s in range(SLOTS)]
        xlo = [sb(f"xlo{s}", [P, KD, S], F32R) for s in range(SLOTS)]
        res = [sb(f"res{s}", [P, NT, D]) for s in range(SLOTS)]
        stats = [sb(f"stats{s}", [P, NT, 6]) for s in range(SLOTS)]
        mv = [sb(f"mv{s}", [P, NT, 2]) for s in range(SLOTS)]
        vareps = [sb(f"vareps{s}", [P, NT]) for s in range(SLOTS)]
        rstd = [sb(f"rstd{s}", [P, NT]) for s in range(SLOTS)]
        shift = [sb(f"shift{s}", [P, NT]) for s in range(SLOTS)]
        amax = [sb(f"amax{s}", [P, 4, NT]) for s in range(SLOTS)]
        amax2 = [sb(f"amax2{s}", [P, 4, NT]) for s in range(SLOTS)]
        ARENA = 14 * S
        arena = [sb(f"arena{s}", [P, ARENA]) for s in range(SLOTS)]

        def carve(s, at, *shape, dt=F32):
            n = int(np.prod(shape)) * (2 if dt == BF16 else 4) // 4
            assert at + n <= ARENA, (at, n)
            a = arena[s][:, at:at + n]
            if dt == BF16:
                a = a.bitcast(BF16)
            if len(shape) == 2:
                a = a.rearrange("p (a b) -> p a b", a=shape[0])
            return a

        PADW = S + 4
        pad = [sb(f"pad{s}", [P, 4, PADW]) for s in range(SLOTS)]
        uconv = [carve(s, 0, 4, S) for s in range(SLOTS)]
        v1 = [carve(s, 4 * S, KD, S) for s in range(SLOTS)]
        vn = [carve(s, 6 * S, NT, D) for s in range(SLOTS)]
        z1 = [carve(s, 8 * S, KD, S) for s in range(SLOTS)]
        side1 = [carve(s, 12 * S, len(SIDE_U), S) for s in range(SLOTS)]
        gconv = [pad[s][:, :, 4:] for s in range(SLOTS)]
        hid = [carve(s, 0, KM, S) for s in range(SLOTS)]
        hq = [carve(s, 8 * S, KM, S, dt=BF16) for s in range(SLOTS)]
        diag = [carve(s, 12 * S, NT, P) for s in range(SLOTS)]
        colmax = [sb(f"colmax{s}", [P, 2, S]) for s in range(SLOTS)]
        th = [carve(s, 0, KI, S) for s in range(SLOTS)]
        aconv = [carve(s, 4 * S, KI, S) for s in range(SLOTS)]
        y4 = [carve(s, 8 * S, KI, S) for s in range(SLOTS)]
        side4 = [carve(s, 12 * S, 2, S) for s in range(SLOTS)]
        qT = [carve(s, 0, KD, S) for s in range(SLOTS)]
        sub = [carve(s, 2 * S, 2, S) for s in range(SLOTS)]
        prob = [carve(s, 4 * S, 2, S) for s in range(SLOTS)]
        pT = [carve(s, 6 * S, 2, S) for s in range(SLOTS)]
        o5 = [carve(s, 8 * S, NT, D) for s in range(SLOTS)]
        oT = [carve(s, 10 * S, KD, S) for s in range(SLOTS)]
        smax = [sb(f"smax{s}", [P, 2, HG]) for s in range(SLOTS)]
        rsum = [sb(f"rsum{s}", [P, HEADS]) for s in range(SLOTS)]
        outb = [carve(s, 12 * S, NT, D) for s in range(SLOTS)]

        w_in_nat = carve(0, 10 * S, KD, 4 * P).rearrange("p k (c n) -> p k c n", n=P)
        W_in_nat = pad[1][:, :, 4:]
        w1_nat = carve(1, 0, KM, D)
        w2_nat = carve(1, 4 * S, KD, HID)
        xw_nat = carve(1, 8 * S, KD, 2 * D)
        wk_sb = carve(1, 10 * S, KD, D)
        wv_sb = carve(1, 11 * S, KD, D)
        ctx_nat = carve(1, 12 * S, 2, D)
        ctxT = carve(1, 13 * S, KD, B * CTX)
        xw2 = xin[1][:, 0:2, :]
        ctxT2 = xn[1][:].rearrange("p t d -> p (t d)").rearrange("p (k n) -> p k n", k=KD)
        bvb = res[1][:, 0, :]
        csum = res[1][:, 1, 0:KD * B]
        fmlp = res[1][:, 2:4, :].rearrange("p t d -> p (t d)")
        misc = colmax[1][:].rearrange("p t d -> p (t d)")

        dft_sb = [carve(1, 8 * S, KD, D), carve(1, 9 * S, KD, D),
                  kbd[0][:, 0, :].rearrange("p (k n) -> p k n", k=KD)]
        wf_nat = [kbd[0][:, 1, :].rearrange("p (k n) -> p k n", k=KD),
                  xT[1][:, 1, :].rearrange("p (k n) -> p k n", k=KD)]
        fAB = [carve(1, 12 * S, KD, D), carve(1, 10 * S, KD, D)]
        fw1b, fw2_sb, fw3_sb = fmlp[0:4, 0:FW], fmlp[0:FW, FW:2 * FW], fmlp[0:FW, 2 * FW:2 * FW + D]
        f_t0, f_h1, f_h2, f_b2 = (fmlp[0:n, 500 + i:501 + i] for i, n in enumerate((4, FW, FW, FW)))
        brow = [[misc[:, i * D:(i + 1) * D] for i in range(3)],
                [misc[:, 3 * D:4 * D]] + [xT[1][:, 0, i * D:(i + 1) * D] for i in range(2)]]
        brow_b = [[kbd[1][:, n, i * D // 2:(i + 1) * D // 2].bitcast(BF16) for i in range(3)] for n in range(2)]
        toep_rev = colmax[0][:, 0, 0:3 * P]

        def full_value(r, name):
            b, n = TURN[name]
            return r * len(TURNS[b]) + n + 1

        class Side:
            def __init__(self, eng, s, r):
                self.eng, self.s, self.r = eng, s, r

            def wait(self, name, n):
                self.eng.wait_ge(ready[name][self.s], self.r * PER_BATCH[name] + n)

            def full(self, name):
                self.eng.wait_ge(bank_full[self.s][TURN[name][0]], full_value(self.r, name))
                return self.psum(name)

            def read(self, name):
                self.eng.wait_ge(bank_read[self.s][TURN[name][0]], full_value(self.r, name))

            def psum(self, name):
                return bank[self.s][TURN[name][0]]

        def done(ins, name, s):
            ins.then_inc(ready[name][s], 1)

        def read_by(s, name, ins):
            ins.then_inc(bank_read[s][TURN[name][0]], 1)

        def job_bank(name):
            return bank[1][JOB[name][0] % 4]

        def wait_job_read(eng, name):
            eng.wait_ge(job_read[READER[name]], JOB[name][1] + 1)

        def two(p):
            return p[:].rearrange("p (a d) -> p a d", a=2)

        def merged(engine, slot_programs):
            for c in MERGE[engine]:
                next(slot_programs[int(c)], None)
            for program in slot_programs:
                for _ in program:
                    pass

        def slot_programs(prepare, batch):
            def program(s):
                if s == 1:
                    yield from prepare()
                for r in range(ROUNDS):
                    yield from batch(s, r)
            return [program(s) for s in range(SLOTS)]

        block = ctx.enter_context(nc.Block())

        def chunks(w):
            return w.rearrange("(k p) n -> p k n", p=P)

        def column(v):
            return v.rearrange("(c p) -> p c", p=P)

        @block.sync
        def _(sp):
            def load(name, dst, src):
                sp.dma_start(dst, src).then_inc(w_loaded[name], 16)

            def load_x(b):
                s = b % SLOTS
                sp.dma_start(xin[s][:], x[b].rearrange("(t p) d -> p t d", p=P)).then_inc(ready["x"][s], 16)

            with nc.allow_non_contiguous_dma(reason="small per-channel constants"):
                load("eye", eye_sb[:], chunks(eye))
                load_x(0)
                for k in range(KD):
                    load("win", w_in_nat[:, k, :, :].rearrange("p (i c) n -> p i (c n)", i=2),
                         w_in[k * P:(k + 1) * P].rearrange("p (i n) -> p i n", i=3)[:, 0:3:2, :])
                for src, dst in ((fw1, fw1b[0:3]), (fb1.rearrange("(o d) -> o d", o=1), fw1b[3:4]),
                                 (fw2, fw2_sb), (fw3, fw3_sb), (time0, f_t0),
                                 (fb2.rearrange("(p o) -> p o", o=1), f_b2)):
                    load("filter", dst, src)
                for i, c in enumerate((0, 2 * D)):
                    e = slice(2 * i, 2 * i + 2)
                    load("uconst", uc[:, e, TAPS0 + 1], column(b_in[c:c + D]))
                    load("uconst", uc[:, e, 0:TAPS0], w_conv[c:c + D].rearrange("(c p) o j -> p c (o j)", p=P))
                    load("uconst", uc[:, e, TAPS0], column(b_conv[c:c + D]))
                load("uconst", fbc[:], column(filt_bias))
                load("xw", xw_nat, chunks(xw))
                load("w1", w1_nat, chunks(w1))
                load("w2", w2_nat, chunks(w2))
                load("ctx", ctx_nat, ctx_in.rearrange("(j b) t d -> (b t) j d", b=2))
                load("wout", w_out_sb[:], chunks(w_out))
                load("cffn", fc[:, :, 0:TAPS_F], cw.rearrange("(c p) o j -> p c (o j)", p=P))
                load("cffn", fc[:, :, TAPS_F], column(cb))
                for k in range(KD):
                    load("W_in", W_in_nat[:, 2 * k:2 * k + 2, :],
                         W_in[k * P:(k + 1) * P].rearrange("p (c n) -> p c n", c=2))
                load("c1", ac[:, :, 0:TAPS1], cw1.rearrange("(c p) o j -> p c (o j)", p=P))
                load("c1", ac[:, :, TAPS1], column(cb1))
                load("W_out", W_out_sb[:], chunks(W_out))
                for src, dst in ((chunks(Wk), wk_sb), (chunks(Wv), wv_sb), (column(bk), bk_sb[:]),
                                 (bv.partition_broadcast(P), bvb), (head_mask, mask_sb[:])):
                    load("kv", dst, src)
                for src, dst in ((chunks(Wq), wq_sb[:]), (column(bq), bq_sb[:]), (chunks(Wo), wo_sb[:])):
                    load("attn", dst, src)
                load("dft", dft_sb[2], chunks(dft[2 * D:3 * D]))
                load("dft", wf_nat[0], chunks(wfr))
                load("dft", wf_nat[1], chunks(wfi))
                sp.wait_ge(job_done, JOB["w2T"][0] + 1)
                load("dft", dft_sb[0], chunks(dft[0:D]))
                load("dft", dft_sb[1], chunks(dft[D:2 * D]))
                wait_job_read(sp, "part2")
                load_x(1)
            for b in range(B):
                s, r = b % SLOTS, b // SLOTS
                side = Side(sp, s, r)
                if b + SLOTS < B:
                    side.wait("xn_even", 2)
                    side.wait("xn_odd", 2)
                    load_x(b + SLOTS)
            for b in range(B):
                s, r = b % SLOTS, b // SLOTS
                for h in range(2):
                    Side(sp, s, r).read(f"m.{h}")
                    sp.dma_start(out[b, 2 * h * P:(2 * h + 2) * P].rearrange("(t p) d -> p t d", p=P),
                                 outb[s][:, 2 * h:2 * h + 2, :]).then_inc(ready["stored"][s], 16)
            for s in range(SLOTS):
                sp.wait_ge(ready["stored"][s], 32 * ROUNDS)

        @block.tensor
        def _(pe):
            def job(name):
                n = JOB[name][0]
                if n >= 4:
                    wait_job_read(pe, JOBS[n - 4][0])
                return job_bank(name)

            def job_end(ins):
                ins.then_inc(job_done, 1)

            def prepare():
                pe.wait_ge(w_loaded["filter"], 6 * 16)
                p = job("filt1")
                job_end(pe.matmul(p[0:FW, 0:1], fw1b, f_t0, start=True, stop=True))
                yield
                wait_job_read(pe, "filt1")
                p = job("filt2")
                job_end(pe.matmul(p[0:FW, 0:1], fw2_sb, f_h1, start=True, stop=True))
                yield
                wait_job_read(pe, "filt2")
                p = job("filt3")
                job_end(pe.matmul(p[0:1, 0:D], f_h2, fw3_sb, start=True, stop=True))
                yield
                pe.wait_ge(w_loaded["eye"], 16)
                pe.wait_ge(w_loaded["xw"], 16)
                for half, name in enumerate(("w1T", "w2T")):
                    p = job(name)
                    for k in range(KD):
                        for j in range(KD):
                            last = pe.transpose(p[:, k * D + j * P:k * D + (j + 1) * P],
                                                xw_nat[:, j, half * D + k * P:half * D + (k + 1) * P], ident)
                    job_end(last)
                    yield
                pe.wait_ge(w_loaded["ctx"], 16)
                p = job("ctxT")
                for k in range(KD):
                    for j in range(2):
                        last = pe.transpose(p[:, k * D + j * P:k * D + (j + 1) * P],
                                            ctx_nat[:, j, k * P:(k + 1) * P], ident)
                job_end(last)
                yield
                pe.wait_ge(csum_ready, 1)
                wait_job_read(pe, "w2T")
                p = job("part2")
                for k in range(KD):
                    last = pe.matmul(p[0:B, 0:D], csum[:, k * B:(k + 1) * B], xw2[:, k, :],
                                     start=k == 0, stop=k == KD - 1)
                job_end(last)
                yield
                pe.wait_ge(consts_set, POOL_CONSTS)
                pe.wait_ge(wsum_ready, 2)
                p = job("abssum")
                job_end(pe.matmul(p[:, 0:2], ones[:], wsum[:], start=True, stop=True))
                yield
                pe.wait_ge(ternary_ready, 1)
                for i in range(4):
                    p = job(f"q1.{i}")
                    k, half = i // 2, i % 2
                    for m in range(4):
                        last = pe.transpose(p[:, m * P:(m + 1) * P],
                                            w1_nat[:, half * 4 + m, k * P:(k + 1) * P], ident)
                    job_end(last)
                    yield
                pe.wait_ge(ternary_ready, 2)
                for i in range(4):
                    p = job(f"q2.{i}")
                    for m in range(2):
                        for j in range(KD):
                            last = pe.transpose(p[:, m * D + j * P:m * D + (j + 1) * P],
                                                w2_nat[:, j, (2 * i + m) * P:(2 * i + m + 1) * P], ident)
                    job_end(last)
                    yield
                pe.wait_ge(w_loaded["kv"], 5 * 16)
                wait_job_read(pe, "ctxT")
                p = job("kT")
                for f in range(KD):
                    for k in range(KD):
                        last = pe.matmul(p[:, f * B * CTX:(f + 1) * B * CTX], wk_sb[:, k, f * P:(f + 1) * P],
                                         ctxT[:, k, :], start=k == 0, stop=k == KD - 1)
                job_end(last)
                yield
                pe.wait_ge(ctxT2_ready, KD)
                for h in range(2):
                    p = job(f"v.{h}")
                    for b in range(2):
                        for k in range(KD):
                            last = pe.matmul(p[:, b * D:(b + 1) * D], ctxT2[:, k, (2 * h + b) * P:(2 * h + b + 1) * P],
                                             wv_sb[:, k, :], start=k == 0, stop=k == KD - 1)
                    job_end(last)
                    yield
                pe.wait_ge(w_loaded["dft"], 5 * 16)
                for name, terms in (("fA", ((0, 0), (1, 1))), ("fB", ((1, 0), (0, 2)))):
                    p = job(name)
                    for j in range(KD):
                        for n, (w, c) in enumerate(terms):
                            for k in range(KD):
                                last = pe.matmul(p[:, j * D:(j + 1) * D], wf_nat[w][:, k, j * P:(j + 1) * P],
                                                 dft_sb[c][:, k, :], start=n == 0 and k == 0,
                                                 stop=n == 1 and k == KD - 1)
                    job_end(last)
                    yield
                wait_job_read(pe, "fB")
                p = job("fM")
                for j in range(KD):
                    for n, c in enumerate((0, 2)):
                        for k in range(KD):
                            last = pe.matmul(p[:, j * D:(j + 1) * D], fAB[n][:, k, j * P:(j + 1) * P],
                                             dft_sb[c][:, k, :], start=n == 0 and k == 0,
                                             stop=n == 1 and k == KD - 1)
                job_end(last)
                yield
                wait_job_read(pe, [n for n, e in JOBS if e == "act"][-1])
                wait_job_read(pe, [n for n, e in JOBS if e == "dve"][-1])

            def batch(s, r):
                b = r * SLOTS + s
                side = Side(pe, s, r)

                def take(name):
                    if full_value(r, name) > 1:
                        pe.wait_ge(bank_read[s][TURN[name][0]], full_value(r, name) - 1)
                    return side.psum(name)

                def fill(name, ins):
                    ins.then_inc(bank_full[s][TURN[name][0]], 1)

                def half(h):
                    return slice(2 * h * P, (2 * h + 2) * P)

                def wait_xn(n, t):
                    side.wait("xn_odd" if t % 2 else "xn_even", 2 * n - 1 + t // 2)

                def transpose_x(layer, src, wait):
                    for h in range(2):
                        p = take(f"{layer}.{h}")
                        for t in range(2):
                            wait(2 * h + t)
                            for k in range(KD):
                                last = pe.transpose(p[:, k * D + t * P:k * D + (t + 1) * P],
                                                    src[:, 2 * h + t, k * P:(k + 1) * P], ident)
                        fill(f"{layer}.{h}", last)
                        yield

                def project_halves(name, weights, wait, row):
                    lhs = oT[s] if name == "k" else xT[s]
                    for h in range(2):
                        p = take(f"{name}.{h}")
                        for t in range(2):
                            tt = 2 * h + t
                            o = p[:, t * D:(t + 1) * D]
                            pe.matmul(o, ones_b[:], row, start=True, stop=False)
                            if t == 0:
                                wait(h)
                            for k in range(KD):
                                last = pe.matmul(o, lhs[:, k, tt * P:(tt + 1) * P], weights[:, k, :],
                                                 start=False, stop=k == KD - 1)
                        fill(f"{name}.{h}", last)
                        yield

                def project_chunks(name, lhs, weights, nk, wait, row=None):
                    p = [take(f"{name}.{h}") for h in range(2)]
                    if row is not None:
                        for tt in range(NT):
                            pe.matmul(p[tt // 2][:, tt % 2 * D:(tt % 2 + 1) * D], ones_b[:], row,
                                      start=tt % 2 == 0, stop=False, skip_group_check=True)
                    for k in range(nk):
                        wait(k)
                        for tt in range(NT):
                            last = pe.matmul(p[tt // 2][:, tt % 2 * D:(tt % 2 + 1) * D],
                                             lhs[:, k, tt * P:(tt + 1) * P], weights[:, k, :],
                                             start=row is None and k == 0 and tt % 2 == 0,
                                             stop=k == nk - 1 and tt % 2 == 1, skip_group_check=True)
                            if k == nk - 1 and tt % 2:
                                fill(f"{name}.{tt // 2}", last)
                        yield

                def three_products(p, layer, halved, w_hi, w_lo):
                    for n, (w, buf) in enumerate(((w_hi, xhi[s]), (w_lo, xhi[s]), (w_hi, xlo[s]))):
                        for h, cols in [(0, half(0)), (1, half(1))] if halved else [(0, slice(0, S))]:
                            if halved and n == 0:
                                side.wait(f"xhi{layer}", h + 1)
                            if halved and n == 2:
                                side.read(f"x1.{h}") if layer == 1 else side.wait("xlo4", h + 1)
                            for k in range(KD):
                                last = pe.matmul(p[:, cols], w[k], buf[:, k, cols], start=n + k + h == 0,
                                                 stop=n + k == 3 and cols.stop == S, skip_group_check=True)
                    return last

                pe.wait_ge(w_loaded["eye"], 16)
                side.wait("x", 16)
                yield from transpose_x("x1", xin[s], lambda t: None)
                pe.wait_ge(win_hi, 1)
                pe.wait_ge(win_split, 1)
                for n, e in enumerate(U_ORDER):
                    p = take(f"u.{e}")
                    fill(f"u.{e}", three_products(p, 1, n == 0, [w_in_hi[:, k, e, :] for k in range(KD)],
                                                  [w_in_lo[:, k, e, :] for k in range(KD)]))
                    yield
                for k in range(KD):
                    p = take(f"v.{k}")
                    side.wait("v", k + 1)
                    for t in range(NT):
                        last = pe.transpose(p[:, t * P:(t + 1) * P], v1[s][:, k, t * P:(t + 1) * P], ident)
                    fill(f"v.{k}", last)
                    yield
                pe.wait_ge(toep_ready, 1)
                for k in range(KD):
                    p = take(f"y.{k}")
                    side.read(f"v.{k}")
                    for t in range(NT):
                        n = min(3 * P, S - t * P)
                        last = pe.matmul(p[:, t * P:t * P + n], vn[s][:, t, k * P:(k + 1) * P], toep[:, 0:n],
                                         start=t == 0, stop=t == NT - 1, skip_group_check=True)
                    fill(f"y.{k}", last)
                    yield
                pe.wait_ge(w_loaded["wout"], 16)
                pe.wait_ge(consts_set, POOL_CONSTS)
                pe.wait_ge(rows_loaded[1], 3 * 16)
                yield from project_chunks("o", z1[s], w_out_sb, KD, lambda k: side.wait("z", k + 1), rows3[:, B, :])
                yield from transpose_x("x2", xn[s], lambda t: wait_xn(1, t))
                wait_job_read(pe, "w1T")
                pe.wait_ge(rows_loaded[0], 3 * 16)
                yield from project_halves("e", xw1, lambda h: side.read(f"x2.{h}"), rows3[:, b, :])
                yield from transpose_x("x3", res[s], lambda t: side.wait("xq_odd" if t % 2 else "xq_even", t // 2 + 1))
                wait_job_read(pe, "q1.3")
                for m in range(KM):
                    p = take(f"g.{m}")
                    for cols in [half(0), half(1)] if m == 0 else [slice(0, S)]:
                        for part, buf in enumerate((xhi[s], xlo[s])):
                            if m == 0 and part == 0:
                                side.wait("xhi", cols.stop // (2 * P))
                            if m == 0 and part == 1:
                                side.read(f"x3.{cols.start // (2 * P)}")
                            for k in range(KD):
                                last = pe.matmul(p[:, cols], w1q[:, k, m * P:(m + 1) * P], buf[:, k, cols],
                                                 start=part + k == 0, stop=part + k == 2)
                    fill(f"g.{m}", last)
                    yield
                p = take("amax")
                side.wait("colmax", 1)
                for t in range(NT):
                    last = pe.transpose(p[:, t * P:(t + 1) * P], colmax[s][:, 0, t * P:(t + 1) * P], ident)
                fill("amax", last)
                yield
                p = take("scale")
                for t in range(NT):
                    side.wait("diag", t + 1)
                    last = pe.matmul(p[:, t * P:(t + 1) * P], ones[:], diag[s][:, t, :], start=True, stop=True)
                fill("scale", last)
                yield
                wait_job_read(pe, "q2.3")
                yield from project_chunks("f", hq[s], w2q, KM, lambda k: side.wait("hq", k + 1))
                yield from transpose_x("x4", xn[s], lambda t: wait_xn(2, t))
                pe.wait_ge(W_in_hi, 1)
                pe.wait_ge(W_in_split, 1)
                for m in range(KI):
                    for name, c in ((f"t.{m}", INNER + m * P), (f"a.{m}", m * P)):
                        p = take(name)
                        fill(name, three_products(p, 4, name == "t.0",
                                                  [W_in_top[:, k, c:c + P] for k in range(KD)],
                                                  [W_in_lo[:, k, c:c + P] for k in range(KD)]))
                        yield
                pe.wait_ge(w_loaded["W_out"], 16)
                yield from project_chunks("j", y4[s], W_out_sb, KI, lambda k: side.wait("y", k + 1))
                yield from transpose_x("x5", xn[s], lambda t: wait_xn(3, t))
                pe.wait_ge(w_loaded["attn"], 3 * 16)
                for h in range(2):
                    p = take(f"q.{h}")
                    side.read(f"x5.{h}")
                    for f in range(KD):
                        for k in range(KD):
                            last = pe.matmul(p[:, f * D:(f + 1) * D], wq_sb[:, k, f * P:(f + 1) * P],
                                             xT[s][:, k, half(h)], start=k == 0, stop=k == 1)
                    fill(f"q.{h}", last)
                    yield
                wait_job_read(pe, "v.1")
                for i in range(UNITS + 2):
                    if i < UNITS:
                        t, g = i // 2, i % 2
                        p = take(f"s.{i}")
                        side.read(f"q.{t // 2}")
                        side.wait("kbd", g + 1)
                        fill(f"s.{i}", pe.matmul(p[:], qT[s][:, g, t * P:(t + 1) * P], kbd[s][:, g, :],
                                                 start=True, stop=True))
                        yield
                    if 0 <= i - 1 < UNITS:
                        n = i - 1
                        p = take(f"pT.{n}")
                        side.wait("p", n + 1)
                        for c in range(4):
                            last = pe.transpose(p[:, c * P:(c + 1) * P], prob[s][:, n % 2, c * P:(c + 1) * P], ident)
                        fill(f"pT.{n}", last)
                        yield
                    if i >= 2:
                        n = i - 2
                        t, g = n // 2, n % 2
                        p = take(f"pv.{t}") if g == 0 else side.psum(f"pv.{t}")
                        side.read(f"pT.{n}")
                        for c in range(4):
                            j = 4 * g + c
                            last = pe.matmul(p[:, j * 2 * VW:(j + 1) * 2 * VW], pT[s][:, n % 2, c * P:(c + 1) * P],
                                             vbd[:, b, j, :], start=True, stop=True)
                        if g == 1:
                            fill(f"pv.{t}", last)
                        yield
                yield from transpose_x("oT", o5[s], lambda t: side.read(f"pv.{t}"))
                yield from project_halves("k", wo_sb, lambda h: side.read(f"oT.{h}"), rows3[:, B + 1, :])
                yield from transpose_x("x6", xn[s], lambda t: wait_xn(4, t))
                wait_job_read(pe, "fM")
                yield from project_halves("m", fm, lambda h: side.read(f"x6.{h}"), rows3[:, B + 2, :])

            merged("pe", slot_programs(prepare, batch))

        @block.scalar
        def _(act):
            def job(name):
                act.wait_ge(job_done, JOB[name][0] + 1)
                return job_bank(name)

            def job_end(ins):
                ins.then_inc(job_read["act"], 1)

            def prepare():
                p = job("filt1")
                job_end(act.activation(f_h1, p[0:FW, 0:1], ACT.Silu))
                yield
                p = job("filt2")
                job_end(act.activation(f_h2, p[0:FW, 0:1], ACT.Silu, bias=f_b2))
                yield
                act.wait_ge(hrow_zeroed, 1)
                p = job("filt3")
                job_end(act.activation(hrow[:, 3 * P - 1:3 * P - 1 - D:-1], p[0:1, 0:D], ACT.Copy))
                wait_job_read(act, "filt3")
                act.dma_start(toep_rev, bass.AP(hrow, 0, [[4 * P, 1], [1, P], [1, 3 * P]])).then_inc(toep_loaded, 16)
                yield
                p = job("w2T")
                job_end(act.activation(xw2, two(p), ACT.Copy))
                yield
                p = job("ctxT")
                for k in range(KD):
                    act.activation(ctxT2[:, k, :].rearrange("p (b r t) -> p b r t", b=B, r=2),
                                   p[:, k * D:(k + 1) * D].rearrange("p (b t) -> p b t", b=B).unsqueeze(2)
                                   .broadcast_to([P, B, 2, CTX]), ACT.Copy).then_inc(ctxT2_ready, 1)
                job_end(act.activation(ctxT, two(p), ACT.Copy))
                yield
                act.wait_ge(consts_set, POOL_CONSTS)
                for i in range(4):
                    p = job(f"q1.{i}")
                    k, half = i // 2, i % 2
                    job_end(act.activation(w1q[:, k, half * S:(half + 1) * S], p[:], ACT.Identity, bias=magicneg[:]))
                    yield
                act.wait_ge(w_loaded["W_in"], KD * 16)
                act.activation(W_in_top[:].rearrange("p k (c n) -> p (k c) n", c=2), W_in_nat, ACT.Copy).then_inc(W_in_hi, 1)
                yield
                for i, name in enumerate(("fA", "fB")):
                    p = job(name)
                    job_end(act.activation(fAB[i], two(p), ACT.Copy))
                    yield
                act.wait_ge(W_in_split, 1)

            def batch(s, r):
                side = Side(act, s, r)

                def copy_xT(layer, to):
                    for h in range(2):
                        p = side.full(f"{layer}.{h}")
                        read_by(s, f"{layer}.{h}", act.activation(to[:, :, h * D:(h + 1) * D], two(p), ACT.Copy))
                        yield

                def normalise(n, to):
                    for h in range(2):
                        side.wait("rstd", 2 * n - 1 + h)
                        side.wait("shift", 2 * n - 1 + h)
                        t = 2 * h + 1
                        done(act.activation(to[:, t, :], res[s][:, t, :], ACT.Identity,
                                            bias=shift[s][:, t:t + 1], scale=rstd[s][:, t:t + 1]), "xn_odd", s)
                        yield

                def normalise_banks(n, name, to):
                    for h in range(2):
                        side.wait("rstd", 2 * n - 1 + h)
                        side.wait("shift", 2 * n - 1 + h)
                        p = side.psum(f"{name}.{h}")
                        for t in range(2):
                            tt = 2 * h + t
                            ins = act.activation(to[:, tt, :], p[:, t * D:(t + 1) * D], ACT.Identity,
                                                 bias=shift[s][:, tt:tt + 1], scale=rstd[s][:, tt:tt + 1])
                        read_by(s, f"{name}.{h}", ins)
                        yield

                def upper_parts(layer, signal, whole):
                    for h in range(2):
                        p = side.full(f"{layer}.{h}")
                        q = slice(h * D, (h + 1) * D)
                        done(act.activation(xhi[s][:, :, q], two(p), ACT.Copy), signal, s)
                        yield
                        if whole:
                            read_by(s, f"{layer}.{h}", act.activation(xT[s][:, :, q], two(p), ACT.Copy))
                            yield

                if s == 0 and r == 0:
                    act.wait_ge(w_loaded["win"], 2 * 16)
                    act.activation(w_in_hi[:], w_in_nat, ACT.Copy).then_inc(win_hi, 1)
                    yield
                yield from upper_parts("x1", "xhi1", False)
                act.wait_ge(w_loaded["uconst"], 7 * 16)
                act.wait_ge(consts_set, POOL_CONSTS)
                if r:
                    act.wait_ge(ready["stored"][s], 32 * r)
                for e in U_ORDER:
                    p = side.full(f"u.{e}")
                    read_by(s, f"u.{e}", act.activation(pad[s][:, e, 4:], p[:], ACT.Identity,
                                                        bias=uc[:, e, TAPS0 + 1:TAPS0 + 2]))
                    yield
                    if e in SIDE_U:
                        side.read(f"u.{e}")
                        done(act.activation(side1[s][:, SIDE_U.index(e), :], pad[s][:, e, 2:2 + S], ACT.Copy,
                                            scale=uc[:, e, 0:1]), "side", s)
                        yield
                for k in range(KD):
                    p = side.full(f"v.{k}")
                    read_by(s, f"v.{k}", act.activation(vn[s][:, :, k * P:(k + 1) * P],
                                                        p[:].rearrange("p (t n) -> p t n", t=NT), ACT.Copy))
                    yield
                yield from normalise(1, xn[s])
                yield from copy_xT("x2", xT[s])
                yield from normalise_banks(2, "e", xn[s])
                yield from upper_parts("x3", "xhi", False)
                act.wait_ge(taps_ready, 2)
                for m in range(KM + 1):
                    if m < KM:
                        p = side.full(f"g.{m}")
                        if m >= 4:
                            side.wait("hid", m - 3)
                        done(act.activation(gconv[s][:, m % 4, :], p[:], ACT.Identity,
                                            bias=fc[:, m, TAPS_F:TAPS_F + 1], scale=fcs[:, m, 1:2]), "gmid", s)
                        yield
                    if m >= 1:
                        side.read(f"g.{m - 1}")
                        done(act.activation(hid[s][:, m - 1, :], gconv[s][:, (m - 1) % 4, :], ACT.Silu), "hid", s)
                        yield
                p = side.full("scale")
                read_by(s, "scale", act.activation(colmax[s][:, 1, :], p[:], ACT.Copy))
                yield
                yield from normalise(3, xn[s])
                yield from upper_parts("x4", "xhi4", True)
                for m in range(KI + 2):
                    if m < KI:
                        p = side.full(f"t.{m}")
                        read_by(s, f"t.{m}", act.activation(th[s][:, m, :], p[:], ACT.Tanh, scale=0.5))
                        yield
                    if 1 <= m <= KI:
                        j = m - 1
                        side.read(f"a.{j}")
                        if j >= 2:
                            side.wait("mid", 4 + j - 1)
                        done(act.activation(side4[s][:, j % 2, :], pad[s][:, j, 1:1 + S], ACT.Copy,
                                            scale=acs[:, j, 0:1]), "side", s)
                        yield
                    if m >= 2:
                        side.wait("conv", m - 1)
                        done(act.activation(y4[s][:, m - 2, :], aconv[s][:, m - 2, :], ACT.Silu), "y", s)
                        yield
                yield from normalise(4, xn[s])
                yield from copy_xT("x5", xT[s])
                act.wait_ge(w_loaded["attn"], 3 * 16)
                for h in range(2):
                    p = side.full(f"q.{h}")
                    for f in range(KD):
                        ins = act.activation(qT[s][:, f, h * D:(h + 1) * D], p[:, f * D:(f + 1) * D], ACT.Identity,
                                             bias=bq_sb[:, f:f + 1])
                    read_by(s, f"q.{h}", ins)
                    yield
                for i in range(UNITS + 1):
                    if i < UNITS:
                        side.read(f"s.{i}")
                        done(act.activation(prob[s][:, i % 2, :], sub[s][:, i % 2, :], ACT.Exp), "p", s)
                        yield
                    if i >= 1:
                        p = side.full(f"pT.{i - 1}")
                        read_by(s, f"pT.{i - 1}", act.activation(pT[s][:, (i - 1) % 2, :], p[:], ACT.Copy))
                        yield
                yield from copy_xT("oT", oT[s])
                yield from normalise(5, xn[s])
                yield from copy_xT("x6", xT[s])
                if r:
                    act.wait_ge(ready["stored"][s], 32 * r)
                yield from normalise_banks(6, "m", outb[s])

            merged("act", slot_programs(prepare, batch))

        @block.gpsimd
        def _(pool):
            def prepare():
                for n, rows in ((1, slice(B, B + 3)), (0, slice(0, B))):
                    pool.wait_ge(rows_split, 2 - n)
                    for i in range(3):
                        pool.dma_start(rows3[i:i + 1, rows], brow_b[n][i][0:rows.stop - rows.start])\
                            .then_inc(rows_loaded[n], 16)
                    yield
                pool.wait_ge(W_in_hi, 1)
                for k in range(KD):
                    ins = pool.tensor_tensor(W_in_lo[:, k, :].rearrange("p (c n) -> p c n", c=2),
                                             W_in_nat[:, 2 * k:2 * k + 2, :],
                                             W_in_top[:, k, :].bitcast(F32).rearrange("p (c n) -> p c n", c=2),
                                             ALU.subtract)
                    if k == KD - 1:
                        ins.then_inc(W_in_split, 1)
                    yield
                for n in range(2):
                    pool.wait_ge(rows_loaded[n], 3 * 16)

            def batch(s, r):
                b = r * SLOTS + s
                side = Side(pool, s, r)

                def power(n):
                    for h in range(2):
                        side.wait("var", 2 * n - 1 + h)
                        done(pool.tensor_tensor(rstd[s][:, 2 * h:2 * h + 2], vareps[s][:, 2 * h:2 * h + 2],
                                                halfneg[:, 0:2], ALU.pow), "rstd", s)
                        yield
                        if n not in (2, 6):
                            t = 2 * h
                            side.wait("rstd", 2 * n - 1 + h)
                            side.wait("shift", 2 * n - 1 + h)
                            done(pool.tensor_scalar(xn[s][:, t, :], res[s][:, t, :], rstd[s][:, t:t + 1],
                                                    shift[s][:, t:t + 1], ALU.mult, ALU.add), "xn_even", s)
                            yield

                def rest_of_x(n):
                    for h in range(2):
                        side.read(f"x{n}.{h}")
                        q = slice(h * D, (h + 1) * D)
                        done(pool.tensor_tensor(xlo[s][:, :, q], xT[s][:, :, q], xhi[s][:, :, q].bitcast(F32),
                                                ALU.subtract), f"xlo{n}", s)
                        yield

                pool.wait_ge(w_loaded["uconst"], 7 * 16)
                for e in U_ORDER:
                    side.read(f"u.{e}")
                    ins = pool.tensor_scalar(uconv[s][:, e, :], pad[s][:, e, 4:], uc[:, e, 2:3],
                                             uc[:, e, TAPS0:TAPS0 + 1], ALU.mult, ALU.add)
                    done(ins, "part" if e in SIDE_U else "mid", s)
                    yield
                    if e in SIDE_U:
                        n = SIDE_U.index(e) + 1
                        side.wait("part", n)
                        side.wait("side", n)
                        done(pool.tensor_tensor(uconv[s][:, e, :], uconv[s][:, e, :], side1[s][:, n - 1, :],
                                                ALU.add), "mid", s)
                        yield
                for n in (1, 2):
                    yield from power(n)
                for h in range(2):
                    t = 2 * h + 1
                    side.wait("xscale", h + 1)
                    done(pool.tensor_scalar(res[s][:, t, :], xn[s][:, t, :], amax[s][:, 3, t:t + 1], MAGIC,
                                            ALU.mult, ALU.add), "xr", s)
                    yield
                    side.wait("xr", h + 1)
                    done(pool.tensor_scalar(res[s][:, t, :], res[s][:, t, :], -MAGIC, amax[s][:, 1, t:t + 1],
                                            ALU.add, ALU.mult), "xq_odd", s)
                    yield
                pool.wait_ge(w_loaded["kv"], 5 * 16)
                wait_job_read(pool, "kT")
                if b == 0:
                    wait_job_read(pool, "fM")
                if r:
                    for i in (UNITS - 2, UNITS - 1):
                        Side(pool, s, r - 1).full(f"s.{i}")
                for g in range(KD):
                    done(pool.tensor_tensor(kbd[s][:, g, :].rearrange("p (h t) -> p h t", h=HG),
                                            kT[:, g, b * CTX:(b + 1) * CTX].unsqueeze(1).broadcast_to([P, HG, CTX]),
                                            mask_sb[:].unsqueeze(2).broadcast_to([P, HG, CTX]), ALU.mult), "kbd", s)
                    yield
                side.wait("scale", 1)
                if r:
                    pool.wait_ge(ready["stored"][s], 32 * r)
                for t in range(NT):
                    done(pool.tensor_scalar(diag[s][:, t, :], ident, amax2[s][:, 3, t:t + 1], 1.0,
                                            ALU.mult, ALU.mult), "diag", s)
                yield
                side.read("scale")
                for m in POOL_SCALES:
                    done(pool.tensor_tensor(hid[s][:, m, :], hid[s][:, m, :], colmax[s][:, 1, :], ALU.mult),
                         "scaled", s)
                    yield
                yield from power(3)
                yield from rest_of_x(4)
                pool.wait_ge(taps_ready, 2)
                for m in range(KI):
                    side.read(f"a.{m}")
                    n = len(SIDE_U) + m + 1
                    done(pool.tensor_scalar(aconv[s][:, m, :], pad[s][:, m, 4:], acs[:, m, 3:4],
                                            ac[:, m, TAPS1:TAPS1 + 1], ALU.mult, ALU.add), "part", s)
                    yield
                    side.wait("part", n)
                    side.wait("side", n)
                    done(pool.tensor_tensor(aconv[s][:, m, :], aconv[s][:, m, :], side4[s][:, m % 2, :], ALU.add),
                         "mid", s)
                    yield
                for n in (4, 5, 6):
                    yield from power(n)

            for n, (buf, value) in enumerate(((ones[:], 1.0), (ones_b[:], 1.0), (halfneg[:], -0.5), (rows3[:], 0.0),
                                              (vbd[:], 0.0), (pad[0][:, :, 0:4], 0.0), (pad[1][:, :, 0:4], 0.0),
                                              (magicneg[:], -MAGIC))):
                pool.memset(buf, value).then_inc(consts_set, 1)
            pool.wait_ge(consts_set, 8)
            for half in range(2):
                pool.memset(vbd[64 * half:64 * half + 64, :, :, half * VW + DK], 1.0).then_inc(consts_set, 1)
            pool.wait_ge(consts_set, POOL_CONSTS)
            for n, v in enumerate((b_out, bo, fbias)):
                pool.dma_start(brow[1][0][n:n + 1], v.rearrange("(o d) -> o d", o=1)).then_inc(w_loaded["rows"], 16)
            pool.dma_start(brow[0][0][0:B], xb.partition_broadcast(B)).then_inc(w_loaded["bias"], 16)
            merged("pool", slot_programs(prepare, batch))

        @block.vector
        def _(vec):
            steps = [0] * SLOTS

            def step(s, ins):
                steps[s] += 1
                ins.then_inc(vec_step[s], 1)
                return steps[s]

            def need(s, n):
                vec.wait_ge(vec_step[s], n)

            def job(name):
                vec.wait_ge(job_done, JOB[name][0] + 1)
                return job_bank(name)

            def job_end(ins):
                ins.then_inc(job_read["dve"], 1)

            def split_rows(n, rows):
                for i in range(2):
                    k = step(1, vec.tensor_copy(brow_b[n][i][0:rows], brow[n][i][0:rows]))
                    need(1, k)
                    k = step(1, vec.tensor_tensor(brow[n][i + 1][0:rows], brow[n][i][0:rows], brow_b[n][i][0:rows],
                                                  ALU.subtract))
                    need(1, k)
                vec.tensor_copy(brow_b[n][2][0:rows], brow[n][2][0:rows]).then_inc(rows_split, 1)

            def prepare():
                vec.wait_ge(w_loaded["rows"], 3 * 16)
                split_rows(1, 3)
                yield
                vec.wait_ge(toep_loaded, 16)
                vec.tensor_copy(toep[:], toep_rev[:, ::-1]).then_inc(toep_ready, 1)
                yield
                p = job("w1T")
                vec.wait_ge(w_loaded["eye"], 16)
                job_end(vec.tensor_tensor(xw1[:], two(p), eye_sb[:], ALU.add))
                yield
                vec.wait_ge(w_loaded["w1"], 16)
                vec.tensor_reduce(wsum[:, 0:1], w1_nat, mybir.AxisListType.XY, ALU.add, apply_absolute_value=True)\
                   .then_inc(wsum_ready, 1)
                yield
                vec.wait_ge(w_loaded["w2"], 16)
                vec.tensor_reduce(wsum[:, 1:2], w2_nat, mybir.AxisListType.XY, ALU.add, apply_absolute_value=True)\
                   .then_inc(wsum_ready, 1)
                yield
                wait_job_read(vec, "ctxT")
                n = step(1, vec.tensor_reduce(csum, ctxT.rearrange("p k (b t) -> p (k b) t", b=B), AX, ALU.add))
                need(1, n)
                vec.tensor_scalar(csum, csum, 1.0 / CTX, None, ALU.mult).then_inc(csum_ready, 1)
                yield
                p = job("part2")
                vec.wait_ge(w_loaded["bias"], 16)
                job_end(vec.tensor_tensor(brow[0][0][0:B], p[0:B, 0:D], brow[0][0][0:B], ALU.add))
                wait_job_read(vec, "part2")
                split_rows(0, B)
                yield
                p = job("abssum")
                n = step(1, vec.tensor_scalar(wmean[:], p[:, 0:2], 1.0 / (HID * D), 1e-5, ALU.mult, ALU.max))
                need(1, n)
                job_end(vec.reciprocal(wscale[:], wmean[:]))
                wait_job_read(vec, "abssum")
                yield
                for i, w in enumerate((w1_nat, w2_nat)):
                    n = step(1, vec.tensor_scalar(w, w, wscale[:, i:i + 1], MAGIC, ALU.mult, ALU.add))
                    yield
                    need(1, n)
                    vec.tensor_scalar(w, w, MAGIC + 1.0, MAGIC - 1.0, ALU.min, ALU.max).then_inc(ternary_ready, 1)
                    yield
                vec.wait_ge(w_loaded["cffn"], 2 * 16)
                vec.wait_ge(w_loaded["c1"], 2 * 16)
                vec.tensor_scalar(fcs[:], fc[:, :, 0:TAPS_F], wmean[:, 0:1], None, ALU.mult).then_inc(taps_ready, 1)
                vec.tensor_scalar(acs[:], ac[:, :, 0:TAPS1], 0.5, None, ALU.mult).then_inc(taps_ready, 1)
                yield
                for i in range(4):
                    p = job(f"q2.{i}")
                    job_end(vec.tensor_scalar(w2q[:, 2 * i:2 * i + 2, :], two(p), -MAGIC, None, ALU.add))
                    yield
                p = job("kT")
                vec.wait_ge(w_loaded["kv"], 5 * 16)
                for f in range(KD):
                    ins = vec.tensor_scalar(kT[:, f, :], p[:, f * D:(f + 1) * D], bk_sb[:, f:f + 1], DK ** -0.5,
                                            ALU.add, ALU.mult)
                job_end(ins)
                yield
                vec.wait_ge(consts_set, POOL_CONSTS)
                for i in range(2):
                    p = job(f"v.{i}")
                    for b in range(2):
                        for half in range(2):
                            q = slice(64 * half, 64 * half + 64)
                            ins = vec.tensor_tensor(
                                vbd[q, 2 * i + b, :, half * VW:half * VW + DK],
                                p[q, b * D:(b + 1) * D].rearrange("p (j r d) -> p j r d", r=2, d=DK)[:, :, half, :],
                                bvb[q, :].rearrange("p (j r d) -> p j r d", r=2, d=DK)[:, :, half, :], ALU.add)
                    job_end(ins)
                    yield
                p = job("fM")
                job_end(vec.scalar_tensor_tensor(fm[:], two(p), 1.0 / D, eye_sb[:], ALU.mult, ALU.add))
                yield

            def batch(s, r):
                side = Side(vec, s, r)

                def st(ins):
                    return step(s, ins)

                def wt(n):
                    need(s, n)

                def layer_norm(n, tile, sums):
                    def shift_of(h):
                        side.wait("rstd", 2 * n - 1 + h)
                        q = slice(2 * h, 2 * h + 2)
                        done(vec.scalar_tensor_tensor(shift[s][:, q], mv[s][:, q, 0], -1.0, rstd[s][:, q],
                                                      ALU.mult, ALU.mult), "shift", s)

                    for h in range(2):
                        q = slice(2 * h, 2 * h + 2)
                        yield from sums(h)
                        for t in (2 * h, 2 * h + 1):
                            k = st(vec.bn_stats(stats[s][:, t, :], tile(t)))
                        yield
                        if h:
                            shift_of(0)
                            yield
                        wt(k)
                        for t in (2 * h, 2 * h + 1):
                            k = st(vec.bn_aggr(mv[s][:, t, :], stats[s][:, t, :]))
                        wt(k)
                        done(vec.tensor_scalar(vareps[s][:, q], mv[s][:, q, 1], EPS, None, ALU.add), "var", s)
                        yield
                    shift_of(1)
                    yield

                def layer_sums(n, name, old):
                    def sums(h):
                        p = side.full(f"{name}.{h}")
                        read_by(s, f"{name}.{h}", vec.tensor_tensor(res[s][:, 2 * h:2 * h + 2, :], two(p),
                                                                    old[:, 2 * h:2 * h + 2, :], ALU.add))
                        yield
                        side.read(f"{name}.{h}")
                    yield from layer_norm(n, lambda t: res[s][:, t, :], sums)

                def bank_sums(n, name):
                    def sums(h):
                        side.full(f"{name}.{h}")
                        yield from ()
                    yield from layer_norm(n, lambda t: side.psum(f"{name}.{t // 2}")[:, t % 2 * D:(t % 2 + 1) * D],
                                          sums)

                def scales(a):
                    k = st(vec.tensor_scalar(a[:, 1, :], a[:, 0, :], 1e-5, 1.0 / 127.0, ALU.max, ALU.mult))
                    wt(k)
                    return vec.reciprocal(a[:, 3, :], a[:, 1, :])

                if s == 0 and r == 0:
                    vec.wait_ge(win_hi, 1)
                    vec.tensor_tensor(w_in_lo[:], w_in_nat, w_in_hi[:].bitcast(F32), ALU.subtract)\
                       .then_inc(win_split, 1)
                    yield
                def rest_of_x(n, signal):
                    for h in range(2):
                        side.wait(signal, h + 1)
                        q = slice(h * D, (h + 1) * D)
                        ins = vec.tensor_tensor(xlo[s][:, :, q], two(side.psum(f"x{n}.{h}")),
                                                xhi[s][:, :, q].bitcast(F32), ALU.subtract)
                        read_by(s, f"x{n}.{h}", ins)
                        yield

                yield from rest_of_x(1, "xhi1")
                vec.wait_ge(w_loaded["uconst"], 7 * 16)
                if s == 0 and r == 0:
                    vec.wait_ge(consts_set, POOL_CONSTS)
                for k in range(KD):
                    tapped = {}
                    for tap in (1, 0):
                        for e in (k, KD + k):
                            if tap == 0 and e in SIDE_U:
                                continue
                            if tap == 1:
                                side.wait("mid", U_ORDER.index(e) + 1)
                            else:
                                wt(tapped[e])
                            tapped[e] = st(vec.scalar_tensor_tensor(uconv[s][:, e, :], pad[s][:, e, 2 + tap:2 + tap + S],
                                                                    uc[:, e, tap:tap + 1], uconv[s][:, e, :],
                                                                    ALU.mult, ALU.add))
                            yield
                    wt(max(tapped.values()))
                    done(vec.tensor_tensor(v1[s][:, k, :], uconv[s][:, KD + k, :], uconv[s][:, k, :], ALU.mult),
                         "v", s)
                    yield
                for k in range(KD):
                    p = side.full(f"y.{k}")
                    side.wait("v", k + 1)
                    read_by(s, f"y.{k}", vec.scalar_tensor_tensor(z1[s][:, k, :], v1[s][:, k, :], fbc[:, k:k + 1],
                                                                  p[:], ALU.mult, ALU.add))
                    yield
                    side.read(f"y.{k}")
                    done(vec.tensor_tensor(z1[s][:, k, :], z1[s][:, k, :], uconv[s][:, k, :], ALU.mult), "z", s)
                    yield
                side.wait("x", 16)
                yield from layer_sums(1, "o", xin[s])
                yield from bank_sums(2, "e")
                for h in range(2):
                    q = slice(2 * h, 2 * h + 2)
                    side.read(f"e.{h}")
                    n = st(vec.tensor_reduce(amax[s][:, 0, q], xn[s][:, q, :], AX, ALU.max,
                                             apply_absolute_value=True))
                    yield
                    wt(n)
                    done(scales(amax[s][:, :, q]), "xscale", s)
                    yield
                    t = 2 * h
                    side.wait("xscale", h + 1)
                    n = st(vec.tensor_scalar(res[s][:, t, :], xn[s][:, t, :], amax[s][:, 3, t:t + 1], MAGIC,
                                             ALU.mult, ALU.add))
                    wt(n)
                    done(vec.tensor_scalar(res[s][:, t, :], res[s][:, t, :], -MAGIC, amax[s][:, 1, t:t + 1],
                                           ALU.add, ALU.mult), "xq_even", s)
                    yield
                yield from rest_of_x(3, "xhi")
                vec.wait_ge(taps_ready, 2)
                for m in range(KM):
                    g = side.psum(f"g.{m}")
                    c = gconv[s][:, m % 4, :]
                    side.wait("gmid", m + 1)
                    n = st(vec.scalar_tensor_tensor(c[:, 1:S], g[:, 0:S - 1], fcs[:, m, 0:1], c[:, 1:S],
                                                    ALU.mult, ALU.add))
                    yield
                    wt(n)
                    read_by(s, f"g.{m}", vec.scalar_tensor_tensor(c[:, 0:S - 1], g[:, 1:S], fcs[:, m, 2:3],
                                                                  c[:, 0:S - 1], ALU.mult, ALU.add))
                    yield
                    if m % 4 == 3:
                        side.wait("hid", m + 1)
                        n = st(vec.tensor_reduce(colmax[s][:, m // 4, :],
                                                 hid[s][:, m - 3:m + 1, :].rearrange("p m t -> p t m"),
                                                 AX, ALU.max, apply_absolute_value=True))
                        yield
                wt(n)
                done(vec.tensor_tensor(colmax[s][:, 0, :], colmax[s][:, 0, :], colmax[s][:, 1, :], ALU.max),
                     "colmax", s)
                yield
                p = side.full("amax")
                read_by(s, "amax", vec.tensor_reduce(amax2[s][:, 0, :], p[:].rearrange("p (t h) -> p t h", t=NT),
                                                     AX, ALU.max))
                side.read("amax")
                done(scales(amax2[s]), "scale", s)
                scaled = st(vec.tensor_scalar(amax2[s][:, 2, :], amax2[s][:, 1, :], wmean[:, 1:2], None, ALU.mult))
                yield
                if r:
                    vec.wait_ge(ready["stored"][s], 32 * r)
                side.read("scale")
                for m in range(KM):
                    if m in POOL_SCALES:
                        side.wait("scaled", POOL_SCALES.index(m) + 1)
                    else:
                        n = st(vec.tensor_tensor(hid[s][:, m, :], hid[s][:, m, :], colmax[s][:, 1, :], ALU.mult))
                        yield
                        wt(n)
                    done(vec.tensor_scalar(hq[s][:, m, :], hid[s][:, m, :], MAGIC, -MAGIC, ALU.add, ALU.add), "hq", s)
                    yield
                def sums(h):
                    p = side.full(f"f.{h}")
                    wt(scaled)
                    for t in range(2):
                        tt = 2 * h + t
                        ins = vec.scalar_tensor_tensor(res[s][:, tt, :], p[:, t * D:(t + 1) * D],
                                                       amax2[s][:, 2, tt:tt + 1], xn[s][:, tt, :], ALU.mult, ALU.add)
                    read_by(s, f"f.{h}", ins)
                    yield
                    side.read(f"f.{h}")
                yield from layer_norm(3, lambda t: res[s][:, t, :], sums)
                for m in range(KI + 1):
                    if m < KI:
                        side.read(f"t.{m}")
                        p = side.full(f"a.{m}")
                        read_by(s, f"a.{m}", vec.scalar_tensor_tensor(pad[s][:, m, 4:], th[s][:, m, :], 1.0,
                                                                      p[:], ALU.add, ALU.mult))
                        yield
                    if m >= 1:
                        j = m - 1
                        c = aconv[s][:, j, :]
                        side.wait("mid", 4 + j + 1)
                        for tap in (2, 1):
                            ins = vec.scalar_tensor_tensor(c, pad[s][:, j, 1 + tap:1 + tap + S],
                                                           acs[:, j, tap:tap + 1], c, ALU.mult, ALU.add)
                            if tap == 2:
                                n = st(ins)
                                yield
                                wt(n)
                        done(ins, "conv", s)
                        yield
                yield from layer_sums(4, "j", xn[s])
                for i in range(UNITS + 3):
                    if i < UNITS:
                        p = side.full(f"s.{i}")[:].rearrange("p (h t) -> p h t", h=HG)
                        n = st(vec.tensor_reduce(smax[s][:, i % 2, :], p, AX, ALU.max))
                        yield
                        wt(n)
                        if i >= 2:
                            side.wait("p", i - 1)
                        read_by(s, f"s.{i}", vec.tensor_tensor(
                            sub[s][:, i % 2, :].rearrange("p (h t) -> p h t", h=HG), p,
                            smax[s][:, i % 2, :].unsqueeze(2).broadcast_to([P, HG, CTX]), ALU.subtract))
                        yield
                    if i >= 4 and i % 2 == 0:
                        t = (i - 4) // 2
                        pv = side.full(f"pv.{t}")[:, 0:HEADS * VW].rearrange("p (h d) -> p h d", h=HEADS)
                        n = st(vec.reciprocal(rsum[s][:], pv[:, :, DK]))
                        wt(n)
                        read_by(s, f"pv.{t}", vec.tensor_tensor(
                            o5[s][:, t, :].rearrange("p (h d) -> p h d", h=HEADS), pv[:, :, 0:DK],
                            rsum[s][:].unsqueeze(2).broadcast_to([P, HEADS, DK]), ALU.mult))
                        yield
                yield from layer_sums(5, "k", xn[s])
                yield from bank_sums(6, "m")

            vec.memset(hrow[:], 0.0).then_inc(hrow_zeroed, 1)
            merged("dve", slot_programs(prepare, batch))

_INS = ['x', 'ctx_1024', 'L0_attn_w_in', 'L0_attn_b_in', 'L0_attn_w_conv', 'L0_attn_b_conv', 'L0_attn_w1',
        'L0_attn_b1', 'L0_attn_w2', 'L0_attn_b2', 'L0_attn_w3', 'L0_attn_filt_bias', 'L0_attn_w_out',
        'L0_attn_b_out', 'L0_xattn_W', 'L0_xattn_b', 'L0_ffn_w1', 'L0_ffn_conv_w', 'L0_ffn_conv_b', 'L0_ffn_w2',
        'L1_attn_W_in', 'L1_attn_conv_w', 'L1_attn_conv_b', 'L1_attn_W_out', 'L1_xattn_Wq', 'L1_xattn_bq',
        'L1_xattn_Wk', 'L1_xattn_bk', 'L1_xattn_Wv', 'L1_xattn_bv', 'L1_xattn_Wo', 'L1_xattn_bo',
        'L1_ffn_w_freq_real', 'L1_ffn_w_freq_imag', 'L1_ffn_bias']


def constants():
    angle = 2 * np.pi * (np.outer(np.arange(D), np.arange(D)) % D) / D
    return {"eye": np.eye(D, dtype=np.float32),
            "dft": np.concatenate([np.cos(angle), np.sin(angle), -np.sin(angle)]).astype(np.float32),
            "head_mask": np.kron(np.eye(HG), np.ones((DK, 1))).astype(np.float32),
            "time0": np.array([[0], [0], [0], [1]], np.float32)}


def kernel(**inputs):
    import concourse.bacc as _bacc
    from concourse import mybir as _mybir
    from concourse.bass_utils import run_bass_kernel_spmd as _run

    nc = _bacc.Bacc("TRN2", target_bir_lowering=False, num_devices=1)
    arrays, args = {}, []
    for name, a in [(n, inputs[n]) for n in _INS] + list(constants().items()):
        a = np.ascontiguousarray(a)
        arrays[f"in_{name}_dram"] = a
        args.append(nc.dram_tensor(f"in_{name}_dram", a.shape, _mybir.dt.from_np(a.dtype), kind="ExternalInput").ap())
    args.append(nc.dram_tensor("out_0_dram", (B, S, D), F32, kind="ExternalOutput").ap())
    build(nc, *args)
    r = _run(nc, [arrays], core_ids=[0])
    return r.results[0]["out_0_dram"]
```
